# Optimizing a Trainium2 kernel written in Bass

```python
import numpy as np
import jax
import jax.numpy as jnp

def _softmax(x, axis=-1):
    return jax.nn.softmax(x, axis=axis)

def _gelu(x):
    return jax.nn.gelu(x, approximate=True)

def _silu(x):
    return jax.nn.silu(x)

def _sigmoid(x):
    return jax.nn.sigmoid(x)

def _layernorm(x, axis=-1, eps=1e-05):
    m = jnp.mean(x, axis=axis, keepdims=True)
    v = jnp.var(x, axis=axis, keepdims=True)
    return (x - m) / jnp.sqrt(v + eps)

def _scatter_add(tgt, idx, src, axis=0):
    return tgt.at[idx].add(src)

def _segment_sum(src, seg, n):
    return jax.ops.segment_sum(src, seg, n)
kernel_name = 'mk_hybrid_d1_jaxref_r4_8e6346'

def setup_inputs(seed: int=0):
    np.random.seed(seed)
    _w = jnp.asarray

    def _L0_attn_a_setup():
        import jax, jax.numpy as jnp
        import numpy as np
        B, T, C, H, N_LAYER, LAYER_ID = (4, 512, 256, 16, 12, 6)
        N = C // H
        Q = 64

        def _forward(x, time_maa_x, time_maa_w, time_maa_k, time_maa_v, time_maa_r, maa_w1, maa_w2, decay_w1, decay_w2, time_decay, time_faaaa, Wr, Wk, Wv, Wo, ln_g, ln_b):
            b, t, c = x.shape
            nc = t // Q
            xx = jnp.pad(x, ((0, 0), (1, 0), (0, 0)))[:, :-1] - x
            xxx = x + xx * time_maa_x
            m = jnp.tanh(xxx @ maa_w1).reshape(b, t, 4, -1)
            m = jnp.einsum('btfd,fdc->fbtc', m, maa_w2)
            mw, mk, mv, mr = (m[0], m[1], m[2], m[3])
            xw = x + xx * (time_maa_w + mw)
            xk = x + xx * (time_maa_k + mk)
            xv = x + xx * (time_maa_v + mv)
            xr = x + xx * (time_maa_r + mr)
            r = (xr @ Wr).reshape(b, t, H, N).transpose(0, 2, 1, 3)
            k = (xk @ Wk).reshape(b, t, H, N).transpose(0, 2, 1, 3)
            v = (xv @ Wv).reshape(b, t, H, N).transpose(0, 2, 1, 3)
            w = time_decay + jnp.tanh(xw @ decay_w1) @ decay_w2
            w = w.reshape(b, t, H, N).transpose(0, 2, 1, 3).mean(axis=-1)
            w_log = -jnp.exp(w)
            wc = w_log.reshape(b, H, nc, Q, 1)
            wc_cum = jnp.cumsum(wc, axis=-2)
            shifted = jnp.pad(wc_cum, ((0, 0), (0, 0), (0, 0), (1, 0), (0, 0)))[..., :-1, :]
            ws_log = wc.sum(axis=-2, keepdims=True)
            w_inter = jnp.exp(ws_log - wc_cum)
            w_intra = jnp.exp(wc_cum - wc)
            ws = jnp.exp(ws_log)
            A = shifted - jnp.swapaxes(wc_cum, -1, -2)
            strict = jnp.tril(jnp.ones((Q, Q), dtype=bool), -1)
            w_mask = jnp.where(strict, jnp.exp(jnp.where(strict, A, 0.0)), 0.0)
            rr = r.reshape(b, H, nc, Q, N)
            kk = k.reshape(b, H, nc, Q, N)
            vv = v.reshape(b, H, nc, Q, N)
            kv = jnp.einsum('bhcqn,bhcqm->bhcnm', kk * w_inter, vv)

            def step(state, inp):
                ws_i, kv_i = inp
                return (ws_i * state + kv_i, state)
            _, states = jax.lax.scan(step, jnp.zeros((b, H, N, N), x.dtype), (jnp.moveaxis(ws, 2, 0), jnp.moveaxis(kv, 2, 0)))
            states = jnp.moveaxis(states, 0, 2)
            inter = jnp.einsum('bhcqn,bhcnm->bhcqm', rr * w_intra, states)
            scores = jnp.einsum('bhcqn,bhckn->bhcqk', rr, kk) * w_mask
            diag = jnp.sum(rr * (time_faaaa * kk), axis=-1)
            intra = jnp.einsum('bhcqk,bhckm->bhcqm', scores, vv) + diag[..., None] * vv
            y = (inter + intra).reshape(b, H, t, N).transpose(0, 2, 1, 3).reshape(b, t, c)
            mu = y.mean(axis=-1, keepdims=True)
            var = ((y - mu) ** 2).mean(axis=-1, keepdims=True)
            y = (y - mu) / jnp.sqrt(var + 1e-05) * ln_g + ln_b
            return y @ Wo
        key = jax.random.key(seed)
        ks = jax.random.split(key, 9)
        r0 = LAYER_ID / (N_LAYER - 1)
        r1 = 1.0 - LAYER_ID / N_LAYER
        ddd = (jnp.arange(C, dtype=jnp.float32) / C)[None, None, :]
        h = jnp.arange(C, dtype=jnp.float32)
        s = 1.0 / np.sqrt(C)
        return {'x': jax.random.normal(ks[0], (B, T, C), jnp.float32), 'time_maa_x': 1.0 - ddd ** r1, 'time_maa_w': 1.0 - ddd ** r1, 'time_maa_k': 1.0 - ddd ** r1, 'time_maa_v': 1.0 - (ddd ** r1 + 0.3 * r0), 'time_maa_r': 1.0 - ddd ** (0.5 * r1), 'maa_w1': jax.random.uniform(ks[1], (C, 4 * 32), jnp.float32, minval=-0.01, maxval=0.01), 'maa_w2': jax.random.uniform(ks[2], (4, 32, C), jnp.float32, minval=-0.01, maxval=0.01), 'decay_w1': jax.random.uniform(ks[3], (C, 64), jnp.float32, minval=-0.01, maxval=0.01), 'decay_w2': jax.random.uniform(ks[4], (64, C), jnp.float32, minval=-0.01, maxval=0.01), 'time_decay': (-6.0 + 5.0 * (h / (C - 1)) ** (0.7 + 1.3 * r0))[None, None, :], 'time_faaaa': (r0 * (1.0 - h / (C - 1))).reshape(1, H, 1, 1, N), 'Wr': jax.random.normal(ks[5], (C, C), jnp.float32) * s, 'Wk': jax.random.normal(ks[6], (C, C), jnp.float32) * s, 'Wv': jax.random.normal(ks[7], (C, C), jnp.float32) * s, 'Wo': jax.random.normal(ks[8], (C, C), jnp.float32) * s, 'ln_g': jnp.ones((C,), jnp.float32), 'ln_b': jnp.zeros((C,), jnp.float32)}
    _L0_attn_a_in = _L0_attn_a_setup()

    def _L0_attn_b_setup():
        import jax, jax.numpy as jnp
        import numpy as np
        B, L, D, H = (2, 256, 256, 8)
        HD = D // H

        def _deltanet(x, Wq, Wk, Wv, Wb, ln_w, ln_b):
            Bb, Ll, Dd = x.shape
            q = (x @ Wq).reshape(Bb, Ll, H, HD)
            k = (x @ Wk).reshape(Bb, Ll, H, HD)
            k = k / jnp.maximum(jnp.linalg.norm(k, axis=-1, keepdims=True), 1e-12)
            v = jax.nn.silu(x @ Wv).reshape(Bb, Ll, H, HD)
            beta = jax.nn.sigmoid(x @ Wb)
            qs = jnp.moveaxis(q, 1, 0)
            ks_ = jnp.moveaxis(k, 1, 0)
            vs = jnp.moveaxis(v, 1, 0)
            bs = jnp.moveaxis(beta, 1, 0)

            def step(S, inp):
                qt, kt, vt, bt = inp
                Sk = jnp.einsum('bhk,bhkv->bhv', kt, S)
                S = S + jnp.einsum('bh,bhk,bhv->bhkv', bt, kt, vt - Sk)
                ot = jnp.einsum('bhk,bhkv->bhv', qt, S)
                return (S, ot)
            S0 = jnp.zeros((Bb, H, HD, HD), x.dtype)
            _, os_ = jax.lax.scan(step, S0, (qs, ks_, vs, bs))
            o = jnp.moveaxis(os_, 0, 1).reshape(Bb, Ll, Dd)
            mu = jnp.mean(o, axis=-1, keepdims=True)
            var = jnp.var(o, axis=-1, keepdims=True)
            return (o - mu) / jnp.sqrt(var + 1e-05) * ln_w + ln_b
        key = jax.random.key(seed)
        ks = jax.random.split(key, 5)
        s = 1.0 / np.sqrt(D)
        x = jax.random.normal(ks[0], (B, L, D), jnp.float32)
        Wq = jax.random.uniform(ks[1], (D, D), jnp.float32, -s, s)
        Wk = jax.random.uniform(ks[2], (D, D), jnp.float32, -s, s)
        Wv = jax.random.uniform(ks[3], (D, D), jnp.float32, -s, s)
        Wb = jax.random.uniform(ks[4], (D, H), jnp.float32, -s, s)
        ln_w = jnp.ones((D,), jnp.float32)
        ln_b = jnp.zeros((D,), jnp.float32)
        return {'x': x, 'Wq': Wq, 'Wk': Wk, 'Wv': Wv, 'Wb': Wb, 'ln_w': ln_w, 'ln_b': ln_b}
    _L0_attn_b_in = _L0_attn_b_setup()

    def _L0_ffn_setup():
        import jax, jax.numpy as jnp
        import numpy as np
        B, S, H = (1, 512, 256)
        E, K = (16, 4)
        G, TG = (4, 2)
        I_MOE = 128
        N_SH = 2
        SCALE = 2.5

        def _mlp(x, gw, uw, dw):
            return jax.nn.silu(x @ gw.T) * (x @ uw.T) @ dw.T

        def _route(x2d, router_weight, e_bias):
            T = x2d.shape[0]
            scores = jax.nn.sigmoid(x2d @ router_weight.T)
            sc = scores + e_bias[None, :]
            group_scores = jnp.sum(jax.lax.top_k(sc.reshape(T, G, E // G), 2)[0], axis=-1)
            _, gidx = jax.lax.top_k(group_scores, TG)
            gmask = jnp.zeros((T, G), sc.dtype).at[jnp.arange(T)[:, None], gidx].set(1.0)
            smask = jnp.repeat(gmask, E // G, axis=1)
            masked = jnp.where(smask > 0, sc, 0.0)
            _, tidx = jax.lax.top_k(masked, K)
            tw = jnp.take_along_axis(scores, tidx, axis=1)
            tw = tw / (jnp.sum(tw, axis=-1, keepdims=True) + 1e-20)
            tw = tw * SCALE
            return (tidx, tw)

        def _moe_forward(hidden_states, router_weight, e_bias, gate_w, up_w, down_w, sh_gate_w, sh_up_w, sh_down_w):
            orig_shape = hidden_states.shape
            x = hidden_states.reshape(-1, H)
            T = x.shape[0]
            tidx, tw = _route(x, router_weight, e_bias)
            g = jnp.einsum('th,eih->tei', x, gate_w)
            u = jnp.einsum('th,eih->tei', x, up_w)
            h = jax.nn.silu(g) * u
            yo = jnp.einsum('tei,ehi->teh', h, down_w)
            combine = jnp.zeros((T, E), tw.dtype).at[jnp.arange(T)[:, None], tidx].add(tw)
            routed = jnp.einsum('te,teh->th', combine, yo)
            shared = _mlp(hidden_states.reshape(-1, H), sh_gate_w, sh_up_w, sh_down_w)
            return (routed + shared).reshape(orig_shape)
        key = jax.random.key(seed)
        ks = jax.random.split(key, 9)
        s = 0.02
        return {'hidden_states': jax.random.normal(ks[0], (B, S, H), jnp.float32), 'router_weight': jax.random.normal(ks[1], (E, H), jnp.float32) * s, 'e_bias': jnp.zeros((E,), jnp.float32), 'gate_w': jax.random.normal(ks[2], (E, I_MOE, H), jnp.float32) * s, 'up_w': jax.random.normal(ks[3], (E, I_MOE, H), jnp.float32) * s, 'down_w': jax.random.normal(ks[4], (E, H, I_MOE), jnp.float32) * s, 'sh_gate_w': jax.random.normal(ks[5], (N_SH * I_MOE, H), jnp.float32) * s, 'sh_up_w': jax.random.normal(ks[6], (N_SH * I_MOE, H), jnp.float32) * s, 'sh_down_w': jax.random.normal(ks[7], (H, N_SH * I_MOE), jnp.float32) * s}
    _L0_ffn_in = _L0_ffn_setup()
    _d = {'L0_attn_a_x': _L0_attn_a_in['x'], 'L0_attn_a_time_maa_x': _L0_attn_a_in['time_maa_x'], 'L0_attn_a_time_maa_w': _L0_attn_a_in['time_maa_w'], 'L0_attn_a_time_maa_k': _L0_attn_a_in['time_maa_k'], 'L0_attn_a_time_maa_v': _L0_attn_a_in['time_maa_v'], 'L0_attn_a_time_maa_r': _L0_attn_a_in['time_maa_r'], 'L0_attn_a_maa_w1': _L0_attn_a_in['maa_w1'], 'L0_attn_a_maa_w2': _L0_attn_a_in['maa_w2'], 'L0_attn_a_decay_w1': _L0_attn_a_in['decay_w1'], 'L0_attn_a_decay_w2': _L0_attn_a_in['decay_w2'], 'L0_attn_a_time_decay': _L0_attn_a_in['time_decay'], 'L0_attn_a_time_faaaa': _L0_attn_a_in['time_faaaa'], 'L0_attn_a_Wr': _L0_attn_a_in['Wr'], 'L0_attn_a_Wk': _L0_attn_a_in['Wk'], 'L0_attn_a_Wv': _L0_attn_a_in['Wv'], 'L0_attn_a_Wo': _L0_attn_a_in['Wo'], 'L0_attn_a_ln_g': _L0_attn_a_in['ln_g'], 'L0_attn_a_ln_b': _L0_attn_a_in['ln_b'], 'L0_attn_b_Wq': _L0_attn_b_in['Wq'], 'L0_attn_b_Wk': _L0_attn_b_in['Wk'], 'L0_attn_b_Wv': _L0_attn_b_in['Wv'], 'L0_attn_b_Wb': _L0_attn_b_in['Wb'], 'L0_attn_b_ln_w': _L0_attn_b_in['ln_w'], 'L0_attn_b_ln_b': _L0_attn_b_in['ln_b'], 'L0_ffn_router_weight': _L0_ffn_in['router_weight'], 'L0_ffn_e_bias': _L0_ffn_in['e_bias'], 'L0_ffn_gate_w': _L0_ffn_in['gate_w'], 'L0_ffn_up_w': _L0_ffn_in['up_w'], 'L0_ffn_down_w': _L0_ffn_in['down_w'], 'L0_ffn_sh_gate_w': _L0_ffn_in['sh_gate_w'], 'L0_ffn_sh_up_w': _L0_ffn_in['sh_up_w'], 'L0_ffn_sh_down_w': _L0_ffn_in['sh_down_w']}
    _x0 = _d['L0_attn_a_x']
    _d['L0_attn_a_x'] = jax.random.normal(jax.random.fold_in(jax.random.key(seed), 1), (16, 512, 256), dtype=_x0.dtype)
    del _x0
    return _d

def reference(L0_attn_a_x, L0_attn_a_time_maa_x, L0_attn_a_time_maa_w, L0_attn_a_time_maa_k, L0_attn_a_time_maa_v, L0_attn_a_time_maa_r, L0_attn_a_maa_w1, L0_attn_a_maa_w2, L0_attn_a_decay_w1, L0_attn_a_decay_w2, L0_attn_a_time_decay, L0_attn_a_time_faaaa, L0_attn_a_Wr, L0_attn_a_Wk, L0_attn_a_Wv, L0_attn_a_Wo, L0_attn_a_ln_g, L0_attn_a_ln_b, L0_attn_b_Wq, L0_attn_b_Wk, L0_attn_b_Wv, L0_attn_b_Wb, L0_attn_b_ln_w, L0_attn_b_ln_b, L0_ffn_router_weight, L0_ffn_e_bias, L0_ffn_gate_w, L0_ffn_up_w, L0_ffn_down_w, L0_ffn_sh_gate_w, L0_ffn_sh_up_w, L0_ffn_sh_down_w):

    def _L0_attn_a_ref(x, time_maa_x, time_maa_w, time_maa_k, time_maa_v, time_maa_r, maa_w1, maa_w2, decay_w1, decay_w2, time_decay, time_faaaa, Wr, Wk, Wv, Wo, ln_g, ln_b):
        import jax, jax.numpy as jnp
        import numpy as np
        B, T, C, H, N_LAYER, LAYER_ID = (4, 512, 256, 16, 12, 6)
        N = C // H
        Q = 64

        def _forward(x, time_maa_x, time_maa_w, time_maa_k, time_maa_v, time_maa_r, maa_w1, maa_w2, decay_w1, decay_w2, time_decay, time_faaaa, Wr, Wk, Wv, Wo, ln_g, ln_b):
            b, t, c = x.shape
            nc = t // Q
            xx = jnp.pad(x, ((0, 0), (1, 0), (0, 0)))[:, :-1] - x
            xxx = x + xx * time_maa_x
            m = jnp.tanh(xxx @ maa_w1).reshape(b, t, 4, -1)
            m = jnp.einsum('btfd,fdc->fbtc', m, maa_w2)
            mw, mk, mv, mr = (m[0], m[1], m[2], m[3])
            xw = x + xx * (time_maa_w + mw)
            xk = x + xx * (time_maa_k + mk)
            xv = x + xx * (time_maa_v + mv)
            xr = x + xx * (time_maa_r + mr)
            r = (xr @ Wr).reshape(b, t, H, N).transpose(0, 2, 1, 3)
            k = (xk @ Wk).reshape(b, t, H, N).transpose(0, 2, 1, 3)
            v = (xv @ Wv).reshape(b, t, H, N).transpose(0, 2, 1, 3)
            w = time_decay + jnp.tanh(xw @ decay_w1) @ decay_w2
            w = w.reshape(b, t, H, N).transpose(0, 2, 1, 3).mean(axis=-1)
            w_log = -jnp.exp(w)
            wc = w_log.reshape(b, H, nc, Q, 1)
            wc_cum = jnp.cumsum(wc, axis=-2)
            shifted = jnp.pad(wc_cum, ((0, 0), (0, 0), (0, 0), (1, 0), (0, 0)))[..., :-1, :]
            ws_log = wc.sum(axis=-2, keepdims=True)
            w_inter = jnp.exp(ws_log - wc_cum)
            w_intra = jnp.exp(wc_cum - wc)
            ws = jnp.exp(ws_log)
            A = shifted - jnp.swapaxes(wc_cum, -1, -2)
            strict = jnp.tril(jnp.ones((Q, Q), dtype=bool), -1)
            w_mask = jnp.where(strict, jnp.exp(jnp.where(strict, A, 0.0)), 0.0)
            rr = r.reshape(b, H, nc, Q, N)
            kk = k.reshape(b, H, nc, Q, N)
            vv = v.reshape(b, H, nc, Q, N)
            kv = jnp.einsum('bhcqn,bhcqm->bhcnm', kk * w_inter, vv)

            def step(state, inp):
                ws_i, kv_i = inp
                return (ws_i * state + kv_i, state)
            _, states = jax.lax.scan(step, jnp.zeros((b, H, N, N), x.dtype), (jnp.moveaxis(ws, 2, 0), jnp.moveaxis(kv, 2, 0)))
            states = jnp.moveaxis(states, 0, 2)
            inter = jnp.einsum('bhcqn,bhcnm->bhcqm', rr * w_intra, states)
            scores = jnp.einsum('bhcqn,bhckn->bhcqk', rr, kk) * w_mask
            diag = jnp.sum(rr * (time_faaaa * kk), axis=-1)
            intra = jnp.einsum('bhcqk,bhckm->bhcqm', scores, vv) + diag[..., None] * vv
            y = (inter + intra).reshape(b, H, t, N).transpose(0, 2, 1, 3).reshape(b, t, c)
            mu = y.mean(axis=-1, keepdims=True)
            var = ((y - mu) ** 2).mean(axis=-1, keepdims=True)
            y = (y - mu) / jnp.sqrt(var + 1e-05) * ln_g + ln_b
            return y @ Wo
        return _forward(x, time_maa_x, time_maa_w, time_maa_k, time_maa_v, time_maa_r, maa_w1, maa_w2, decay_w1, decay_w2, time_decay, time_faaaa, Wr, Wk, Wv, Wo, ln_g, ln_b)

    def _L0_attn_b_ref(x, Wq, Wk, Wv, Wb, ln_w, ln_b):
        import jax, jax.numpy as jnp
        import numpy as np
        B, L, D, H = (2, 256, 256, 8)
        HD = D // H

        def _deltanet(x, Wq, Wk, Wv, Wb, ln_w, ln_b):
            Bb, Ll, Dd = x.shape
            q = (x @ Wq).reshape(Bb, Ll, H, HD)
            k = (x @ Wk).reshape(Bb, Ll, H, HD)
            k = k / jnp.maximum(jnp.linalg.norm(k, axis=-1, keepdims=True), 1e-12)
            v = jax.nn.silu(x @ Wv).reshape(Bb, Ll, H, HD)
            beta = jax.nn.sigmoid(x @ Wb)
            qs = jnp.moveaxis(q, 1, 0)
            ks_ = jnp.moveaxis(k, 1, 0)
            vs = jnp.moveaxis(v, 1, 0)
            bs = jnp.moveaxis(beta, 1, 0)

            def step(S, inp):
                qt, kt, vt, bt = inp
                Sk = jnp.einsum('bhk,bhkv->bhv', kt, S)
                S = S + jnp.einsum('bh,bhk,bhv->bhkv', bt, kt, vt - Sk)
                ot = jnp.einsum('bhk,bhkv->bhv', qt, S)
                return (S, ot)
            S0 = jnp.zeros((Bb, H, HD, HD), x.dtype)
            _, os_ = jax.lax.scan(step, S0, (qs, ks_, vs, bs))
            o = jnp.moveaxis(os_, 0, 1).reshape(Bb, Ll, Dd)
            mu = jnp.mean(o, axis=-1, keepdims=True)
            var = jnp.var(o, axis=-1, keepdims=True)
            return (o - mu) / jnp.sqrt(var + 1e-05) * ln_w + ln_b
        return _deltanet(x, Wq, Wk, Wv, Wb, ln_w, ln_b)

    def _L0_ffn_ref(hidden_states, router_weight, e_bias, gate_w, up_w, down_w, sh_gate_w, sh_up_w, sh_down_w):
        import jax, jax.numpy as jnp
        import numpy as np
        B, S, H = (1, 512, 256)
        E, K = (16, 4)
        G, TG = (4, 2)
        I_MOE = 128
        N_SH = 2
        SCALE = 2.5

        def _mlp(x, gw, uw, dw):
            return jax.nn.silu(x @ gw.T) * (x @ uw.T) @ dw.T

        def _route(x2d, router_weight, e_bias):
            T = x2d.shape[0]
            scores = jax.nn.sigmoid(x2d @ router_weight.T)
            sc = scores + e_bias[None, :]
            group_scores = jnp.sum(jax.lax.top_k(sc.reshape(T, G, E // G), 2)[0], axis=-1)
            _, gidx = jax.lax.top_k(group_scores, TG)
            gmask = jnp.zeros((T, G), sc.dtype).at[jnp.arange(T)[:, None], gidx].set(1.0)
            smask = jnp.repeat(gmask, E // G, axis=1)
            masked = jnp.where(smask > 0, sc, 0.0)
            _, tidx = jax.lax.top_k(masked, K)
            tw = jnp.take_along_axis(scores, tidx, axis=1)
            tw = tw / (jnp.sum(tw, axis=-1, keepdims=True) + 1e-20)
            tw = tw * SCALE
            return (tidx, tw)

        def _moe_forward(hidden_states, router_weight, e_bias, gate_w, up_w, down_w, sh_gate_w, sh_up_w, sh_down_w):
            orig_shape = hidden_states.shape
            x = hidden_states.reshape(-1, H)
            T = x.shape[0]
            tidx, tw = _route(x, router_weight, e_bias)
            g = jnp.einsum('th,eih->tei', x, gate_w)
            u = jnp.einsum('th,eih->tei', x, up_w)
            h = jax.nn.silu(g) * u
            yo = jnp.einsum('tei,ehi->teh', h, down_w)
            combine = jnp.zeros((T, E), tw.dtype).at[jnp.arange(T)[:, None], tidx].add(tw)
            routed = jnp.einsum('te,teh->th', combine, yo)
            shared = _mlp(hidden_states.reshape(-1, H), sh_gate_w, sh_up_w, sh_down_w)
            return (routed + shared).reshape(orig_shape)
        return _moe_forward(hidden_states, router_weight, e_bias, gate_w, up_w, down_w, sh_gate_w, sh_up_w, sh_down_w)
    x = L0_attn_a_x
    x = x + _L0_attn_a_ref(_layernorm(x, axis=-1), L0_attn_a_time_maa_x, L0_attn_a_time_maa_w, L0_attn_a_time_maa_k, L0_attn_a_time_maa_v, L0_attn_a_time_maa_r, L0_attn_a_maa_w1, L0_attn_a_maa_w2, L0_attn_a_decay_w1, L0_attn_a_decay_w2, L0_attn_a_time_decay, L0_attn_a_time_faaaa, L0_attn_a_Wr, L0_attn_a_Wk, L0_attn_a_Wv, L0_attn_a_Wo, L0_attn_a_ln_g, L0_attn_a_ln_b)
    x = x + _L0_ffn_ref(_layernorm(x, axis=-1), L0_ffn_router_weight, L0_ffn_e_bias, L0_ffn_gate_w, L0_ffn_up_w, L0_ffn_down_w, L0_ffn_sh_gate_w, L0_ffn_sh_up_w, L0_ffn_sh_down_w)
    x = x + _L0_attn_b_ref(_layernorm(x, axis=-1), L0_attn_b_Wq, L0_attn_b_Wk, L0_attn_b_Wv, L0_attn_b_Wb, L0_attn_b_ln_w, L0_attn_b_ln_b)
    x = x + _L0_ffn_ref(_layernorm(x, axis=-1), L0_ffn_router_weight, L0_ffn_e_bias, L0_ffn_gate_w, L0_ffn_up_w, L0_ffn_down_w, L0_ffn_sh_gate_w, L0_ffn_sh_up_w, L0_ffn_sh_down_w)
    return x

_drawn_inputs = setup_inputs


def setup_inputs(seed=0):
    import zlib

    import numpy as np

    out = dict(_drawn_inputs(seed))
    spreads = {'L0_attn_a_ln_g': (1.0, 0.2),
     'L0_attn_a_ln_b': (0.0, 0.1),
     'L0_attn_b_ln_w': (1.0, 0.2),
     'L0_attn_b_ln_b': (0.0, 0.1),
     'L0_ffn_e_bias': (0.0, 0.396)}
    factors = {'L0_attn_a_time_maa_x': 8.0,
     'L0_attn_a_time_maa_w': 24.672,
     'L0_attn_a_maa_w1': 8.0,
     'L0_attn_a_maa_w2': 8.0,
     'L0_attn_a_decay_w1': 23.739,
     'L0_attn_a_decay_w2': 22.437,
     'L0_ffn_router_weight': 6.753,
     'L0_ffn_gate_w': 3.072,
     'L0_ffn_up_w': 3.019,
     'L0_ffn_down_w': 3.025,
     'L0_ffn_sh_gate_w': 2.705,
     'L0_ffn_sh_up_w': 2.671,
     'L0_ffn_sh_down_w': 2.679}
    for name, (base, spread) in spreads.items():
        noise = np.random.default_rng([zlib.crc32(name.encode()), seed]).standard_normal(out[name].shape)
        drawn = base * np.exp(spread * noise) if base else spread * noise
        out[name] = jnp.asarray(drawn.astype(out[name].dtype))
    for name, factor in factors.items():
        out[name] = (out[name] * factor).astype(out[name].dtype)
    return out
```

```python
import concourse.bass as bass
from concourse import mybir
from contextlib import ExitStack

B, T, C = 16, 512, 256
P = 128
NT = T // P
NH = C // P
E, EH = 16, 128
NS = 2
NE = NS + E
RH, RN, RQ = 16, 16, 64
DH, DN, DQ = 8, 32, 32
EPS = 1e-5
BIG = 1e9

CONST32 = {"ident": 128, "before": 128, "after": 128, "earlier": RQ, "chunks": 2, "heads8": 8,
           "same16": 128, "same32": 128, "heads4": 4, "causal": DQ, "group_low": 16,
           "expert_low": 256, "nhalf": 32, "lane_eye": DQ * DQ}
CONST16 = {"identb": 128, "forbid": 512, "pick": E * P}

ORDER_A = [("norm",), ("ffn_in",), 0, ("mix_in",), 1, ("mix", 0), 2, ("mix", 1), 3, ("mix", 2), 4, ("mix", 3),
           5, ("decay",), 6, ("prep",)]
for _t in range(NT):
    ORDER_A += [("tile_a", _t), 7 + 2 * _t, ("tile_b", _t), 8 + 2 * _t, ("tile_c", _t)]
ORDER_A += [15, 16, 17, ("ffn_out",)]
ORDER_B = [("ffn_in",), ("norm",), 0, ("project_in",)]
for _t in range(NT):
    ORDER_B += [("project", _t), 1 + _t, ("pairs", _t)]
ORDER_B += [("load",), 5, 6, 7, 8, ("invert",), 9]
for _g in range(16):
    ORDER_B += [("solve", _g), ("update", _g)]
    if _g % 2 == 1:
        ORDER_B += [10 + _g // 2]
ORDER_B += [("ffn_out",), ("finish",)]


def hybrid_layers(nc, x, maa, maa_w1, maa_w2, decay_w1, decay_w2, time_decay, u_col, w_rkvo, ln_a,
                  w_delta_kv, w_delta_qb, ln_b, router, e_bias, gate, up, down, c32, c16, out):
    f32, bf16 = mybir.dt.float32, mybir.dt.bfloat16
    ALU, ACT, AX = mybir.AluOpType, mybir.ActivationFunctionType, mybir.AxisListType
    x_rows = x.rearrange("b (t p) c -> b p t c", p=P)
    out_rows = out.rearrange("b (t p) c -> b p t c", p=P)

    ctx = ExitStack()
    with ctx:
        copies = [0]

        def sb(name, shape, dt=f32, stack=ctx):
            if stack is not ctx:
                name = f"{name}_{copies[0]}"
            return stack.enter_context(nc.sbuf_tensor(name, shape, dt))

        WG, WU = sb("WG", [P, NH, NE * EH]), sb("WU", [P, NH, NE * EH])
        WD = sb("WD", [EH, NE, C])
        WRT = sb("WRT", [P, NH, E])
        EB = sb("EB", [P, E])
        MAA = sb("MAA", [P, 5, NH])
        W1 = sb("W1", [P, NH, P])
        W2 = sb("W2", [P, 4, C])
        DW1 = sb("DW1", [P, NH, 64])
        DW2 = sb("DW2", [64, C])
        TD = sb("TD", [64, C])
        DWM = sb("DWM", [P, RH])
        UC = sb("UC", [P, NH])
        UB = sb("UB", [P, NH, P])
        WR = sb("WR", [P, 4, NH, C])
        LNA = sb("LNA", [P, 2, NH])
        WKV, WQB = sb("WKV", [P, NH, 2 * C]), sb("WQB", [P, NH, C + DH])
        LNB = sb("LNB", [P, 2, C])
        K32 = {k: sb("c_" + k, [P, n]) for k, n in CONST32.items() if k != "lane_eye"}
        K16 = {k: sb("c_" + k, [P, n], bf16) for k, n in CONST16.items()}
        X1, X2, X2L, X3 = (sb(n, [P, NT, C]) for n in ("X1", "X2", "X2L", "X3"))
        KWP = sb("KWP", [P, 2, C])
        RP = sb("RP", [P, 4, C])
        VP = sb("VP", [P, 4, C])
        INV = sb("INV", [P, DQ, DQ])
        C3 = sb("C3", [P, NT, P], bf16)
        MAT = sb("MAT", [P, DQ, DQ])
        a_dram = nc.dram_tensor("a_scratch", (P, DQ, DQ), f32).ap()
        t_dram = nc.dram_tensor("t_scratch", (P, DQ, DQ), f32).ap()
        ident, identb = K32["ident"], K16["identb"]

        banks = [ctx.enter_context(nc.psum_tensor(f"bank{i}", [P, 512], f32)) for i in range(8)]
        GB, UBK, CBK, YA, YB = banks[:5]
        RING = banks[5:]

        sems = {}

        def sem(name):
            sems[name] = ctx.enter_context(nc.semaphore(name))
            return sems[name]

        loaded = sem("loaded")
        d_chain, p_chain, a_chain = sem("dve_chain"), sem("pool_chain"), sem("act_chain")
        f_var, f_rstd, f_xn = sem("ffn_var"), sem("ffn_rstd"), sem("ffn_xn")
        f_tr, f_xt = sem("ffn_transposed"), sem("ffn_xt")
        f_lg, f_th, f_lt, f_c3, f_ct, f_cs = (sem(n) for n in (
            "ffn_logits", "ffn_logit_tanh", "ffn_logit_turned", "ffn_parts", "ffn_parts_turned", "ffn_parts_ready"))
        f_g, f_u, f_c, f_tanh, f_gd, f_h, f_dn = (sem(n) for n in (
            "ffn_gate", "ffn_up", "ffn_spread", "ffn_tanh", "ffn_gate_read", "ffn_hidden", "ffn_down"))
        f_res, f_out = sem("ffn_result"), sem("ffn_stored")
        filled = sem("ring_filled")
        emptied = [sem(f"ring{i}_emptied") for i in range(3)]
        x_in = sem("x_loaded")
        r_var, r_rstd, r_xn, r_xt, r_xx = (sem(n) for n in ("r_var", "r_rstd", "r_xn", "r_xt", "r_xx"))
        r_mixin, r_m, r_half, r_mixed, r_proj = (sem(n) for n in ("r_mix_in", "r_tanh", "r_half_mixed", "r_mixed", "r_projected"))
        r_dt, r_we, r_dec, r_ws = (sem(n) for n in ("r_decay_tanh", "r_rate", "r_decays", "r_chunk_decay"))
        r_k, r_v, r_r, r_kt, r_prod, r_rx = (sem(n) for n in ("r_k", "r_v", "r_rT", "r_kT", "r_product", "r_spread"))
        r_wm, r_e, r_p, r_kw, r_s, r_kv = (sem(n) for n in ("r_rate_masked", "r_weights", "r_scores", "r_kw", "r_state", "r_kv"))
        r_yv, r_yr, r_yn, r_yt, r_used = (sem(n) for n in ("r_y_var", "r_y_rstd", "r_y_norm", "r_yT", "r_scores_used"))
        r_wx = sem("r_rate_by_channel")
        d_var, d_rstd, d_xn, d_xt = (sem(n) for n in ("d_var", "d_rstd", "d_xn", "d_xt"))
        d_qk, d_sq, d_ss, d_rn, d_kh, d_pt, d_turn, d_exp, d_a, d_st = (sem(n) for n in (
            "d_evacuated", "d_squares", "d_sums", "d_rnorm", "d_keys", "d_causal", "d_turned", "d_spread", "d_pairs", "d_pairs_stored_even"))
        d_stores = [d_st, sem("d_pairs_stored_odd")]
        d_mat, d_inv, d_tst, d_tld = (sem(n) for n in ("d_problems", "d_inverse", "d_inverse_stored", "d_inverse_loaded"))
        d_ks, d_r, d_v, d_vs, d_up, d_s, d_o, d_os = (sem(n) for n in (
            "d_key_state", "d_rhs", "d_solved", "d_values", "d_updated", "d_state", "d_out", "d_out_read"))
        d_ov, d_or, d_x2 = sem("d_out_var"), sem("d_out_rstd"), sem("d_x2_kept")
        d_aev = sem("d_pairs_read")

        numbers = [s.num for s in sems.values()]
        assert numbers == list(range(numbers[0], numbers[0] + len(numbers)))
        every_sem = range(numbers[0], numbers[-1] + 1)

        def end_block():
            copies[0] += 1
            nc.sync.sem_clear(every_sem)
            nc.all_engine_barrier(sem_only=True)

        def linker(eng, chain):
            count = [0]

            def link(ins):
                count[0] += 1
                ins.then_inc(chain, 1)
                eng.wait_ge(chain, count[0])
            return link

        with nc.Block() as block:
            @block.sync
            def _(sp):
                n = 0
                for k, (dst, src) in enumerate([
                        (WG[:, :, :], gate.rearrange("(a p) n -> p a n", p=P)),
                        (WU[:, :, :], up.rearrange("(a p) n -> p a n", p=P)),
                        (WD[:, :, :], down.rearrange("e p n -> p e n")),
                        (WRT[:, :, :], router.rearrange("(a p) n -> p a n", p=P)),
                        (EB[:, :], e_bias.unsqueeze(0).to_broadcast([P, E])),
                        (MAA[:, :, :], maa.rearrange("p (f a) -> p f a", a=NH)),
                        (W1[:, :, :], maa_w1.rearrange("(a p) n -> p a n", p=P)),
                        (DW1[:, :, :], decay_w1.rearrange("(a p) n -> p a n", p=P)),
                        (DW2[:, :], decay_w2),
                        (TD[:, :], time_decay.unsqueeze(0).to_broadcast([64, C])),
                        (UC[:, :], u_col),
                        (WR[:, :, :, :], w_rkvo.rearrange("f (a p) n -> p f a n", p=P)),
                        (LNA[:, :, :], ln_a.rearrange("p (f a) -> p f a", a=NH)),
                        (WKV[:, :, :], w_delta_kv.rearrange("(a p) n -> p a n", p=P)),
                        (WQB[:, :, :], w_delta_qb.rearrange("(a p) n -> p a n", p=P)),
                        (LNB[:, :, :], ln_b.unsqueeze(0).to_broadcast([P, 2, C]))]):
                    sp.dma_start(dst, src).then_inc(loaded, 16)
                    n += 16
                at = 0
                for k, cols in CONST32.items():
                    dst = INV[:, :, :].rearrange("p a b -> p (a b)") if k == "lane_eye" else K32[k][:, :]
                    sp.dma_start(dst, c32[:, at:at + cols]).then_inc(loaded, 16)
                    at += cols
                    n += 16
                at = 0
                for k, cols in CONST16.items():
                    sp.dma_start(K16[k][:, :], c16[:, at:at + cols]).then_inc(loaded, 16)
                    at += cols
                    n += 16
                sp.wait_ge(p_chain, 1)
                for f in range(4):
                    sp.dma_start(W2[32 * f:32 * f + 32, f, :], maa_w2[f]).then_inc(loaded, 16)
                    n += 16
                sp.wait_ge(loaded, n)
                sp.sem_inc(d_chain, 1)

            @block.gpsimd
            def _(pool):
                pool.memset(W2[:, :, :], 0.0).then_inc(p_chain, 1)
                pool.memset(KWP[:, :, :], 0.0)
                pool.memset(RP[:, :, :], 0.0)
                pool.memset(VP[:, :, :], 0.0)
                pool.memset(C3[:, :, :], 0.0)
                pool.memset(DWM[:, :], 0.0).then_inc(p_chain, 1)

            @block.vector
            def _(dve):
                dve.wait_ge(d_chain, 1)
                dve.wait_ge(p_chain, 2)
                dve.tensor_reduce(DWM[0:64, :], DW2[:, :].rearrange("p (h n) -> p h n", n=RN), AX.X, ALU.add)
                dve.tensor_reduce(DWM[64:65, :], TD[0:1, :].rearrange("p (h n) -> p h n", n=RN), AX.X, ALU.add)\
                   .then_inc(d_chain, 1)
                dve.wait_ge(d_chain, 2)
                dve.tensor_scalar(DWM[0:64, :], DWM[0:64, :], 1.0 / RN, None, ALU.mult)
                dve.tensor_scalar(DWM[64:65, :], DWM[64:65, :], 1.0 / RN, None, ALU.mult)
                for a in range(NH):
                    dve.tensor_scalar(UB[:, a, :], K32["same16"][:, :], UC[:, a:a + 1], None, ALU.mult)
        end_block()

        def turns(names):
            return {name: n for n, name in enumerate(names)}

        def layer_norm(dve, link, src, work, var, rstd, dst, done, tiles=NT):
            stats, mv, ve = work
            for t in range(tiles):
                last = dve.bn_stats(stats[:, t, :], src[:, t, :])
            link(last)
            for t in range(tiles):
                last = dve.bn_aggr(mv[:, t, :], stats[:, t, :])
            link(last)
            dve.tensor_scalar(ve[:, :, 0], mv[:, :, 1], EPS, None, ALU.add).then_inc(var, 1)
            dve.wait_ge(rstd, 1)
            for t in range(tiles):
                last = dve.tensor_scalar(dst[:, t, :], src[:, t, :], mv[:, t, 0:1], ve[:, t, 1:2],
                                         ALU.subtract, ALU.mult)
            last.then_inc(done, 1)

        def root(pool, work, var, rstd):
            pool.wait_ge(var, 1)
            ve = work[2]
            pool.tensor_tensor(ve[:, :, 1], ve[:, :, 0], K32["nhalf"][:, 0:NT], ALU.pow).then_inc(rstd, 1)

        def norm_work(name, stack):
            return (sb(name + "_st", [P, NT, 6], stack=stack), sb(name + "_mv", [P, NT, 2], stack=stack),
                    sb(name + "_ve", [P, NT, 2], stack=stack))

        class Ffn:

            def __init__(self, tag, src, dst, stack):
                def t(n, shape, dt=f32):
                    return sb(f"{tag}_{n}", shape, dt, stack)
                self.src, self.dst = src, dst
                self.work = norm_work(tag, stack)
                self.xn, self.xt = t("xn", [P, NT, C]), t("xt", [P, NH, T])
                self.th, self.s, self.h = t("th", [P, 512]), t("s", [P, 2, 512]), t("h", [P, 2, 512])
                self.lt = t("lt", [E, T])
                self.sc, self.scb, self.gs, self.rk, self.wt, self.cw = (
                    t(n, [P, NT * E]) for n in ("sc", "scb", "gs", "rk", "wt", "cw"))
                self.pair, self.sum = t("pair", [P, NT * 4, 6]), t("sum", [P, 2 * NT])
                self.gt, self.eq = (v[:, :, :].rearrange("p a n -> p (a n)").rearrange("p (t a b) -> p t a b", a=E, b=E)
                                    for v in (self.s, self.h))
                self.c3t = t("c3t", [P, T], bf16)

            def pe_in(self, pe):
                pe.wait_ge(f_xn, 1)
                for a, bank in enumerate((YA, YB)):
                    for t in range(NT):
                        last = pe.transpose(bank[:, t * P:t * P + P], self.xn[:, t, a * P:a * P + P], ident[:, :])
                last.then_inc(f_tr, 1)
                pe.wait_ge(f_xt, 2)
                for a in range(NH):
                    last = pe.matmul(GB[0:E, :], WRT[:, a, :], self.xt[:, a, :], start=a == 0, stop=a == NH - 1)
                last.then_inc(f_lg, 1)
                pe.wait_ge(f_th, 1)
                for t in range(NT):
                    last = pe.transpose(CBK[:, t * E:t * E + E], self.lt[:, t * P:t * P + P], ident[0:E, 0:E])
                last.then_inc(f_lt, 1)

            def pe_down(self, pe, e):
                pe.wait_ge(f_h, e + 1)
                for t in range(NT):
                    last = pe.matmul((YA, YB)[t // 2][:, (t % 2) * C:(t % 2) * C + C],
                                     self.h[:, e % 2, t * P:t * P + P], WD[:, e, :],
                                     start=e == 0 and t % 2 == 0, stop=e == NE - 1 and t % 2 == 1)
                last.then_inc(f_dn, 1)

            def pe_expert(self, pe, e):
                if e > 0:
                    pe.wait_ge(f_gd, e)
                else:
                    pe.wait_ge(f_th, 1)
                for w, bank, done in ((WG, GB, f_g), (WU, UBK, f_u)):
                    if w is WU and e > 0:
                        pe.wait_ge(f_h, e)
                    for a in range(NH):
                        last = pe.matmul(bank[:, :], w[:, a, e * EH:e * EH + EH], self.xt[:, a, :],
                                         start=a == 0, stop=a == NH - 1)
                    last.then_inc(done, 1)
                if e == NS:
                    pe.wait_ge(f_c3, 1)
                    cb = CBK[:, :].bitcast(bf16)
                    for t in range(NT):
                        last = pe.transpose(cb[:, t * P:t * P + P], C3[:, t, :], identb[:, :])
                    last.then_inc(f_ct, 1)
                    self.pe_down(pe, e - 1)
                    pe.wait_ge(f_cs, 1)
                    pe.matmul(CBK[:, :], K16["pick"][:, 0:P], self.c3t[:, :], start=True, stop=True).then_inc(f_c, 1)
                elif e > NS:
                    r = e - NS
                    pe.matmul(CBK[:, :], K16["pick"][:, r * P:r * P + P], self.c3t[:, :], start=True, stop=True)\
                      .then_inc(f_c, 1)
                    self.pe_down(pe, e - 1)
                elif e > 0:
                    self.pe_down(pe, e - 1)

            def pe_out(self, pe):
                self.pe_down(pe, NE - 1)

            def act_in(self, act):
                act.wait_ge(f_tr, 1)
                for a, bank in enumerate((YA, YB)):
                    act.copy(self.xt[:, a, :], bank[:, :]).then_inc(f_xt, 1)
                act.wait_ge(f_lg, 1)
                act.activation(self.lt[:, :], GB[0:E, :], ACT.Tanh, scale=0.5).then_inc(f_th, 1)

            def act_expert(self, act, e):
                act.wait_ge(f_g, e + 1)
                if e > 0:
                    act.wait_ge(f_gd, e)
                act.activation(self.th[:, :], GB[:, :], ACT.Tanh, scale=0.5).then_inc(f_tanh, 1)
                if e == NS:
                    act.wait_ge(f_ct, 1)
                    act.copy(self.c3t[:, :], CBK[:, :].bitcast(bf16)[:, 0:T]).then_inc(f_cs, 1)

            def dve_in(self, dve, link):
                layer_norm(dve, link, self.src, self.work, f_var, f_rstd, self.xn, f_xn)
                dve.wait_ge(f_lt, 1)
                link(dve.tensor_scalar(self.sc[:, :], CBK[:, 0:NT * E], 0.5, 0.5, ALU.mult, ALU.add))
                sc4 = self.sc[:, :].rearrange("p (t e) -> p t e", e=E)
                link(dve.tensor_tensor(self.scb[:, :].rearrange("p (t e) -> p t e", e=E), sc4,
                                       EB[:, :].unsqueeze(1).to_broadcast([P, NT, E]), ALU.add))
                g4 = self.scb[:, :].rearrange("p (g e) -> p g e", e=4)
                dve.tensor_tensor(self.pair[:, :, 0:3], g4[:, :, 0:3], g4[:, :, 1:4], ALU.add)
                dve.tensor_tensor(self.pair[:, :, 3:5], g4[:, :, 0:2], g4[:, :, 2:4], ALU.add)
                link(dve.tensor_tensor(self.pair[:, :, 5:6], g4[:, :, 0:1], g4[:, :, 3:4], ALU.add))
                link(dve.tensor_reduce(self.gs[:, 0:16], self.pair[:, :, :], AX.X, ALU.max))

                def ranks(values, n, low, ranks_out):
                    v = values.rearrange("p (t e) -> p t e", e=n)
                    mine = v.unsqueeze(3).to_broadcast([P, NT, n, n])
                    other = v.unsqueeze(2).to_broadcast([P, NT, n, n])
                    gt = self.gt[:, :, 0:n, 0:n]
                    eq = self.eq[:, :, 0:n, 0:n]
                    dve.tensor_tensor(gt, other, mine, ALU.is_gt)
                    link(dve.tensor_tensor(eq, other, mine, ALU.is_equal))
                    lo = low.rearrange("p (a b) -> p a b", b=n).unsqueeze(1).to_broadcast([P, NT, n, n])
                    link(dve.tensor_tensor(eq, eq, lo, ALU.mult))
                    link(dve.tensor_tensor(gt, gt, eq, ALU.add))
                    link(dve.tensor_reduce(ranks_out.rearrange("p (t e) -> p t e", e=n), gt, AX.X, ALU.add))

                ranks(self.gs[:, 0:16], 4, K32["group_low"][:, :], self.rk[:, 0:16])
                link(dve.tensor_scalar(self.gs[:, 16:32], self.rk[:, 0:16], 1.5, None, ALU.is_lt))
                link(dve.tensor_tensor(self.wt[:, :].rearrange("p (g e) -> p g e", e=4), g4,
                                       self.gs[:, 16:32].unsqueeze(2).to_broadcast([P, 16, 4]), ALU.mult))
                ranks(self.wt[:, :], E, K32["expert_low"][:, :], self.rk[:, :])
                link(dve.scalar_tensor_tensor(self.cw[:, :], self.rk[:, :], 3.5, self.sc[:, :], ALU.is_lt, ALU.mult))
                cw4 = self.cw[:, :].rearrange("p (t e) -> p t e", e=E)
                link(dve.tensor_reduce(self.sum[:, 0:NT], cw4, AX.X, ALU.add))
                link(dve.tensor_scalar(self.sum[:, 0:NT], self.sum[:, 0:NT], 1e-20, None, ALU.add))
                link(dve.reciprocal(self.sum[:, NT:], self.sum[:, 0:NT]))
                link(dve.tensor_tensor(cw4, cw4, self.sum[:, NT:].unsqueeze(2).to_broadcast([P, NT, E]), ALU.mult))
                link(dve.tensor_scalar(self.cw[:, :], self.cw[:, :], 2.5, None, ALU.mult))
                link(dve.tensor_copy(C3[:, :, 0:E], cw4))
                link(dve.tensor_tensor(cw4, cw4, C3[:, :, 0:E], ALU.subtract))
                link(dve.tensor_copy(C3[:, :, E:2 * E], cw4))
                link(dve.tensor_tensor(cw4, cw4, C3[:, :, E:2 * E], ALU.subtract))
                dve.tensor_copy(C3[:, :, 2 * E:3 * E], cw4).then_inc(f_c3, 1)

            def dve_expert(self, dve, link, e):
                dve.wait_ge(f_tanh, e + 1)
                if e > 0:
                    dve.wait_ge(f_h, e)
                dve.scalar_tensor_tensor(self.s[:, 0, :], self.th[:, :], 1.0, GB[:, :], ALU.add, ALU.mult)\
                   .then_inc(f_gd, 1)
                dve.wait_ge(f_gd, e + 1)
                dve.wait_ge(f_u, e + 1)
                if e >= 2:
                    dve.wait_ge(f_dn, e - 1)
                if e < NS:
                    dve.scalar_tensor_tensor(self.h[:, e % 2, :], UBK[:, :], 0.5, self.s[:, 0, :],
                                             ALU.mult, ALU.mult).then_inc(f_h, 1)
                else:
                    link(dve.scalar_tensor_tensor(self.s[:, 1, :], UBK[:, :], 0.5, self.s[:, 0, :],
                                                  ALU.mult, ALU.mult))
                    dve.wait_ge(f_c, e - NS + 1)
                    dve.tensor_tensor(self.h[:, e % 2, :], self.s[:, 1, :], CBK[:, :], ALU.mult).then_inc(f_h, 1)

            def dve_out(self, dve):
                dve.wait_ge(f_dn, NE)
                for n, bank in enumerate((YA, YB)):
                    dve.tensor_tensor(self.dst[:, 2 * n:2 * n + 2, :], self.src[:, 2 * n:2 * n + 2, :],
                                      bank[:, :].rearrange("p (t c) -> p t c", c=C), ALU.add).then_inc(f_res, 1)

            def pool_in(self, pool):
                root(pool, self.work, f_var, f_rstd)

        def rwkv_ffn(row, rwkv=True, ffn_row=None):
            with ExitStack() as stack:
                def t(n, shape, dt=f32):
                    return sb("a_" + n, shape, dt, stack)

                ffn = None
                if ffn_row is not None:
                    ffn = Ffn("fa", X3, X3, stack)
                if rwkv:
                    work, ywork = norm_work("a", stack), norm_work("ay", stack)
                    XN, XT, XX = t("xn", [P, NT, C]), t("xt", [P, NH, T + 1]), t("xx", [P, NH, T])
                    TM = t("tm", [P, T])
                    XF = t("xf", [P, 2, NH, T])
                    DT = t("dt", [P, T])
                    WE = t("we", [P, NT * RH])
                    WX = XN[:, :, :].rearrange("p t c -> p (t c)")
                    EW = XF
                    KK, VV, RT, KT = t("k", [P, NT, C]), t("v", [P, NT, C]), t("rT", [P, NH, T]), t("kT", [P, NH, T])
                    RX = t("rx", [P, NH, 8, P])
                    WM = t("wm", [P, 2, 512])
                    DEC, WS = t("dec", [P, 2, NT * RH]), t("ws", [P, NH, NT, 2])
                    S = t("s", [P, 2, NH, P])
                    SM, Y, YN, YT, DV = t("sm", [P, NH, P]), t("y", [P, C]), t("yn", [P, C]), t("yT", [P, C]), t("dv", [P, C])
                PR = XX if rwkv else None

                fills = ["x0", "x1", "m"]
                for f in range(4):
                    fills += [("mix", f, 0), ("mix", f, 1)]
                    fills += {0: ["dt"], 1: ["k0", "k1"], 2: ["v0", "v1"], 3: ["r0", "r1"]}[f]
                fills += ["w", "dec", "kT0", "kT1"]
                for i in range(NT):
                    fills += [("arg", i, 0), ("arg", i, 1), ("score", i, 0), ("score", i, 1),
                              ("diag", i), ("kv", i), ("y", i), ("yT", i), ("o", i)]
                TURN = turns(fills)

                def bank(name):
                    return RING[TURN[name] % 3]

                def take(pe, name):
                    n = TURN[name]
                    if n >= 3:
                        pe.wait_ge(emptied[n % 3], n // 3)
                    return RING[n % 3]

                def wait_fill(eng, name):
                    eng.wait_ge(filled, TURN[name] + 1)
                    return bank(name)

                def empty(name):
                    return emptied[TURN[name] % 3]

                with nc.Block() as block:
                    @block.sync
                    def _(sp):
                        if rwkv:
                            sp.dma_start(X1[:, :, :], x_rows[row]).then_inc(x_in, 16)
                        if ffn:
                            sp.wait_ge(f_res, 2)
                            sp.dma_start(out_rows[ffn_row], X3[:, :, :]).then_inc(f_out, 16)
                            sp.wait_ge(f_out, 16)
                        if rwkv:
                            sp.wait_ge(x_in, 16)

                    @block.tensor
                    def _(pe):
                        def mix_in():
                            pe.wait_ge(r_xn, 1)
                            for a in range(NH):
                                b = take(pe, f"x{a}")
                                for i in range(NT):
                                    last = pe.transpose(b[:, i * P:i * P + P], XN[:, i, a * P:a * P + P], ident[:, :])
                                last.then_inc(filled, 1)
                            b = take(pe, "m")
                            pe.wait_ge(r_mixin, 1)
                            for a in range(NH):
                                last = pe.matmul(b[:, :], W1[:, a, :], XF[:, 1, a, :], start=a == 0, stop=a == NH - 1)
                            last.then_inc(filled, 1)

                        def mix(f):
                            pe.wait_ge(r_m, 1)
                            for a in range(NH):
                                pe.matmul(take(pe, ("mix", f, a))[:, :], W2[:, f, a * P:a * P + P], TM[:, :],
                                          start=True, stop=True).then_inc(filled, 1)
                            pe.wait_ge(r_mixed, f + 1)
                            xf = XF[:, f % 2, :, :]
                            if f == 0:
                                b = take(pe, "dt")
                                for a in range(NH):
                                    last = pe.matmul(b[0:64, :], DW1[:, a, :], xf[:, a, :], start=a == 0, stop=a == NH - 1)
                                last.then_inc(filled, 1)
                            elif f < 3:
                                for n in range(2):
                                    b = take(pe, f"{'_kv'[f]}{n}")
                                    for j in range(2):
                                        i = 2 * n + j
                                        for a in range(NH):
                                            last = pe.matmul(b[:, j * C:j * C + C], xf[:, a, i * P:i * P + P],
                                                             WR[:, f, a, :], start=a == 0, stop=a == NH - 1)
                                    last.then_inc(filled, 1)
                            else:
                                for n in range(NH):
                                    b = take(pe, f"r{n}")
                                    for a in range(NH):
                                        last = pe.matmul(b[:, :], WR[:, 0, a, n * P:n * P + P], xf[:, a, :],
                                                         start=a == 0, stop=a == NH - 1)
                                    last.then_inc(filled, 1)

                        def decay():
                            b = take(pe, "w")
                            pe.wait_ge(r_dt, 1)
                            for i in range(NT):
                                last = pe.matmul(b[:, i * RH:i * RH + RH], DT[:, i * P:i * P + P], DWM[:, :],
                                                 start=True, stop=True)
                            last.then_inc(filled, 1)
                            b = take(pe, "dec")
                            pe.wait_ge(r_we, 1)
                            pe.matmul(b[:, 0:64], K32["before"][:, :], WE[:, :], start=True, stop=True)
                            pe.matmul(b[:, 64:128], K32["after"][:, :], WE[:, :], start=True, stop=True)
                            pe.wait_ge(r_wx, 1)
                            for i in range(NT):
                                for a in range(NH):
                                    rates = WX[:, i * C + a * P:i * C + a * P + P]
                                    at = 128 + a * 8 + 2 * i
                                    last = pe.matmul(b[:, at:at + 2], rates, K32["chunks"][:, :], start=True, stop=True)
                            last.then_inc(filled, 1)

                        def prep():
                            pe.wait_ge(r_k, 2)
                            for a in range(NH):
                                b = take(pe, f"kT{a}")
                                for i in range(NT):
                                    last = pe.transpose(b[:, i * P:i * P + P], KK[:, i, a * P:a * P + P], ident[:, :])
                                last.then_inc(filled, 1)

                        def tile_a(i):
                            for n in range(2):
                                b = take(pe, ("arg", i, n))
                                pe.wait_ge(r_wm, 2 * i + n + 1)
                                pe.matmul(b[:, :], K32["after"][:, :], WM[:, n, :], start=True, stop=False)
                                pe.matmul(b[:, :], identb[:, :], K16["forbid"][:, :], start=False, stop=True)\
                                  .then_inc(filled, 1)
                            pe.wait_ge(r_kt, 2)
                            pe.wait_ge(r_rx, i + 1)
                            for a in range(NH):
                                b = take(pe, ("score", i, a))
                                for c in range(2):
                                    at = i * P + c * RQ
                                    last = pe.matmul(b[c * RQ:c * RQ + RQ, :], KT[:, a, at:at + RQ],
                                                     RX[:, a, :, c * RQ:c * RQ + RQ], start=True, stop=True)
                                last.then_inc(filled, 1)

                        def tile_b(i):
                            b = take(pe, ("y", i))
                            pe.wait_ge(r_p, 2 * i + 2)
                            pe.wait_ge(r_v, 2)
                            for c in range(2):
                                rows = slice(c * RQ, c * RQ + RQ)
                                for h in range(RH):
                                    last = pe.matmul(b[rows, h * RN:h * RN + RN],
                                                     EW[rows, i % 2, h // 8, (h % 8) * RQ:(h % 8) * RQ + RQ],
                                                     VV[rows, i, h * RN:h * RN + RN], start=True, stop=True)
                            last.then_inc(r_used, 1)
                            for c in range(2):
                                n = 2 * i + c
                                pe.wait_ge(r_s, n + 1)
                                at = i * P + c * RQ
                                for a in range(NH):
                                    last = pe.matmul(b[c * RQ:c * RQ + RQ, C + a * P:C + a * P + P],
                                                     RT[:, a, at:at + RQ], S[:, c, a, :], start=True, stop=True)
                                if c == 0:
                                    kb = take(pe, ("diag", i))
                                    pe.wait_ge(r_prod, 1)
                                    for a in range(NH):
                                        last = pe.matmul(kb[:, a * P:a * P + P], PR[:, a, i * P:i * P + P], UB[:, a, :],
                                                         start=True, stop=True)
                                    last.then_inc(filled, 1)
                                    kb = take(pe, ("kv", i))
                                    pe.wait_ge(r_kw, 2 * i + 2)
                                    for cc in range(2):
                                        for a in range(NH):
                                            last = pe.matmul(kb[:, cc * C + a * P:cc * C + a * P + P],
                                                             KWP[:, cc, a * P:a * P + P], VV[:, i, a * P:a * P + P],
                                                             start=True, stop=True)
                                    last.then_inc(filled, 1)
                            last.then_inc(filled, 1)

                        def tile_c(i):
                            b = take(pe, ("yT", i))
                            pe.wait_ge(r_yn, i + 1)
                            for a in range(NH):
                                last = pe.transpose(b[:, a * P:a * P + P], YN[:, a * P:a * P + P], ident[:, :])
                            last.then_inc(filled, 1)
                            b = take(pe, ("o", i))
                            pe.wait_ge(r_yt, 2 * i + 2)
                            for a in range(NH):
                                last = pe.matmul(b[:, 0:C], YT[:, a * P:a * P + P], WR[:, 3, a, :],
                                                 start=a == 0, stop=a == NH - 1)
                            last.then_inc(filled, 1)

                        stages = dict(mix_in=mix_in, mix=mix, decay=decay, prep=prep, tile_a=tile_a, tile_b=tile_b,
                                      tile_c=tile_c)
                        for step in ORDER_A:
                            if isinstance(step, int):
                                if ffn:
                                    ffn.pe_expert(pe, step)
                            elif step[0] == "ffn_in":
                                if ffn:
                                    ffn.pe_in(pe)
                            elif step[0] == "ffn_out":
                                if ffn:
                                    ffn.pe_out(pe)
                            elif rwkv and step[0] in stages:
                                stages[step[0]](*step[1:])

                    @block.scalar
                    def _(act):
                        def mix_in():
                            for a in range(NH):
                                b = wait_fill(act, f"x{a}")
                                act.copy(XT[:, a, 1:T + 1], b[:, :]).then_inc(r_xt, 1)
                                act.wait_ge(r_xt, a + 1)
                                act.sem_inc(empty(f"x{a}"), 1)
                            b = wait_fill(act, "m")
                            act.activation(TM[:, :], b[:, :], ACT.Tanh).then_inc(r_m, 1)
                            act.wait_ge(r_m, 1)
                            act.sem_inc(empty("m"), 1)

                        def mix(f):
                            if f == 0:
                                b = wait_fill(act, "dt")
                                act.activation(DT[0:64, :], b[0:64, :], ACT.Tanh).then_inc(r_dt, 1)
                                act.wait_ge(r_dt, 1)
                                act.sem_inc(empty("dt"), 1)
                                return
                            done = (None, r_k, r_v, r_r)[f]
                            for n in range(2):
                                b = wait_fill(act, f"{'_kvr'[f]}{n}")
                                if f < 3:
                                    dst = (None, KK, VV)[f][:, 2 * n:2 * n + 2, :]
                                    act.copy(dst, b[:, :].rearrange("p (t c) -> p t c", c=C)).then_inc(done, 1)
                                else:
                                    act.copy(RT[:, n, :], b[:, :]).then_inc(done, 1)
                                act.wait_ge(done, n + 1)
                                act.sem_inc(empty(f"{'_kvr'[f]}{n}"), 1)

                        def decay():
                            b = wait_fill(act, "w")
                            act.activation(WE[:, :], b[:, 0:NT * RH], ACT.Exp).then_inc(r_we, 1)
                            act.wait_ge(r_we, 1)
                            act.sem_inc(empty("w"), 1)
                            b = wait_fill(act, "dec")
                            act.activation(DEC[:, :, :], b[:, 0:128].rearrange("p (a n) -> p a n", a=2), ACT.Exp)\
                               .then_inc(r_dec, 1)
                            act.activation(WS[:, :, :, :].rearrange("p a t c -> p (a t c)"), b[:, 128:144], ACT.Exp)\
                               .then_inc(r_ws, 1)
                            act.wait_ge(r_ws, 1)
                            act.sem_inc(empty("dec"), 1)

                        def prep():
                            for a in range(NH):
                                b = wait_fill(act, f"kT{a}")
                                act.copy(KT[:, a, :], b[:, :]).then_inc(r_kt, 1)
                                act.wait_ge(r_kt, a + 1)
                                act.sem_inc(empty(f"kT{a}"), 1)

                        def tile_a(i):
                            for n in range(2):
                                b = wait_fill(act, ("arg", i, n))
                                if i >= 2:
                                    act.wait_ge(r_used, i - 1)
                                act.activation(EW[:, i % 2, n, :], b[:, :], ACT.Exp).then_inc(r_e, 1)
                                act.wait_ge(r_e, 2 * i + n + 1)
                                act.sem_inc(empty(("arg", i, n)), 1)

                        def tile_c(i):
                            b = wait_fill(act, ("yT", i))
                            for a in range(NH):
                                act.activation(YT[:, a * P:a * P + P], b[:, a * P:a * P + P], ACT.Identity,
                                               bias=LNA[:, 1, a:a + 1], scale=LNA[:, 0, a:a + 1]).then_inc(r_yt, 1)
                            act.wait_ge(r_yt, 2 * i + 2)
                            act.sem_inc(empty(("yT", i)), 1)

                        stages = dict(mix_in=mix_in, mix=mix, decay=decay, prep=prep, tile_a=tile_a, tile_c=tile_c)
                        for step in ORDER_A:
                            if isinstance(step, int):
                                if ffn:
                                    ffn.act_expert(act, step)
                            elif step[0] == "ffn_in":
                                if ffn:
                                    ffn.act_in(act)
                            elif rwkv and step[0] in stages:
                                stages[step[0]](*step[1:])

                    @block.vector
                    def _(dve):
                        link = linker(dve, d_chain)

                        def norm():
                            dve.wait_ge(x_in, 16)
                            dve.memset(XT[:, :, 0:1], 0.0)
                            dve.memset(DT[64:128, :], 1.0)
                            dve.memset(S[:, 0, :, :], 0.0).then_inc(r_s, 1)
                            layer_norm(dve, link, X1, work, r_var, r_rstd, XN, r_xn)

                        def mix_in():
                            dve.wait_ge(r_xt, 2)
                            dve.tensor_tensor(XX[:, :, :], XT[:, :, 0:T], XT[:, :, 1:T + 1], ALU.subtract).then_inc(r_xx, 1)
                            dve.wait_ge(r_xx, 1)
                            for a in range(NH):
                                last = dve.scalar_tensor_tensor(XF[:, 1, a, :], XX[:, a, :], MAA[:, 0, a:a + 1],
                                                                XT[:, a, 1:T + 1], ALU.mult, ALU.add)
                            last.then_inc(r_mixin, 1)

                        def mix(f):
                            if f >= 1:
                                dve.wait_ge(filled, TURN[{1: "m", 2: "dt", 3: "k1"}[f]] + 1)
                            for a in range(NH):
                                b = wait_fill(dve, ("mix", f, a))
                                dve.scalar_tensor_tensor(XF[:, f % 2, a, :], b[:, :], MAA[:, f + 1, a:a + 1],
                                                         XX[:, a, :], ALU.add, ALU.mult).then_inc(r_half, 1)
                                dve.wait_ge(r_half, 2 * f + a + 1)
                                dve.sem_inc(empty(("mix", f, a)), 1)
                            xf = XF[:, f % 2, :, :]
                            dve.tensor_tensor(xf, xf, XT[:, :, 1:T + 1], ALU.add).then_inc(r_mixed, 1)

                        def spread(i):
                            dve.wait_ge(r_r, 2)
                            if i >= 1:
                                dve.wait_ge(filled, TURN["score", i - 1, 1] + 1)
                            for a in range(NH):
                                last = dve.tensor_tensor(
                                    RX[:, a, :, :], RT[:, a, i * P:i * P + P].unsqueeze(1).to_broadcast([P, 8, P]),
                                    K32["heads8"][:, :].unsqueeze(2).to_broadcast([P, 8, P]), ALU.mult)
                            last.then_inc(r_rx, 1)

                        def decay():
                            dve.wait_ge(r_we, 1)
                            dve.tensor_copy(WX[:, :].rearrange("p (h n) -> p h n", n=RN),
                                            WE[:, :].unsqueeze(2).to_broadcast([P, NT * RH, RN])).then_inc(r_wx, 1)

                        def prep():
                            spread(0)

                        def tile_a(i):
                            for n in range(2):
                                b = wait_fill(dve, ("score", i, n))
                                dve.wait_ge(r_e, 2 * i + n + 1)
                                ew = EW[:, i % 2, n, :]
                                dve.tensor_tensor(ew, ew, b[:, :], ALU.mult).then_inc(r_p, 1)
                                dve.wait_ge(r_p, 2 * i + n + 1)
                                dve.sem_inc(empty(("score", i, n)), 1)
                            if i < NT - 1:
                                spread(i + 1)

                        def tile_b(i):
                            b = wait_fill(dve, ("diag", i))
                            link(dve.tensor_tensor(DV[:, :], b[:, 0:C], VV[:, i, :], ALU.mult))
                            dve.sem_inc(empty(("diag", i)), 1)
                            b = wait_fill(dve, ("kv", i))
                            dve.wait_ge(r_ws, 1)
                            for c in range(2):
                                n = 2 * i + c
                                link(dve.tensor_tensor(SM[:, :, :], b[:, c * C:c * C + C].rearrange("p (a n) -> p a n", a=NH),
                                                       K32["same16"][:, :].unsqueeze(1).to_broadcast([P, NH, P]), ALU.mult))
                                if c == 1:
                                    dve.sem_inc(empty(("kv", i)), 1)
                                if n == 2 * NT - 1:
                                    break
                                if c == 0 and i >= 1:
                                    dve.wait_ge(filled, TURN["y", i - 1] + 1)
                                for a in range(NH):
                                    last = dve.scalar_tensor_tensor(S[:, (c + 1) % 2, a, :], S[:, c, a, :],
                                                                    WS[:, a, i, c:c + 1], SM[:, a, :], ALU.mult, ALU.add)
                                last.then_inc(r_s, 1)
                                dve.wait_ge(r_s, n + 2)
                            b = wait_fill(dve, ("y", i))
                            dve.wait_ge(r_dec, 1)
                            dec = DEC[:, 0, i * RH:i * RH + RH].unsqueeze(2).to_broadcast([P, RH, RN])
                            link(dve.tensor_tensor(Y[:, :].rearrange("p (h n) -> p h n", n=RN),
                                                   b[:, C:2 * C].rearrange("p (h n) -> p h n", n=RN), dec, ALU.mult))
                            link(dve.tensor_tensor(Y[:, :], Y[:, :], b[:, 0:C], ALU.add))
                            dve.sem_inc(empty(("y", i)), 1)
                            link(dve.tensor_tensor(Y[:, :], Y[:, :], DV[:, :], ALU.add))
                            stats, mv, ve = ywork
                            link(dve.bn_stats(stats[:, i, :], Y[:, :]))
                            link(dve.bn_aggr(mv[:, i, :], stats[:, i, :]))
                            dve.tensor_scalar(ve[:, i, 0:1], mv[:, i, 1:2], EPS, None, ALU.add).then_inc(r_yv, 1)
                            dve.wait_ge(r_yr, i + 1)
                            if i >= 1:
                                dve.wait_ge(filled, TURN["yT", i - 1] + 1)
                            dve.tensor_scalar(YN[:, :], Y[:, :], mv[:, i, 0:1], ve[:, i, 1:2], ALU.subtract, ALU.mult)\
                               .then_inc(r_yn, 1)
                            dve.wait_ge(r_yn, i + 1)

                        def tile_c(i):
                            b = wait_fill(dve, ("o", i))
                            link(dve.tensor_tensor(X1[:, i, :], X1[:, i, :], b[:, 0:C], ALU.add))
                            dve.sem_inc(empty(("o", i)), 1)

                        stages = dict(norm=norm, mix_in=mix_in, mix=mix, decay=decay, prep=prep, tile_a=tile_a, tile_b=tile_b, tile_c=tile_c)
                        for step in ORDER_A:
                            if isinstance(step, int):
                                if ffn:
                                    ffn.dve_expert(dve, link, step)
                            elif step[0] == "ffn_in":
                                if ffn:
                                    ffn.dve_in(dve, link)
                            elif step[0] == "ffn_out":
                                if ffn:
                                    ffn.dve_out(dve)
                            elif rwkv and step[0] in stages:
                                stages[step[0]](*step[1:])

                    @block.gpsimd
                    def _(pool):
                        def norm():
                            root(pool, work, r_var, r_rstd)

                        def rates(i):
                            for n in range(2):
                                if i >= 1:
                                    pool.wait_ge(filled, TURN["arg", i - 1, n] + 1)
                                pool.tensor_tensor(
                                    WM[:, n, :].rearrange("p (h q) -> p h q", q=RQ),
                                    WE[:, i * RH + 8 * n:i * RH + 8 * n + 8].unsqueeze(2).to_broadcast([P, 8, RQ]),
                                    K32["earlier"][:, :].unsqueeze(1).to_broadcast([P, 8, RQ]), ALU.mult).then_inc(r_wm, 1)

                        def decayed(i):
                            if i >= 1:
                                pool.wait_ge(filled, TURN["kv", i - 1] + 1)
                            pool.wait_ge(r_wm, 2 * min(i + 1, NT))
                            for c in range(2):
                                rows = slice(c * RQ, c * RQ + RQ)
                                pool.tensor_tensor(
                                    KWP[rows, c, :].rearrange("p (h n) -> p h n", n=RN),
                                    KK[rows, i, :].rearrange("p (h n) -> p h n", n=RN),
                                    DEC[rows, 1, i * RH:i * RH + RH].unsqueeze(2).to_broadcast([RQ, RH, RN]), ALU.mult)\
                                    .then_inc(r_kw, 1)
                                pool.wait_ge(r_kw, 2 * i + c + 1)

                        def prep():
                            pool.wait_ge(r_we, 1)
                            rates(0)
                            pool.wait_ge(r_dec, 1)
                            pool.wait_ge(r_k, 2)
                            decayed(0)
                            pool.wait_ge(r_kt, 2)
                            pool.wait_ge(r_r, 2)
                            pool.wait_ge(r_mixed, 4)
                            pool.tensor_tensor(PR[:, :, :], RT[:, :, :], KT[:, :, :], ALU.mult).then_inc(r_prod, 1)

                        def tile_a(i):
                            if i < NT - 1:
                                rates(i + 1)

                        def tile_b(i):
                            if i < NT - 1:
                                decayed(i + 1)
                            pool.wait_ge(r_yv, i + 1)
                            ve = ywork[2]
                            pool.tensor_tensor(ve[:, i, 1:2], ve[:, i, 0:1], K32["nhalf"][:, 0:1], ALU.pow)\
                                .then_inc(r_yr, 1)

                        stages = dict(norm=norm, prep=prep, tile_a=tile_a, tile_b=tile_b)
                        for step in ORDER_A:
                            if isinstance(step, int):
                                continue
                            if step[0] == "ffn_in":
                                if ffn:
                                    ffn.pool_in(pool)
                            elif rwkv and step[0] in stages:
                                stages[step[0]](*step[1:])
            end_block()

        def delta_ffn(delta=True, ffn_on=True):
            with ExitStack() as stack:
                def t(n, shape, dt=f32):
                    return sb("b_" + n, shape, dt, stack)

                ffn = Ffn("fb", X1, X2, stack) if ffn_on else None
                if delta:
                    work, owork = norm_work("b", stack), norm_work("bo", stack)
                    XN, XT = t("xn", [P, NT, C]), t("xt", [P, NH, T])
                    Q, KH, KB, VB = t("q", [P, NT, C]), t("kh", [P, NT, C]), t("kb", [P, 2, C]), t("vb", [P, NT, C])
                    SQ, SG, SS = t("sq", [P, C]), t("sg", [P, 2, C + DH]), t("ss", [P, NT, 2, DH])
                    QT, KHT, KBT = t("qT", [P, NH, T]), t("khT", [P, NH, T]), t("kbT", [P, NH, T])
                    QX, KX = t("qx", [P, NH, 4, P]), t("kx", [P, NH, 4, P])
                    TMP = QX[:, :, :, :].rearrange("p a h n -> p (a h n)").rearrange("p (c j) -> p c j", j=DQ)
                    AS = t("as", [P, 2, C])
                    PT = t("pT", [P, NT, DH, DQ])
                    TI = t("ti", [P, NT, DH, DQ])
                    S = t("s", [P, NH, P])
                    O = XN

                fills = ["x0", "x1"]
                for i in range(NT):
                    fills += [("kv", i), ("qb", i), ("t1", i), ("t2", i), ("ap", i)]
                TURN = turns(fills)
                KS, OB, SP = RING

                def take(pe, name):
                    n = TURN[name]
                    if n >= 3:
                        pe.wait_ge(emptied[n % 3], n // 3)
                    return RING[n % 3]

                def wait_fill(eng, name):
                    eng.wait_ge(filled, TURN[name] + 1)
                    return RING[TURN[name] % 3]

                def empty(name):
                    return emptied[TURN[name] % 3]

                def uses(k):
                    return len([n for n in TURN.values() if n % 3 == k])

                with nc.Block() as block:
                    @block.sync
                    def _(sp):
                        if not delta:
                            return
                        a_v = a_dram.rearrange("(t c h) i j -> t c i h j", t=NT, c=4)
                        t_v = t_dram.rearrange("(t c h) i j -> c i t h j", t=NT, c=4)
                        for i in range(NT):
                            sp.wait_ge(d_a, i + 1)
                            for c in range(4):
                                sp.dma_start(a_v[i, c], AS[32 * c:32 * c + 32, i % 2, :].rearrange("p (h j) -> p h j", h=DH))\
                                  .then_inc(d_stores[i % 2], 16)
                        for parity in d_stores:
                            sp.wait_ge(parity, 8 * 16)
                        sp.dma_start(MAT[:, :, :], a_dram).then_inc(d_mat, 16)
                        sp.wait_ge(d_inv, 31)
                        sp.dma_start(t_dram, INV[:, :, :]).then_inc(d_tst, 16)
                        sp.wait_ge(d_tst, 16)
                        for c in range(4):
                            for i in range(NT):
                                sp.dma_start(TI[32 * c:32 * c + 32, i, :, :], t_v[c][:, i, :, :]).then_inc(d_tld, 16)
                        sp.wait_ge(d_tld, 16 * 16)

                    @block.tensor
                    def _(pe):
                        def project_in():
                            pe.wait_ge(d_xn, 1)
                            for a in range(NH):
                                b = take(pe, f"x{a}")
                                for i in range(NT):
                                    last = pe.transpose(b[:, i * P:i * P + P], XN[:, i, a * P:a * P + P], ident[:, :])
                                last.then_inc(filled, 1)

                        def project(i):
                            pe.wait_ge(d_xt, 2)
                            b = take(pe, ("kv", i))
                            for a in range(NH):
                                last = pe.matmul(b[:, :], XT[:, a, i * P:i * P + P], WKV[:, a, :], start=a == 0, stop=a == NH - 1)
                            last.then_inc(filled, 1)
                            b = take(pe, ("qb", i))
                            for a in range(NH):
                                last = pe.matmul(b[:, 0:C + DH], XT[:, a, i * P:i * P + P], WQB[:, a, :],
                                                 start=a == 0, stop=a == NH - 1)
                            last.then_inc(filled, 1)

                        def pairs(i):
                            pe.wait_ge(d_kh, i + 1)
                            b = take(pe, ("t1", i))
                            for a in range(NH):
                                pe.transpose(b[:, a * P:a * P + P], Q[:, i, a * P:a * P + P], ident[:, :])
                                last = pe.transpose(b[:, C + a * P:C + a * P + P], KH[:, i, a * P:a * P + P], ident[:, :])
                            last.then_inc(filled, 1)
                            b = take(pe, ("t2", i))
                            for a in range(NH):
                                last = pe.transpose(b[:, a * P:a * P + P], KB[:, i % 2, a * P:a * P + P], ident[:, :])
                            last.then_inc(filled, 1)
                            pe.wait_ge(d_turn, 3 * i + 3)
                            pe.wait_ge(d_exp, i + 1)
                            b = take(pe, ("ap", i))
                            for c in range(4):
                                rows, toks = slice(32 * c, 32 * c + 32), slice(i * P + 32 * c, i * P + 32 * c + 32)
                                for a in range(NH):
                                    pe.matmul(b[rows, a * P:a * P + P], KBT[:, a, toks], KX[:, a, :, rows], start=True, stop=True)
                                    last = pe.matmul(b[rows, C + a * P:C + a * P + P], KHT[:, a, toks], QX[:, a, :, rows],
                                                     start=True, stop=True)
                            last.then_inc(filled, 1)

                        def solve(g):
                            i, c = g // 4, g % 4
                            rows, toks = slice(32 * c, 32 * c + 32), slice(g * 32, g * 32 + 32)
                            if g == 0:
                                for k in range(3):
                                    pe.wait_ge(emptied[k], uses(k))
                                pe.wait_ge(d_tld, 16 * 16)
                            pe.wait_ge(d_s, g + 1)
                            for a in range(NH):
                                last = pe.matmul(KS[rows, a * P:a * P + P], KBT[:, a, toks], S[:, a, :], start=True, stop=True)
                            last.then_inc(d_ks, 1)
                            if c == 0 and i > 0:
                                pe.wait_ge(d_os, i)
                            for a in range(NH):
                                pe.matmul(OB[rows, a * P:a * P + P], QT[:, a, toks], S[:, a, :], start=a == 0, stop=False)
                            pe.wait_ge(d_r, g + 1)
                            for h in range(DH):
                                last = pe.matmul(KS[rows, C + 32 * h:C + 32 * h + 32], TI[:, i, h, :],
                                                 RP[:, c, 32 * h:32 * h + 32], start=True, stop=True)
                            last.then_inc(d_v, 1)

                        def update(g):
                            i, c = g // 4, g % 4
                            rows = slice(32 * c, 32 * c + 32)
                            pe.wait_ge(d_vs, g + 1)
                            if g < 15:
                                for a in range(NH):
                                    last = pe.matmul(SP[:, a * P:a * P + P], KH[:, i, a * P:a * P + P],
                                                     VP[:, c, a * P:a * P + P], start=g == 0 and a == 0,
                                                     stop=True, skip_group_check=True)
                                last.then_inc(d_up, 1)
                            for h in range(DH):
                                last = pe.matmul(OB[rows, 32 * h:32 * h + 32], PT[:, i, h, :],
                                                 VP[:, c, 32 * h:32 * h + 32], start=False, stop=h == DH - 1)
                            if c == 3:
                                last.then_inc(d_o, 1)

                        stages = dict(project_in=project_in, project=project, pairs=pairs, solve=solve, update=update)
                        for step in ORDER_B:
                            if isinstance(step, int):
                                if ffn:
                                    ffn.pe_expert(pe, step)
                            elif step[0] == "ffn_in":
                                if ffn:
                                    ffn.pe_in(pe)
                            elif step[0] == "ffn_out":
                                if ffn:
                                    ffn.pe_out(pe)
                            elif delta and step[0] in stages:
                                stages[step[0]](*step[1:])

                    @block.scalar
                    def _(act):
                        link = linker(act, a_chain)

                        def project_in():
                            for a in range(NH):
                                b = wait_fill(act, f"x{a}")
                                act.copy(XT[:, a, :], b[:, :]).then_inc(d_xt, 1)
                                act.wait_ge(d_xt, a + 1)
                                act.sem_inc(empty(f"x{a}"), 1)

                        def project(i):
                            b = wait_fill(act, ("kv", i))
                            if i >= 1:
                                act.wait_ge(d_ss, i)
                            act.activation(SQ[:, :], b[:, 0:C], ACT.Square).then_inc(d_sq, 1)
                            if i >= 2:
                                act.wait_ge(d_kh, i - 1)
                            act.activation(SG[:, i % 2, 0:C], b[:, C:2 * C], ACT.Tanh, scale=0.5)
                            b = wait_fill(act, ("qb", i))
                            act.activation(SG[:, i % 2, C:C + DH], b[:, C:C + DH], ACT.Tanh, scale=0.5)
                            act.copy(Q[:, i, :], b[:, 0:C]).then_inc(d_qk, 1)
                            act.wait_ge(d_qk, i + 1)
                            act.sem_inc(empty(("qb", i)), 1)

                        def pairs(i):
                            b = wait_fill(act, ("t1", i))
                            toks = slice(i * P, i * P + P)
                            act.copy(QT[:, :, toks], b[:, 0:C].rearrange("p (a n) -> p a n", a=NH)).then_inc(d_turn, 1)
                            act.copy(KHT[:, :, toks], b[:, C:2 * C].rearrange("p (a n) -> p a n", a=NH)).then_inc(d_turn, 1)
                            act.wait_ge(d_turn, 3 * i + 2)
                            act.sem_inc(empty(("t1", i)), 1)
                            b = wait_fill(act, ("t2", i))
                            act.copy(KBT[:, :, toks], b[:, 0:C].rearrange("p (a n) -> p a n", a=NH)).then_inc(d_turn, 1)
                            act.wait_ge(d_turn, 3 * i + 3)
                            act.sem_inc(empty(("t2", i)), 1)
                            b = wait_fill(act, ("ap", i))
                            if i >= 2:
                                act.wait_ge(d_stores[i % 2], 64 * (i // 2))
                            act.copy(AS[:, i % 2, :], b[:, 0:C]).then_inc(d_a, 1)

                        def solve(g):
                            c = g % 4
                            rows = slice(32 * c, 32 * c + 32)
                            act.wait_ge(d_v, g + 1)
                            if g >= 4:
                                act.wait_ge(d_o, g // 4)
                            act.copy(VP[rows, c, :], KS[rows, C:2 * C]).then_inc(d_vs, 1)

                        def update(g):
                            if g % 4 == 3:
                                act.wait_ge(d_o, g // 4 + 1)
                                act.copy(O[:, g // 4, :], OB[:, 0:C]).then_inc(d_os, 1)

                        stages = dict(project_in=project_in, project=project, pairs=pairs, solve=solve, update=update)
                        for step in ORDER_B:
                            if isinstance(step, int):
                                if ffn:
                                    ffn.act_expert(act, step)
                            elif step[0] == "ffn_in":
                                if ffn:
                                    ffn.act_in(act)
                            elif delta and step[0] in stages:
                                stages[step[0]](*step[1:])

                    @block.vector
                    def _(dve):
                        link = linker(dve, d_chain)

                        def norm():
                            dve.memset(S[:, :, :], 0.0).then_inc(d_s, 1)
                            layer_norm(dve, link, X2L, work, d_var, d_rstd, XN, d_xn)

                        def project(i):
                            b = wait_fill(dve, ("kv", i))
                            dve.wait_ge(d_sq, i + 1)
                            link(dve.tensor_reduce(SS[:, i, 0, :], SQ[:, :].rearrange("p (h n) -> p h n", n=DN), AX.X, ALU.add))
                            dve.tensor_scalar(SS[:, i, 0, :], SS[:, i, 0, :], 1e-24, None, ALU.max).then_inc(d_ss, 1)
                            dve.wait_ge(d_qk, i + 1)
                            sg = SG[:, i % 2, :]
                            link(dve.tensor_scalar(sg, sg, 0.5, 0.5, ALU.mult, ALU.add))
                            beta = SG[:, i % 2, C:C + DH].unsqueeze(2).to_broadcast([P, DH, DN])
                            link(dve.tensor_tensor(VB[:, i, :], b[:, C:2 * C], SG[:, i % 2, 0:C], ALU.mult))
                            vb = VB[:, i, :].rearrange("p (h n) -> p h n", n=DN)
                            link(dve.tensor_tensor(vb, vb, beta, ALU.mult))
                            dve.wait_ge(d_rn, i + 1)
                            kh = KH[:, i, :].rearrange("p (h n) -> p h n", n=DN)
                            link(dve.tensor_tensor(kh, b[:, 0:C].rearrange("p (h n) -> p h n", n=DN),
                                                   SS[:, i, 1, :].unsqueeze(2).to_broadcast([P, DH, DN]), ALU.mult))
                            dve.sem_inc(empty(("kv", i)), 1)
                            if i >= 2:
                                dve.wait_ge(filled, TURN["t2", i - 2] + 1)
                            dve.tensor_tensor(KB[:, i % 2, :].rearrange("p (h n) -> p h n", n=DN), kh, beta, ALU.mult)\
                               .then_inc(d_kh, 1)

                        def pairs(i):
                            b = wait_fill(dve, ("ap", i))
                            dve.wait_ge(d_a, i + 1)
                            dve.tensor_tensor(PT[:, i, :, :], b[:, C:2 * C].rearrange("p (h n) -> p h n", n=DQ),
                                              K32["causal"][:, :].unsqueeze(1).to_broadcast([P, DH, DQ]), ALU.mult)\
                               .then_inc(d_pt, 1)
                            dve.wait_ge(d_pt, i + 1)
                            dve.sem_inc(empty(("ap", i)), 1)

                        def invert():
                            dve.wait_ge(d_mat, 16)
                            for r in range(1, DQ):
                                link(dve.tensor_tensor(TMP[:, 0:r, 0:r], INV[:, 0:r, 0:r],
                                                       MAT[:, r, 0:r].unsqueeze(1).to_broadcast([P, r, r]), ALU.mult))
                                dve.tensor_reduce(INV[:, 0:r, r], TMP[:, 0:r, 0:r], AX.X, ALU.add, negate=True)\
                                   .then_inc(d_inv, 1)
                                dve.wait_ge(d_inv, r)

                        def solve(g):
                            i, c = g // 4, g % 4
                            rows = slice(32 * c, 32 * c + 32)
                            dve.wait_ge(d_ks, g + 1)
                            dve.tensor_tensor(RP[rows, c, :], VB[rows, i, :], KS[rows, 0:C], ALU.subtract).then_inc(d_r, 1)

                        def update(g):
                            if g < 15:
                                dve.wait_ge(d_up, g + 1)
                                dve.tensor_tensor(S[:, :, :], SP[:, 0:C].rearrange("p (a n) -> p a n", a=NH),
                                                  K32["same32"][:, :].unsqueeze(1).to_broadcast([P, NH, P]), ALU.mult)\
                                   .then_inc(d_s, 1)

                        def finish():
                            dve.wait_ge(d_os, NT)
                            stats, mv, ve = owork
                            for i in range(NT):
                                last = dve.bn_stats(stats[:, i, :], O[:, i, :])
                            link(last)
                            for i in range(NT):
                                last = dve.bn_aggr(mv[:, i, :], stats[:, i, :])
                            link(last)
                            dve.tensor_scalar(ve[:, :, 0], mv[:, :, 1], EPS, None, ALU.add).then_inc(d_ov, 1)
                            dve.wait_ge(d_or, 1)
                            for i in range(NT):
                                last = dve.tensor_scalar(O[:, i, :], O[:, i, :], mv[:, i, 0:1], ve[:, i, 1:2],
                                                         ALU.subtract, ALU.mult)
                            link(last)
                            link(dve.tensor_tensor(O[:, :, :], O[:, :, :], LNB[:, 0, :].unsqueeze(1).to_broadcast([P, NT, C]), ALU.mult))
                            link(dve.tensor_tensor(O[:, :, :], O[:, :, :], LNB[:, 1, :].unsqueeze(1).to_broadcast([P, NT, C]), ALU.add))
                            dve.tensor_tensor(X3[:, :, :], O[:, :, :], X2L[:, :, :], ALU.add).then_inc(d_x2, 1)

                        stages = dict(norm=norm, project=project, pairs=pairs, invert=invert, solve=solve, update=update, finish=finish)
                        for step in ORDER_B:
                            if isinstance(step, int):
                                if ffn:
                                    ffn.dve_expert(dve, link, step)
                            elif step[0] == "ffn_in":
                                if ffn:
                                    ffn.dve_in(dve, link)
                            elif step[0] == "ffn_out":
                                if ffn:
                                    ffn.dve_out(dve)
                            elif delta and step[0] in stages:
                                stages[step[0]](*step[1:])

                    @block.gpsimd
                    def _(pool):
                        def norm():
                            root(pool, work, d_var, d_rstd)

                        def project(i):
                            pool.wait_ge(d_ss, i + 1)
                            pool.tensor_tensor(SS[:, i, 1, :], SS[:, i, 0, :], K32["nhalf"][:, 0:DH], ALU.pow).then_inc(d_rn, 1)

                        def pairs(i):
                            pool.wait_ge(d_turn, 3 * i + 2)
                            if i >= 1:
                                pool.wait_ge(filled, TURN["ap", i - 1] + 1)
                            toks = slice(i * P, i * P + P)
                            for dst, src in ((KX, KHT), (QX, QT)):
                                for a in range(NH):
                                    last = pool.tensor_tensor(
                                        dst[:, a, :, :], src[:, a, toks].unsqueeze(1).to_broadcast([P, 4, P]),
                                        K32["heads4"][:, :].unsqueeze(2).to_broadcast([P, 4, P]), ALU.mult)
                            last.then_inc(d_exp, 1)

                        def finish():
                            pool.wait_ge(d_ov, 1)
                            ve = owork[2]
                            pool.tensor_tensor(ve[:, :, 1], ve[:, :, 0], K32["nhalf"][:, 0:NT], ALU.pow).then_inc(d_or, 1)

                        stages = dict(norm=norm, project=project, pairs=pairs, finish=finish)
                        for step in ORDER_B:
                            if isinstance(step, int):
                                continue
                            if step[0] == "ffn_in":
                                if ffn:
                                    ffn.pool_in(pool)
                            elif delta and step[0] in stages:
                                stages[step[0]](*step[1:])
                        if delta:
                            pool.wait_ge(d_x2, 1)
                        if ffn_on:
                            pool.wait_ge(f_res, 2)
                            pool.tensor_copy(X2L[:, :, :], X2[:, :, :])
            end_block()

        rwkv_ffn(0)
        delta_ffn(delta=False)
        rwkv_ffn(1)
        delta_ffn()
        with nc.Fori(2, B) as i:
            rwkv_ffn(i, ffn_row=i - 2)
            delta_ffn()
        rwkv_ffn(None, rwkv=False, ffn_row=B - 2)
        delta_ffn(ffn_on=False)
        rwkv_ffn(None, rwkv=False, ffn_row=B - 1)


def constants():
    import numpy as np
    p = np.arange(P)
    chunk, q = p // RQ, p % RQ
    same = chunk[:, None] == chunk[None, :]
    eye = np.eye(P)
    mats = {
        "ident": eye,
        "before": -(same & (p[:, None] < p[None, :])).astype(np.float32),
        "after": -(same & (p[:, None] > p[None, :])).astype(np.float32),
        "earlier": q[:, None] < np.arange(RQ)[None, :],
        "chunks": -(chunk[:, None] == np.arange(2)[None, :]).astype(np.float32),
        "heads8": p[:, None] // RN == np.arange(8)[None, :],
        "same16": p[:, None] // RN == p[None, :] // RN,
        "same32": p[:, None] // DN == p[None, :] // DN,
        "heads4": p[:, None] // DN == np.arange(4)[None, :],
        "causal": np.arange(DQ)[None, :] >= (p % DQ)[:, None],
        "group_low": np.tile((np.arange(4)[None, :] < np.arange(4)[:, None]).reshape(1, -1), (P, 1)),
        "expert_low": np.tile((np.arange(E)[None, :] < np.arange(E)[:, None]).reshape(1, -1), (P, 1)),
        "nhalf": np.full((P, 32), -0.5),
        "lane_eye": np.tile(np.eye(DQ).reshape(1, -1), (P, 1)),
    }
    c32 = np.concatenate([np.asarray(mats[k], np.float32) for k in CONST32], 1)
    forbid = np.where(np.arange(RQ)[None, :] <= q[:, None], -BIG, 0.0)
    pick = [(p[:, None] % E == e) & (p[:, None] < 3 * E) & np.ones((1, P), bool) for e in range(E)]
    b16 = mybir.dt.np(mybir.dt.bfloat16)
    c16 = np.concatenate([eye, np.tile(forbid, (1, 8)), np.concatenate(pick, 1)], 1).astype(b16)
    return np.ascontiguousarray(c32), np.ascontiguousarray(c16)


def kernel(**inputs):
    import numpy as np
    import concourse.bacc as bacc
    from concourse.bass_utils import run_bass_kernel_spmd as run

    i = {k[3:]: np.asarray(v) for k, v in inputs.items()}

    def halves(v):
        return v.reshape(NH, P).T

    def experts(routed, shared):
        return np.concatenate([shared, routed.reshape(E * EH, C)], 0).T

    down = np.concatenate([i["ffn_sh_down_w"].T.reshape(NS, EH, C), i["ffn_down_w"].transpose(0, 2, 1)], 0)
    c32, c16 = constants()
    arrays = {
        "x": i["attn_a_x"],
        "maa": np.concatenate([halves(i["attn_a_time_maa_" + f]) for f in "xwkvr"], 1),
        "maa_w1": i["attn_a_maa_w1"], "maa_w2": i["attn_a_maa_w2"],
        "decay_w1": i["attn_a_decay_w1"], "decay_w2": i["attn_a_decay_w2"],
        "time_decay": i["attn_a_time_decay"].reshape(C),
        "u_col": halves(i["attn_a_time_faaaa"].reshape(C)) ,
        "w_rkvo": np.stack([i["attn_a_W" + f] for f in "rkvo"]),
        "ln_a": np.concatenate([halves(i["attn_a_ln_g"]), halves(i["attn_a_ln_b"])], 1),
        "w_delta_kv": np.concatenate([i["attn_b_Wk"], i["attn_b_Wv"]], 1),
        "w_delta_qb": np.concatenate([i["attn_b_Wq"], i["attn_b_Wb"]], 1),
        "ln_b": np.stack([i["attn_b_ln_w"], i["attn_b_ln_b"]]),
        "router": i["ffn_router_weight"].T, "e_bias": i["ffn_e_bias"],
        "gate": experts(i["ffn_gate_w"], i["ffn_sh_gate_w"]),
        "up": experts(i["ffn_up_w"], i["ffn_sh_up_w"]),
        "down": down, "c32": c32, "c16": c16,
    }
    nc = bacc.Bacc("TRN2", target_bir_lowering=False, num_devices=1)
    args, feeds = [], {}
    for name, a in arrays.items():
        a = np.ascontiguousarray(a)
        feeds[f"in_{name}"] = a
        args.append(nc.dram_tensor(f"in_{name}", a.shape, mybir.dt.from_np(a.dtype), kind="ExternalInput").ap())
    out = nc.dram_tensor("out", (B, T, C), mybir.dt.float32, kind="ExternalOutput").ap()
    hybrid_layers(nc, *args, out)
    r = run(nc, [feeds], core_ids=[0])
    return r.results[0]["out"]
```

```python
import concourse.bass as bass
from concourse import mybir
from contextlib import ExitStack

B, T, C = 16, 512, 256
P = 128
NT = T // P
NH = C // P
E, EH = 16, 128
NS = 2
NE = NS + E
RH, RN, RQ = 16, 16, 64
DH, DN, DQ = 8, 32, 32
EPS = 1e-5
BIG = 1e9

CONST32 = {"ident": 128, "before": 128, "after": 128, "earlier": RQ, "chunks": 2, "heads8": 8,
           "same16": 128, "same32": 128, "heads4": 4, "causal": DQ, "group_low": 16,
           "expert_low": 256, "nhalf": 32, "lane_eye": DQ * DQ}
CONST16 = {"identb": 128, "forbid": 512, "pick": E * P}



def experts_in_order():
    for e in range(NE):
        yield from (("g", e, 0), ("g", e, 1), ("u", e, 0), ("u", e, 1))
        if e > 0:
            yield from (("d", e - 1, 0), ("d", e - 1, 1))
    yield from (("d", NE - 1, 0), ("d", NE - 1, 1))


def between(items, n):
    return [next(items) for _ in range(n)]


def order_a():
    items = experts_in_order()
    order = [("ffn_turn",), ("mix_in",), ("route",)] + between(items, 2)
    order += [("rank_groups",), ("mix_first",)] + between(items, 1)
    order += [("mix", 0), ("rank_experts",)] + between(items, 3)
    order += [("use", 0), ("mix", 1), ("weigh",)] + between(items, 4)
    order += [("use", 1), ("decay_rates",), ("parts",), ("mix", 2)] + between(items, 4)
    order += [("use", 2), ("decays",), ("mix", 3)] + between(items, 4)
    order += [("use", 3)] + between(items, 2) + [("prep",)] + between(items, 6)
    for i in range(NT):
        order += [("args", i)] + between(items, 2) + [("scores", i)] + between(items, 4)
        if i > 0:
            order += [("turn_y", i - 1)] + between(items, 2) + [("project_y", i - 1)]
        order += [("intra", i)] + between(items, 4 if i else 6) + [("inter", i)] + between(items, 6)
        if i == 1:
            order += [("norm_x2",)]
    order += [("turn_y", NT - 1)] + between(items, 4) + [("project_y", NT - 1)]
    return order + list(items) + [("ffn_out",)]


def order_b():
    items = experts_in_order()
    order = [("project_in",), ("ffn_turn",), ("project", 0), ("route",), ("project", 1)] + between(items, 2)
    order += [("turn", 0), ("rank_groups",)] + between(items, 2) + [("project", 2), ("pairs", 0)] + between(items, 2)
    order += [("turn", 1), ("project", 3)] + between(items, 2) + [("pairs", 1), ("turn", 2), ("rank_experts",)]
    order += between(items, 1) + [("pairs", 2), ("turn", 3)] + between(items, 4) + [("pairs", 3), ("weigh",), ("parts",)]
    order += between(items, 3)
    for r in range(1, DQ):
        order += [("invert", r)]
        order += between(items, 1 if r < 12 else 2)
    order += between(items, 10) + [("norm_x",)]
    for g in range(T // DQ):
        order += [("key_state", g)] + between(items, 1) + [("solve", g), ("update", g)] + between(items, g % 3 == 1)
        if g >= 4:
            order += [("finish", g // 4 - 1, g % 4)]
    return order + [("finish", NT - 1, part) for part in range(4)] + list(items) + [("ffn_out",)]


ORDER_A, ORDER_B = order_a(), order_b()


def follow(order, *stages):
    for step in order:
        for named in stages:
            if step[0] in named:
                named[step[0]](*step[1:])


def hybrid_layers(nc, x, maa, maa_w1, maa_w2, decay_w1, decay_w2, time_decay, u_col, w_rkvo, ln_a,
                  w_delta_kv, w_delta_qb, ln_b, router, e_bias, gate, up, down, c32, c16, out):
    f32, bf16 = mybir.dt.float32, mybir.dt.bfloat16
    ALU, ACT, AX = mybir.AluOpType, mybir.ActivationFunctionType, mybir.AxisListType
    x_rows = x.rearrange("b (t p) c -> b p t c", p=P)
    out_rows = out.rearrange("b (t p) c -> b p t c", p=P)

    ctx = ExitStack()
    with ctx:
        copies = [0]

        def sb(name, shape, dt=f32, stack=ctx):
            if stack is not ctx:
                name = f"{name}_{copies[0]}"
            return stack.enter_context(nc.sbuf_tensor(name, shape, dt))

        WG, WU = sb("WG", [P, NH, NE * EH]), sb("WU", [P, NH, NE * EH])
        WD = sb("WD", [EH, NE, C])
        WRT = sb("WRT", [P, NH, E])
        EB = sb("EB", [P, E])
        MAA = sb("MAA", [P, 5, NH])
        W1 = sb("W1", [P, NH, P])
        W2 = sb("W2", [P, 4, C])
        DW1 = sb("DW1", [P, NH, 64])
        DWM = sb("DWM", [P, RH])
        UC = sb("UC", [P, NH])
        UB = sb("UB", [P, NH, P])
        WR = sb("WR", [P, 4, NH, C])
        LNA = sb("LNA", [P, 2, NH])
        WKV, WQB = sb("WKV", [P, NH, 2 * C]), sb("WQB", [P, NH, C + DH])
        LNB = sb("LNB", [P, 2, C])
        K32 = {k: sb("c_" + k, [P, n]) for k, n in CONST32.items() if k != "lane_eye"}
        K16 = {k: sb("c_" + k, [P, n], bf16) for k, n in CONST16.items()}
        XR, X1, X2, X3 = (sb(n, [P, NT, C]) for n in ("XR", "X1", "X2", "X3"))
        NR, NF, ND = (sb(n, [P, NT, C]) for n in ("NR", "NF", "ND"))
        stats, mv, ve = sb("stats", [P, NT, 6]), sb("mv", [P, NT, 2]), sb("ve", [P, NT, 2])
        KWP = sb("KWP", [P, 2, C])
        RP = sb("RP", [P, 4, C])
        VP = sb("VP", [P, 4, C])
        INV = sb("INV", [P, DQ, DQ])
        C3 = sb("C3", [P, NT, P], bf16)
        MAT = sb("MAT", [P, DQ, DQ])
        DW2, TD = (MAT[0:64, 8 * k:8 * k + 8, :].rearrange("p a b -> p (a b)") for k in range(2))
        a_dram = nc.dram_tensor("a_scratch", (P, DQ, DQ), f32).ap()
        t_dram = nc.dram_tensor("t_scratch", (P, DQ, DQ), f32).ap()
        ident, identb = K32["ident"], K16["identb"]

        banks = [ctx.enter_context(nc.psum_tensor(f"bank{i}", [P, 512], f32)) for i in range(8)]
        GB, UBK, CBK, YA, YB = banks[:5]
        RING = banks[5:]

        sems = {}

        def sem(name):
            sems[name] = ctx.enter_context(nc.semaphore(name))
            return sems[name]

        loaded = sem("loaded")
        n_var, n_rstd = sem("norm_var"), sem("norm_rstd")
        d_chain, p_chain, a_chain = sem("dve_chain"), sem("pool_chain"), sem("act_chain")
        f_tr, f_xt = sem("ffn_transposed"), sem("ffn_xt")
        f_lg, f_th, f_lt, f_c3, f_ct, f_cs = (sem(n) for n in (
            "ffn_logits", "ffn_logit_tanh", "ffn_logit_turned", "ffn_parts", "ffn_parts_turned", "ffn_parts_ready"))
        f_g, f_u, f_c, f_tanh, f_gd, f_h, f_dn = (sem(n) for n in (
            "ffn_gate", "ffn_up", "ffn_spread", "ffn_tanh", "ffn_gate_read", "ffn_hidden", "ffn_down"))
        f_res, f_out = sem("ffn_result"), sem("ffn_stored")
        filled = sem("ring_filled")
        emptied = [sem(f"ring{i}_emptied") for i in range(3)]
        x_in = sem("x_loaded")
        r_xt, r_xx = sem("r_xt"), sem("r_xx")
        f_eq = sem("ffn_equals")
        r_mixin, r_m, r_half, r_mixed, r_proj = (sem(n) for n in ("r_mix_in", "r_tanh", "r_half_mixed", "r_mixed", "r_projected"))
        r_dt, r_we, r_dec, r_ws = (sem(n) for n in ("r_decay_tanh", "r_rate", "r_decays", "r_chunk_decay"))
        r_k, r_v, r_r, r_kt, r_prod, r_rx = (sem(n) for n in ("r_k", "r_v", "r_rT", "r_kT", "r_product", "r_spread"))
        r_wm, r_e, r_p, r_kw, r_s, r_kv = (sem(n) for n in ("r_rate_masked", "r_weights", "r_scores", "r_kw", "r_state", "r_kv"))
        r_yn, r_yt, r_used = (sem(n) for n in ("r_y_norm", "r_yT", "r_scores_used"))
        r_yv, r_yr = sem("r_y_var"), sem("r_y_rstd")
        r_wx = sem("r_rate_by_channel")
        d_xt, d_vb, d_kb, d_vbb = (sem(n) for n in ("d_xt", "d_values_silu", "d_keys_by_beta", "d_values_by_beta"))
        d_ov, d_or, d_kc = sem("d_out_var"), sem("d_out_rstd"), sem("d_k_copied")
        d_zero, d_kx = sem("d_spread_cleared"), sem("d_keys_spread")
        d_qk, d_sq, d_ss, d_rn, d_kh, d_pt, d_turn, d_exp, d_a, d_st = (sem(n) for n in (
            "d_evacuated", "d_squares", "d_sums", "d_rnorm", "d_keys", "d_causal", "d_turned", "d_spread", "d_pairs", "d_pairs_stored_even"))
        d_stores = [d_st, sem("d_pairs_stored_odd")]
        d_mat, d_inv, d_tst, d_tld = (sem(n) for n in ("d_problems", "d_inverse", "d_inverse_stored", "d_inverse_loaded"))
        d_ks, d_r, d_v, d_vs, d_up, d_s, d_o, d_os = (sem(n) for n in (
            "d_key_state", "d_rhs", "d_solved", "d_values", "d_updated", "d_state", "d_out", "d_out_read"))

        numbers = [s.num for s in sems.values()]
        assert numbers == list(range(numbers[0], numbers[0] + len(numbers)))
        every_sem = range(numbers[0], numbers[-1] + 1)

        def end_block():
            copies[0] += 1
            nc.sync.sem_clear(every_sem)
            nc.all_engine_barrier(sem_only=True)

        def linker(eng, chain):
            count = [0]

            def link(ins):
                count[0] += 1
                ins.then_inc(chain, 1)
                eng.wait_ge(chain, count[0])
            return link

        with nc.Block() as block:
            @block.sync
            def _(sp):
                n = 0
                for k, (dst, src) in enumerate([
                        (WG[:, :, :], gate.rearrange("(a p) n -> p a n", p=P)),
                        (WU[:, :, :], up.rearrange("(a p) n -> p a n", p=P)),
                        (WD[:, :, :], down.rearrange("e p n -> p e n")),
                        (WRT[:, :, :], router.rearrange("(a p) n -> p a n", p=P)),
                        (EB[:, :], e_bias.unsqueeze(0).to_broadcast([P, E])),
                        (MAA[:, :, :], maa.rearrange("p (f a) -> p f a", a=NH)),
                        (W1[:, :, :], maa_w1.rearrange("(a p) n -> p a n", p=P)),
                        (DW1[:, :, :], decay_w1.rearrange("(a p) n -> p a n", p=P)),
                        (DW2[:, :], decay_w2),
                        (TD[:, :], time_decay.unsqueeze(0).to_broadcast([64, C])),
                        (UC[:, :], u_col),
                        (WR[:, :, :, :], w_rkvo.rearrange("f (a p) n -> p f a n", p=P)),
                        (LNA[:, :, :], ln_a.rearrange("p (f a) -> p f a", a=NH)),
                        (WKV[:, :, :], w_delta_kv.rearrange("(a p) n -> p a n", p=P)),
                        (WQB[:, :, :], w_delta_qb.rearrange("(a p) n -> p a n", p=P)),
                        (LNB[:, :, :], ln_b.unsqueeze(0).to_broadcast([P, 2, C]))]):
                    sp.dma_start(dst, src).then_inc(loaded, 16)
                    n += 16
                at = 0
                for k, cols in CONST32.items():
                    dst = INV[:, :, :].rearrange("p a b -> p (a b)") if k == "lane_eye" else K32[k][:, :]
                    sp.dma_start(dst, c32[:, at:at + cols]).then_inc(loaded, 16)
                    at += cols
                    n += 16
                at = 0
                for k, cols in CONST16.items():
                    sp.dma_start(K16[k][:, :], c16[:, at:at + cols]).then_inc(loaded, 16)
                    at += cols
                    n += 16
                sp.wait_ge(p_chain, 1)
                for f in range(4):
                    sp.dma_start(W2[32 * f:32 * f + 32, f, :], maa_w2[f]).then_inc(loaded, 16)
                    n += 16
                sp.wait_ge(loaded, n)
                sp.sem_inc(d_chain, 1)

            @block.gpsimd
            def _(pool):
                pool.memset(W2[:, :, :], 0.0).then_inc(p_chain, 1)
                pool.memset(KWP[:, :, :], 0.0)
                pool.memset(RP[:, :, :], 0.0)
                pool.memset(VP[:, :, :], 0.0)
                pool.memset(C3[:, :, :], 0.0)
                pool.memset(DWM[:, :], 0.0).then_inc(p_chain, 1)

            @block.vector
            def _(dve):
                dve.wait_ge(d_chain, 1)
                dve.wait_ge(p_chain, 2)
                dve.tensor_reduce(DWM[0:64, :], DW2[:, :].rearrange("p (h n) -> p h n", n=RN), AX.X, ALU.add)
                dve.tensor_reduce(DWM[64:65, :], TD[0:1, :].rearrange("p (h n) -> p h n", n=RN), AX.X, ALU.add)\
                   .then_inc(d_chain, 1)
                dve.wait_ge(d_chain, 2)
                dve.tensor_scalar(DWM[0:64, :], DWM[0:64, :], 1.0 / RN, None, ALU.mult)
                dve.tensor_scalar(DWM[64:65, :], DWM[64:65, :], 1.0 / RN, None, ALU.mult)
                for a in range(NH):
                    dve.tensor_scalar(UB[:, a, :], K32["same16"][:, :], UC[:, a:a + 1], None, ALU.mult)
        end_block()

        def turns(names):
            return {name: n for n, name in enumerate(names)}

        def normalise(dve, link, src, dst, tiles, turn):
            a, b = tiles
            for t in range(a, b):
                last = dve.bn_stats(stats[:, t, :], src[:, t, :])
            link(last)
            for t in range(a, b):
                last = dve.bn_aggr(mv[:, t, :], stats[:, t, :])
            link(last)
            dve.tensor_scalar(ve[:, a:b, 0], mv[:, a:b, 1], EPS, None, ALU.add).then_inc(n_var, 1)
            dve.wait_ge(n_rstd, turn)
            for t in range(a, b):
                last = dve.tensor_scalar(dst[:, t, :], src[:, t, :], mv[:, t, 0:1], ve[:, t, 1:2],
                                         ALU.subtract, ALU.mult)
            link(last)

        def root(pool, tiles, turn):
            a, b = tiles
            pool.wait_ge(n_var, turn)
            pool.tensor_tensor(ve[:, a:b, 1], ve[:, a:b, 0], K32["nhalf"][:, 0:b - a], ALU.pow).then_inc(n_rstd, 1)
            pool.wait_ge(n_rstd, turn)

        class Ffn:

            def __init__(self, tag, src, dst, stack, spare=None):
                def t(n, shape, dt=f32):
                    return sb(f"{tag}_{n}", shape, dt, stack)
                self.src, self.dst = src, dst
                self.xt = t("xt", [P, NH, T])
                self.th, self.s, self.h = t("th", [P, 512]), t("s", [P, 512]), t("h", [P, 2, 512])
                self.lt = t("lt", [E, T])
                self.sc, self.scb, self.gs, self.rk, self.wt, self.cw = (
                    t(n, [P, NT * E]) for n in ("sc", "scb", "gs", "rk", "wt", "cw"))
                self.pair, self.sum = t("pair", [P, NT * 4, 6]), t("sum", [P, 2 * NT])
                self.gt, self.eq = (v.rearrange("p (t a b) -> p t a b", a=E, b=E)
                                    for v in spare or (t("gt", [P, 1024])[:, :], t("eq", [P, 1024])[:, :]))
                self.c3t = t("c3t", [P, T], bf16)

            def pe_turn(self, pe):
                for a, bank in enumerate((YA, YB)):
                    for t in range(NT):
                        last = pe.transpose(bank[:, t * P:t * P + P], NF[:, t, a * P:a * P + P], ident[:, :])
                last.then_inc(f_tr, 1)

            def pe_route(self, pe):
                pe.wait_ge(f_xt, 2)
                for a in range(NH):
                    last = pe.matmul(GB[0:E, :], WRT[:, a, :], self.xt[:, a, :], start=a == 0, stop=a == NH - 1)
                last.then_inc(f_lg, 1)
                pe.wait_ge(f_th, 1)
                for t in range(NT):
                    last = pe.transpose(CBK[:, t * E:t * E + E], self.lt[:, t * P:t * P + P], ident[0:E, 0:E])
                last.then_inc(f_lt, 1)

            def pe_gate(self, pe, e, a):
                if a == 0 and e > 0:
                    pe.wait_ge(f_gd, e)
                last = pe.matmul(GB[:, :], WG[:, a, e * EH:e * EH + EH], self.xt[:, a, :], start=a == 0, stop=a == NH - 1)
                if a == NH - 1:
                    last.then_inc(f_g, 1)

            def pe_up(self, pe, e, a):
                if a == 0 and e > 0:
                    pe.wait_ge(f_h, e)
                last = pe.matmul(UBK[:, :], WU[:, a, e * EH:e * EH + EH], self.xt[:, a, :], start=a == 0, stop=a == NH - 1)
                if a < NH - 1:
                    return
                last.then_inc(f_u, 1)
                if e >= NS:
                    r = e - NS
                    if r == 0:
                        pe.wait_ge(f_cs, 1)
                    pe.matmul(CBK[:, :], K16["pick"][:, r * P:r * P + P], self.c3t[:, :], start=True, stop=True)\
                      .then_inc(f_c, 1)

            def pe_parts(self, pe):
                pe.wait_ge(f_c3, 1)
                cb = CBK[:, :].bitcast(bf16)
                for t in range(NT):
                    last = pe.transpose(cb[:, t * P:t * P + P], C3[:, t, :], identb[:, :])
                last.then_inc(f_ct, 1)

            def pe_down(self, pe, e, part):
                pe.wait_ge(f_h, e + 1)
                for t in (2 * part, 2 * part + 1):
                    last = pe.matmul((YA, YB)[t // 2][:, (t % 2) * C:(t % 2) * C + C],
                                     self.h[:, e % 2, t * P:t * P + P], WD[:, e, :],
                                     start=e == 0 and t % 2 == 0, stop=e == NE - 1 and t % 2 == 1)
                if part == 1:
                    last.then_inc(f_dn, 1)

            def on_tensor(self, pe):
                return {"ffn_turn": lambda: self.pe_turn(pe), "route": lambda: self.pe_route(pe),
                        "parts": lambda: self.pe_parts(pe), "g": lambda e, a: self.pe_gate(pe, e, a),
                        "u": lambda e, a: self.pe_up(pe, e, a), "d": lambda e, part: self.pe_down(pe, e, part)}

            def act_turn(self, act):
                act.wait_ge(f_tr, 1)
                for a, bank in enumerate((YA, YB)):
                    act.copy(self.xt[:, a, :], bank[:, :]).then_inc(f_xt, 1)

            def act_route(self, act):
                act.wait_ge(f_lg, 1)
                act.activation(self.lt[:, :], GB[0:E, :], ACT.Tanh, scale=0.5).then_inc(f_th, 1)

            def act_parts(self, act):
                act.wait_ge(f_ct, 1)
                act.copy(self.c3t[:, :], CBK[:, :].bitcast(bf16)[:, 0:T]).then_inc(f_cs, 1)

            def act_gate(self, act, e, a):
                if a < NH - 1:
                    return
                act.wait_ge(f_g, e + 1)
                if e > 0:
                    act.wait_ge(f_gd, e)
                act.activation(self.th[:, :], GB[:, :], ACT.Tanh, scale=0.5).then_inc(f_tanh, 1)

            def on_scalar(self, act):
                return {"ffn_turn": lambda: self.act_turn(act), "route": lambda: self.act_route(act),
                        "parts": lambda: self.act_parts(act), "g": lambda e, a: self.act_gate(act, e, a)}

            def dve_ranks(self, dve, link, values, n, low, ranks_out):
                v = values.rearrange("p (t e) -> p t e", e=n)
                mine = v.unsqueeze(3).to_broadcast([P, NT, n, n])
                other = v.unsqueeze(2).to_broadcast([P, NT, n, n])
                gt, eq = self.gt[:, :, 0:n, 0:n], self.eq[:, :, 0:n, 0:n]
                dve.tensor_tensor(gt, other, mine, ALU.is_gt)
                link(dve.tensor_tensor(eq, other, mine, ALU.is_equal))
                lo = low.rearrange("p (a b) -> p a b", b=n).unsqueeze(1).to_broadcast([P, NT, n, n])
                link(dve.tensor_tensor(eq, eq, lo, ALU.mult))
                link(dve.tensor_tensor(gt, gt, eq, ALU.add))
                link(dve.tensor_reduce(ranks_out.rearrange("p (t e) -> p t e", e=n), gt, AX.X, ALU.add))

            def dve_rank_groups(self, dve, link):
                dve.wait_ge(f_lt, 1)
                link(dve.tensor_scalar(self.sc[:, :], CBK[:, 0:NT * E], 0.5, 0.5, ALU.mult, ALU.add))
                sc4 = self.sc[:, :].rearrange("p (t e) -> p t e", e=E)
                link(dve.tensor_tensor(self.scb[:, :].rearrange("p (t e) -> p t e", e=E), sc4,
                                       EB[:, :].unsqueeze(1).to_broadcast([P, NT, E]), ALU.add))
                g4 = self.scb[:, :].rearrange("p (g e) -> p g e", e=4)
                dve.tensor_tensor(self.pair[:, :, 0:3], g4[:, :, 0:3], g4[:, :, 1:4], ALU.add)
                dve.tensor_tensor(self.pair[:, :, 3:5], g4[:, :, 0:2], g4[:, :, 2:4], ALU.add)
                link(dve.tensor_tensor(self.pair[:, :, 5:6], g4[:, :, 0:1], g4[:, :, 3:4], ALU.add))
                link(dve.tensor_reduce(self.gs[:, 0:16], self.pair[:, :, :], AX.X, ALU.max))
                self.dve_ranks(dve, link, self.gs[:, 0:16], 4, K32["group_low"][:, :], self.rk[:, 0:16])
                link(dve.tensor_scalar(self.gs[:, 16:32], self.rk[:, 0:16], 1.5, None, ALU.is_lt))
                link(dve.tensor_tensor(self.wt[:, :].rearrange("p (g e) -> p g e", e=4), g4,
                                       self.gs[:, 16:32].unsqueeze(2).to_broadcast([P, 16, 4]), ALU.mult))

            def dve_rank_experts(self, dve, link):
                self.dve_ranks(dve, link, self.wt[:, :], E, K32["expert_low"][:, :], self.rk[:, :])

            def dve_weigh(self, dve, link):
                link(dve.scalar_tensor_tensor(self.cw[:, :], self.rk[:, :], 3.5, self.sc[:, :], ALU.is_lt, ALU.mult))
                cw4 = self.cw[:, :].rearrange("p (t e) -> p t e", e=E)
                link(dve.tensor_reduce(self.sum[:, 0:NT], cw4, AX.X, ALU.add))
                link(dve.tensor_scalar(self.sum[:, 0:NT], self.sum[:, 0:NT], 1e-20, None, ALU.add))
                link(dve.reciprocal(self.sum[:, NT:], self.sum[:, 0:NT]))
                link(dve.tensor_tensor(cw4, cw4, self.sum[:, NT:].unsqueeze(2).to_broadcast([P, NT, E]), ALU.mult))
                link(dve.tensor_scalar(self.cw[:, :], self.cw[:, :], 2.5, None, ALU.mult))
                link(dve.tensor_copy(C3[:, :, 0:E], cw4))
                link(dve.tensor_tensor(cw4, cw4, C3[:, :, 0:E], ALU.subtract))
                link(dve.tensor_copy(C3[:, :, E:2 * E], cw4))
                link(dve.tensor_tensor(cw4, cw4, C3[:, :, E:2 * E], ALU.subtract))
                dve.tensor_copy(C3[:, :, 2 * E:3 * E], cw4).then_inc(f_c3, 1)

            def dve_gate(self, dve, e, a):
                if a < NH - 1:
                    return
                dve.wait_ge(f_tanh, e + 1)
                if e > 0:
                    dve.wait_ge(f_h, e)
                dve.scalar_tensor_tensor(self.s[:, :], self.th[:, :], 1.0, GB[:, :], ALU.add, ALU.mult)\
                   .then_inc(f_gd, 1)

            def dve_up(self, dve, link, e, a):
                if a < NH - 1:
                    return
                dve.wait_ge(f_gd, e + 1)
                dve.wait_ge(f_u, e + 1)
                if e >= 2:
                    dve.wait_ge(f_dn, e - 1)
                h = self.h[:, e % 2, :]
                if e < NS:
                    dve.scalar_tensor_tensor(h, UBK[:, :], 0.5, self.s[:, :], ALU.mult, ALU.mult).then_inc(f_h, 1)
                else:
                    link(dve.scalar_tensor_tensor(h, UBK[:, :], 0.5, self.s[:, :], ALU.mult, ALU.mult))
                    dve.wait_ge(f_c, e - NS + 1)
                    dve.tensor_tensor(h, h, CBK[:, :], ALU.mult).then_inc(f_h, 1)

            def dve_out(self, dve):
                dve.wait_ge(f_dn, NE)
                for n, bank in enumerate((YA, YB)):
                    dve.tensor_tensor(self.dst[:, 2 * n:2 * n + 2, :], self.src[:, 2 * n:2 * n + 2, :],
                                      bank[:, :].rearrange("p (t c) -> p t c", c=C), ALU.add).then_inc(f_res, 1)

            def on_vector(self, dve, link):
                return {"rank_groups": lambda: self.dve_rank_groups(dve, link),
                        "rank_experts": lambda: self.dve_rank_experts(dve, link), "weigh": lambda: self.dve_weigh(dve, link),
                        "g": lambda e, a: self.dve_gate(dve, e, a), "u": lambda e, a: self.dve_up(dve, link, e, a),
                        "ffn_out": lambda: self.dve_out(dve)}

        def rwkv_ffn(rwkv=True, ffn_on=True, norm_row=True, store_row=None):
            def x1_turn(i):
                return i + 1 + (norm_row and i >= 1)

            def x2_turn():
                return 2 if rwkv else 1

            with ExitStack() as stack:
                def t(n, shape, dt=f32):
                    return sb("a_" + n, shape, dt, stack)

                if rwkv:
                    ystats, ymv, yve = (t(n, [P, NT, k]) for n, k in (("yst", 6), ("ymv", 2), ("yve", 2)))
                    XT, XX = t("xt", [P, NH, T + 1]), t("xx", [P, NH, T])
                    TM = t("tm", [P, T])
                    XF = t("xf", [P, 2, NH, T])
                    DT = t("dt", [P, T])
                    WE = t("we", [P, NT * RH])
                    WX = NR[:, :, :].rearrange("p t c -> p (t c)")
                    EW = XF
                    KK, VV, RT, KT = t("k", [P, NT, C]), t("v", [P, NT, C]), t("rT", [P, NH, T]), t("kT", [P, NH, T])
                    RX = t("rx", [P, NH, 8, P])
                    WM = t("wm", [P, 2, 512])
                    DEC, WS = t("dec", [P, 2, NT * RH]), t("ws", [P, NH, NT, 2])
                    S = t("s", [P, 2, NH, P])
                    SM, Y, YN, YT, DV = t("sm", [P, NH, P]), t("y", [P, C]), t("yn", [P, C]), t("yT", [P, C]), t("dv", [P, C])
                PR = XX if rwkv else None
                ffn = None
                if ffn_on:
                    spare = [RX[:, a, :, :].rearrange("p h n -> p (h n)") for a in range(NH)] if rwkv else None
                    ffn = Ffn("fa", X3, X3, stack, spare)

                def fills(step):
                    n = step[1] if len(step) > 1 else None
                    return {"mix_in": ["x0", "x1"], "mix_first": ["m"], "mix": [("mix", n, 0), ("mix", n, 1)],
                            "use": {0: ["dt"], 1: ["k0", "k1"], 2: ["v0", "v1"], 3: ["r0", "r1"]}.get(n),
                            "decay_rates": ["w"], "decays": ["dec"], "prep": ["kT0", "kT1"],
                            "args": [("arg", n, 0), ("arg", n, 1)], "scores": [("score", n, 0), ("score", n, 1)],
                            "intra": [("diag", n), ("kv", n)], "inter": [("y", n)],
                            "turn_y": [("yT", n)], "project_y": [("o", n)]}.get(step[0], [])

                TURN = turns([name for step in ORDER_A for name in fills(step)])

                def bank(name):
                    return RING[TURN[name] % 3]

                def take(pe, name):
                    n = TURN[name]
                    if n >= 3:
                        pe.wait_ge(emptied[n % 3], n // 3)
                    return RING[n % 3]

                def wait_fill(eng, name):
                    eng.wait_ge(filled, TURN[name] + 1)
                    return bank(name)

                def empty(name):
                    return emptied[TURN[name] % 3]

                with nc.Block() as block:
                    @block.sync
                    def _(sp):
                        if store_row is not None:
                            sp.wait_ge(f_res, 2)
                            sp.dma_start(out_rows[store_row], X3[:, :, :]).then_inc(f_out, 16)
                            sp.wait_ge(f_out, 16)

                    @block.tensor
                    def _(pe):
                        def mix_in():
                            for a in range(NH):
                                b = take(pe, f"x{a}")
                                for i in range(NT):
                                    last = pe.transpose(b[:, i * P:i * P + P], NR[:, i, a * P:a * P + P], ident[:, :])
                                last.then_inc(filled, 1)

                        def mix_first():
                            b = take(pe, "m")
                            pe.wait_ge(r_mixin, 1)
                            for a in range(NH):
                                last = pe.matmul(b[:, :], W1[:, a, :], XF[:, 1, a, :], start=a == 0, stop=a == NH - 1)
                            last.then_inc(filled, 1)

                        def mix(f):
                            pe.wait_ge(r_m, 1)
                            for a in range(NH):
                                pe.matmul(take(pe, ("mix", f, a))[:, :], W2[:, f, a * P:a * P + P], TM[:, :],
                                          start=True, stop=True).then_inc(filled, 1)

                        def use(f):
                            pe.wait_ge(r_mixed, f + 1)
                            xf = XF[:, f % 2, :, :]
                            if f == 0:
                                b = take(pe, "dt")
                                for a in range(NH):
                                    last = pe.matmul(b[0:64, :], DW1[:, a, :], xf[:, a, :], start=a == 0, stop=a == NH - 1)
                                last.then_inc(filled, 1)
                            elif f < 3:
                                for n in range(2):
                                    b = take(pe, f"{'_kv'[f]}{n}")
                                    for j in range(2):
                                        i = 2 * n + j
                                        for a in range(NH):
                                            last = pe.matmul(b[:, j * C:j * C + C], xf[:, a, i * P:i * P + P],
                                                             WR[:, f, a, :], start=a == 0, stop=a == NH - 1)
                                    last.then_inc(filled, 1)
                            else:
                                for n in range(NH):
                                    b = take(pe, f"r{n}")
                                    for a in range(NH):
                                        last = pe.matmul(b[:, :], WR[:, 0, a, n * P:n * P + P], xf[:, a, :],
                                                         start=a == 0, stop=a == NH - 1)
                                    last.then_inc(filled, 1)

                        def decay_rates():
                            b = take(pe, "w")
                            pe.wait_ge(r_dt, 1)
                            for i in range(NT):
                                last = pe.matmul(b[:, i * RH:i * RH + RH], DT[:, i * P:i * P + P], DWM[:, :],
                                                 start=True, stop=True)
                            last.then_inc(filled, 1)

                        def decays():
                            b = take(pe, "dec")
                            pe.wait_ge(r_we, 1)
                            pe.matmul(b[:, 0:64], K32["before"][:, :], WE[:, :], start=True, stop=True)
                            pe.matmul(b[:, 64:128], K32["after"][:, :], WE[:, :], start=True, stop=True)
                            pe.wait_ge(r_wx, 1)
                            for i in range(NT):
                                for a in range(NH):
                                    rates = WX[:, i * C + a * P:i * C + a * P + P]
                                    at = 128 + a * 8 + 2 * i
                                    last = pe.matmul(b[:, at:at + 2], rates, K32["chunks"][:, :], start=True, stop=True)
                            last.then_inc(filled, 1)

                        def prep():
                            pe.wait_ge(r_k, 2)
                            for a in range(NH):
                                b = take(pe, f"kT{a}")
                                for i in range(NT):
                                    last = pe.transpose(b[:, i * P:i * P + P], KK[:, i, a * P:a * P + P], ident[:, :])
                                last.then_inc(filled, 1)

                        def args(i):
                            for n in range(2):
                                b = take(pe, ("arg", i, n))
                                pe.wait_ge(r_wm, 2 * i + n + 1)
                                pe.matmul(b[:, :], K32["after"][:, :], WM[:, n, :], start=True, stop=False)
                                pe.matmul(b[:, :], identb[:, :], K16["forbid"][:, :], start=False, stop=True)\
                                  .then_inc(filled, 1)

                        def scores(i):
                            pe.wait_ge(r_kt, 2)
                            pe.wait_ge(r_rx, 2 * i + 2)
                            for a in range(NH):
                                b = take(pe, ("score", i, a))
                                for c in range(2):
                                    at = i * P + c * RQ
                                    last = pe.matmul(b[c * RQ:c * RQ + RQ, :], KT[:, a, at:at + RQ],
                                                     RX[:, a, :, c * RQ:c * RQ + RQ], start=True, stop=True)
                                last.then_inc(filled, 1)

                        def carried(i, c):
                            b, at = bank(("y", i)), i * P + c * RQ
                            pe.wait_ge(r_s, 2 * i + c + 1)
                            for a in range(NH):
                                last = pe.matmul(b[c * RQ:c * RQ + RQ, C + a * P:C + a * P + P],
                                                 RT[:, a, at:at + RQ], S[:, c, a, :], start=True, stop=True)
                            return last

                        def intra(i):
                            b = take(pe, ("y", i))
                            pe.wait_ge(r_p, 2 * i + 2)
                            pe.wait_ge(r_v, 2)
                            for c in range(2):
                                rows = slice(c * RQ, c * RQ + RQ)
                                for h in range(RH):
                                    last = pe.matmul(b[rows, h * RN:h * RN + RN],
                                                     EW[rows, i % 2, h // 8, (h % 8) * RQ:(h % 8) * RQ + RQ],
                                                     VV[rows, i, h * RN:h * RN + RN], start=True, stop=True)
                            last.then_inc(r_used, 1)
                            carried(i, 0)
                            b = take(pe, ("diag", i))
                            pe.wait_ge(r_prod, 1)
                            for a in range(NH):
                                last = pe.matmul(b[:, a * P:a * P + P], PR[:, a, i * P:i * P + P], UB[:, a, :],
                                                 start=True, stop=True)
                            last.then_inc(filled, 1)
                            b = take(pe, ("kv", i))
                            pe.wait_ge(r_kw, 2 * i + 2)
                            for c in range(2):
                                for a in range(NH):
                                    last = pe.matmul(b[:, c * C + a * P:c * C + a * P + P],
                                                     KWP[:, c, a * P:a * P + P], VV[:, i, a * P:a * P + P],
                                                     start=True, stop=True)
                            last.then_inc(filled, 1)

                        def inter(i):
                            carried(i, 1).then_inc(filled, 1)

                        def turn_y(i):
                            b = take(pe, ("yT", i))
                            pe.wait_ge(r_yn, i + 1)
                            for a in range(NH):
                                last = pe.transpose(b[:, a * P:a * P + P], YN[:, a * P:a * P + P], ident[:, :])
                            last.then_inc(filled, 1)

                        def project_y(i):
                            b = take(pe, ("o", i))
                            pe.wait_ge(r_yt, 2 * i + 2)
                            for a in range(NH):
                                last = pe.matmul(b[:, 0:C], YT[:, a * P:a * P + P], WR[:, 3, a, :],
                                                 start=a == 0, stop=a == NH - 1)
                            last.then_inc(filled, 1)

                        stages = dict(mix_in=mix_in, mix_first=mix_first, mix=mix, use=use, decay_rates=decay_rates,
                                      decays=decays, prep=prep, args=args, scores=scores, intra=intra, inter=inter,
                                      turn_y=turn_y, project_y=project_y)
                        follow(ORDER_A, ffn.on_tensor(pe) if ffn else {}, stages if rwkv else {})
                    @block.scalar
                    def _(act):
                        def mix_in():
                            for a in range(NH):
                                b = wait_fill(act, f"x{a}")
                                act.copy(XT[:, a, 1:T + 1], b[:, :]).then_inc(r_xt, 1)
                                act.wait_ge(r_xt, a + 1)
                                act.sem_inc(empty(f"x{a}"), 1)

                        def mix_first():
                            b = wait_fill(act, "m")
                            act.activation(TM[:, :], b[:, :], ACT.Tanh).then_inc(r_m, 1)
                            act.wait_ge(r_m, 1)
                            act.sem_inc(empty("m"), 1)

                        def use(f):
                            if f == 0:
                                b = wait_fill(act, "dt")
                                act.activation(DT[0:64, :], b[0:64, :], ACT.Tanh).then_inc(r_dt, 1)
                                act.wait_ge(r_dt, 1)
                                act.sem_inc(empty("dt"), 1)
                                return
                            done = (None, r_k, r_v, r_r)[f]
                            for n in range(2):
                                b = wait_fill(act, f"{'_kvr'[f]}{n}")
                                if f < 3:
                                    dst = (None, KK, VV)[f][:, 2 * n:2 * n + 2, :]
                                    act.copy(dst, b[:, :].rearrange("p (t c) -> p t c", c=C)).then_inc(done, 1)
                                else:
                                    act.copy(RT[:, n, :], b[:, :]).then_inc(done, 1)
                                act.wait_ge(done, n + 1)
                                act.sem_inc(empty(f"{'_kvr'[f]}{n}"), 1)

                        def decay_rates():
                            b = wait_fill(act, "w")
                            act.activation(WE[:, :], b[:, 0:NT * RH], ACT.Exp).then_inc(r_we, 1)
                            act.wait_ge(r_we, 1)
                            act.sem_inc(empty("w"), 1)

                        def decays():
                            b = wait_fill(act, "dec")
                            act.activation(DEC[:, :, :], b[:, 0:128].rearrange("p (a n) -> p a n", a=2), ACT.Exp)\
                               .then_inc(r_dec, 1)
                            act.activation(WS[:, :, :, :].rearrange("p a t c -> p (a t c)"), b[:, 128:144], ACT.Exp)\
                               .then_inc(r_ws, 1)
                            act.wait_ge(r_ws, 1)
                            act.sem_inc(empty("dec"), 1)

                        def prep():
                            for a in range(NH):
                                b = wait_fill(act, f"kT{a}")
                                act.copy(KT[:, a, :], b[:, :]).then_inc(r_kt, 1)
                                act.wait_ge(r_kt, a + 1)
                                act.sem_inc(empty(f"kT{a}"), 1)

                        def args(i):
                            for n in range(2):
                                b = wait_fill(act, ("arg", i, n))
                                if i >= 2:
                                    act.wait_ge(r_used, i - 1)
                                act.activation(EW[:, i % 2, n, :], b[:, :], ACT.Exp).then_inc(r_e, 1)
                                act.wait_ge(r_e, 2 * i + n + 1)
                                act.sem_inc(empty(("arg", i, n)), 1)

                        def turn_y(i):
                            b = wait_fill(act, ("yT", i))
                            for a in range(NH):
                                act.activation(YT[:, a * P:a * P + P], b[:, a * P:a * P + P], ACT.Identity,
                                               bias=LNA[:, 1, a:a + 1], scale=LNA[:, 0, a:a + 1]).then_inc(r_yt, 1)
                            act.wait_ge(r_yt, 2 * i + 2)
                            act.sem_inc(empty(("yT", i)), 1)

                        stages = dict(mix_in=mix_in, mix_first=mix_first, use=use, decay_rates=decay_rates, decays=decays,
                                      prep=prep, args=args, turn_y=turn_y)
                        follow(ORDER_A, ffn.on_scalar(act) if ffn else {}, stages if rwkv else {})
                    @block.vector
                    def _(dve):
                        link = linker(dve, d_chain)

                        def mix_in():
                            dve.memset(XT[:, :, 0:1], 0.0)
                            dve.memset(DT[64:128, :], 1.0)
                            link(dve.memset(S[:, 0, :, :], 0.0))
                            dve.sem_inc(r_s, 1)
                            dve.wait_ge(r_xt, 2)
                            dve.tensor_tensor(XX[:, :, :], XT[:, :, 0:T], XT[:, :, 1:T + 1], ALU.subtract).then_inc(r_xx, 1)
                            dve.wait_ge(r_xx, 1)
                            for a in range(NH):
                                last = dve.scalar_tensor_tensor(XF[:, 1, a, :], XX[:, a, :], MAA[:, 0, a:a + 1],
                                                                XT[:, a, 1:T + 1], ALU.mult, ALU.add)
                            last.then_inc(r_mixin, 1)

                        def mix(f):
                            if f >= 1:
                                dve.wait_ge(filled, TURN[{1: "m", 2: "dt", 3: "k1"}[f]] + 1)
                            for a in range(NH):
                                b = wait_fill(dve, ("mix", f, a))
                                dve.scalar_tensor_tensor(XF[:, f % 2, a, :], b[:, :], MAA[:, f + 1, a:a + 1],
                                                         XX[:, a, :], ALU.add, ALU.mult).then_inc(r_half, 1)
                                dve.wait_ge(r_half, 2 * f + a + 1)
                                dve.sem_inc(empty(("mix", f, a)), 1)
                            xf = XF[:, f % 2, :, :]
                            dve.tensor_tensor(xf, xf, XT[:, :, 1:T + 1], ALU.add).then_inc(r_mixed, 1)

                        def decay_rates():
                            dve.wait_ge(r_we, 1)
                            dve.tensor_copy(WX[:, :].rearrange("p (h n) -> p h n", n=RN),
                                            WE[:, :].unsqueeze(2).to_broadcast([P, NT * RH, RN])).then_inc(r_wx, 1)

                        def scores(i):
                            for n in range(2):
                                b = wait_fill(dve, ("score", i, n))
                                dve.wait_ge(r_e, 2 * i + n + 1)
                                ew = EW[:, i % 2, n, :]
                                dve.tensor_tensor(ew, ew, b[:, :], ALU.mult).then_inc(r_p, 1)
                                dve.wait_ge(r_p, 2 * i + n + 1)
                                dve.sem_inc(empty(("score", i, n)), 1)

                        def intra(i):
                            b = wait_fill(dve, ("diag", i))
                            link(dve.tensor_tensor(DV[:, :], b[:, 0:C], VV[:, i, :], ALU.mult))
                            dve.sem_inc(empty(("diag", i)), 1)
                            b = wait_fill(dve, ("kv", i))
                            dve.wait_ge(r_ws, 1)
                            for c in range(2):
                                n = 2 * i + c
                                link(dve.tensor_tensor(SM[:, :, :], b[:, c * C:c * C + C].rearrange("p (a n) -> p a n", a=NH),
                                                       K32["same16"][:, :].unsqueeze(1).to_broadcast([P, NH, P]), ALU.mult))
                                if c == 1:
                                    dve.sem_inc(empty(("kv", i)), 1)
                                if n == 2 * NT - 1:
                                    break
                                if c == 0 and i >= 1:
                                    dve.wait_ge(filled, TURN["y", i - 1] + 1)
                                for a in range(NH):
                                    last = dve.scalar_tensor_tensor(S[:, (c + 1) % 2, a, :], S[:, c, a, :],
                                                                    WS[:, a, i, c:c + 1], SM[:, a, :], ALU.mult, ALU.add)
                                last.then_inc(r_s, 1)
                                dve.wait_ge(r_s, n + 2)

                        def inter(i):
                            b = wait_fill(dve, ("y", i))
                            dve.wait_ge(r_dec, 1)
                            dec = DEC[:, 0, i * RH:i * RH + RH].unsqueeze(2).to_broadcast([P, RH, RN])
                            link(dve.tensor_tensor(Y[:, :].rearrange("p (h n) -> p h n", n=RN),
                                                   b[:, C:2 * C].rearrange("p (h n) -> p h n", n=RN), dec, ALU.mult))
                            link(dve.tensor_tensor(Y[:, :], Y[:, :], b[:, 0:C], ALU.add))
                            dve.sem_inc(empty(("y", i)), 1)
                            link(dve.tensor_tensor(Y[:, :], Y[:, :], DV[:, :], ALU.add))
                            link(dve.bn_stats(ystats[:, i, :], Y[:, :]))
                            link(dve.bn_aggr(ymv[:, i, :], ystats[:, i, :]))
                            dve.tensor_scalar(yve[:, i, 0:1], ymv[:, i, 1:2], EPS, None, ALU.add).then_inc(r_yv, 1)

                        def turn_y(i):
                            dve.wait_ge(r_yr, i + 1)
                            if i >= 1:
                                dve.wait_ge(filled, TURN["yT", i - 1] + 1)
                            dve.tensor_scalar(YN[:, :], Y[:, :], ymv[:, i, 0:1], yve[:, i, 1:2], ALU.subtract, ALU.mult)\
                               .then_inc(r_yn, 1)
                            dve.wait_ge(r_yn, i + 1)

                        def project_y(i):
                            b = wait_fill(dve, ("o", i))
                            link(dve.tensor_tensor(X1[:, i, :], XR[:, i, :], b[:, 0:C], ALU.add))
                            dve.sem_inc(empty(("o", i)), 1)
                            normalise(dve, link, X1, NF, (i, i + 1), x1_turn(i))

                        stages = dict(mix_in=mix_in, mix=mix, decay_rates=decay_rates, scores=scores,
                                      intra=intra, inter=inter, turn_y=turn_y, project_y=project_y)
                        always = {"norm_x2": lambda: normalise(dve, link, X2, ND, (0, NT), x2_turn())} if norm_row else {}
                        follow(ORDER_A, ffn.on_vector(dve, link) if ffn else {}, stages if rwkv else {}, always)
                    @block.gpsimd
                    def _(pool):
                        def rates(i):
                            for n in range(2):
                                if i >= 1:
                                    pool.wait_ge(filled, TURN["arg", i - 1, n] + 1)
                                pool.tensor_tensor(
                                    WM[:, n, :].rearrange("p (h q) -> p h q", q=RQ),
                                    WE[:, i * RH + 8 * n:i * RH + 8 * n + 8].unsqueeze(2).to_broadcast([P, 8, RQ]),
                                    K32["earlier"][:, :].unsqueeze(1).to_broadcast([P, 8, RQ]), ALU.mult).then_inc(r_wm, 1)

                        def spread(i):
                            if i >= 1:
                                pool.wait_ge(filled, TURN["score", i - 1, 1] + 1)
                            elif ffn:
                                pool.wait_ge(f_c3, 1)
                            for a in range(NH):
                                pool.tensor_tensor(
                                    RX[:, a, :, :], RT[:, a, i * P:i * P + P].unsqueeze(1).to_broadcast([P, 8, P]),
                                    K32["heads8"][:, :].unsqueeze(2).to_broadcast([P, 8, P]), ALU.mult).then_inc(r_rx, 1)

                        def decayed(i):
                            if i >= 1:
                                pool.wait_ge(filled, TURN["kv", i - 1] + 1)
                                pool.wait_ge(r_yr, i)
                            pool.wait_ge(r_wm, 2 * i + 2)
                            pool.wait_ge(r_rx, 2 * i + 2)
                            for c in range(2):
                                rows = slice(c * RQ, c * RQ + RQ)
                                pool.tensor_tensor(
                                    KWP[rows, c, :].rearrange("p (h n) -> p h n", n=RN),
                                    KK[rows, i, :].rearrange("p (h n) -> p h n", n=RN),
                                    DEC[rows, 1, i * RH:i * RH + RH].unsqueeze(2).to_broadcast([RQ, RH, RN]), ALU.mult)\
                                    .then_inc(r_kw, 1)
                                pool.wait_ge(r_kw, 2 * i + c + 1)

                        def decays():
                            pool.wait_ge(r_we, 1)
                            rates(0)

                        def prep():
                            pool.wait_ge(r_r, 2)
                            spread(0)
                            pool.wait_ge(r_dec, 1)
                            pool.wait_ge(r_k, 2)
                            decayed(0)
                            pool.wait_ge(r_kt, 2)
                            pool.wait_ge(r_mixed, 4)
                            pool.tensor_tensor(PR[:, :, :], RT[:, :, :], KT[:, :, :], ALU.mult).then_inc(r_prod, 1)
                            pool.wait_ge(r_prod, 1)

                        def scores(i):
                            if i < NT - 1:
                                rates(i + 1)
                                spread(i + 1)

                        def inter(i):
                            pool.wait_ge(r_yv, i + 1)
                            pool.tensor_tensor(yve[:, i, 1:2], yve[:, i, 0:1], K32["nhalf"][:, 0:1], ALU.pow)\
                                .then_inc(r_yr, 1)

                        def turn_y(i):
                            if i < NT - 1:
                                decayed(i + 1)

                        def project_y(i):
                            root(pool, (i, i + 1), x1_turn(i))

                        stages = dict(decays=decays, prep=prep, scores=scores, inter=inter, turn_y=turn_y,
                                      project_y=project_y)
                        always = {"norm_x2": lambda: root(pool, (0, NT), x2_turn())} if norm_row else {}
                        follow(ORDER_A, stages if rwkv else {}, always)
            end_block()

        def delta_ffn(delta=True, ffn_on=True, load_row=None, store_row=None):
            loads = load_row is not None

            def x3_turn(i):
                return i + 1 + loads

            with ExitStack() as stack:
                def t(n, shape, dt=f32):
                    return sb("b_" + n, shape, dt, stack)

                if delta:
                    XT = t("xt", [P, NH, T])
                    ostats, omv, ove = (t(n, [P, NT, k]) for n, k in (("ost", 6), ("omv", 2), ("ove", 2)))
                    Q, KH, KB, VB = t("q", [P, NT, C]), t("kh", [P, NT, C]), t("kb", [P, 2, C]), t("vb", [P, NT, C])
                    SQ, SG, SS = t("sq", [P, C]), t("sg", [P, 2, C + DH]), t("ss", [P, NT, 2, DH])
                    QT, KHT, KBT = t("qT", [P, NH, T]), t("khT", [P, NH, T]), t("kbT", [P, NH, T])
                    QX, KX = t("qx", [P, NH, 4, P]), t("kx", [P, NH, 4, P])
                    TMP = QX[:, :, :, :].rearrange("p a h n -> p (a h n)").rearrange("p (c j) -> p c j", j=DQ)
                    AS = t("as", [P, 2, C])
                    PT = t("pT", [P, NT, DH, DQ])
                    TI = t("ti", [P, NT, DH, DQ])
                    S = t("s", [P, NH, P])
                    O = ND

                spare = [v.rearrange("p a b -> p (a b)") for v in
                         (MAT[:, :, :], TI[:, :, :, :].rearrange("p t h j -> p (t h) j"))] if delta else None
                ffn = Ffn("fb", X1, X2, stack, spare) if ffn_on else None

                def fills(step):
                    n = step[1] if len(step) > 1 else None
                    return {"project_in": ["x0", "x1"], "project": [("kv", n), ("qb", n)],
                            "turn": [("t1", n), ("t2", n)], "pairs": [("ap", n)]}.get(step[0], [])

                TURN = turns([name for step in ORDER_B for name in fills(step)])
                KS, OB, SP = RING

                def take(pe, name):
                    n = TURN[name]
                    if n >= 3:
                        pe.wait_ge(emptied[n % 3], n // 3)
                    return RING[n % 3]

                def wait_fill(eng, name):
                    eng.wait_ge(filled, TURN[name] + 1)
                    return RING[TURN[name] % 3]

                def empty(name):
                    return emptied[TURN[name] % 3]

                def uses(k):
                    return len([n for n in TURN.values() if n % 3 == k])

                with nc.Block() as block:
                    @block.sync
                    def _(sp):
                        if loads:
                            sp.dma_start(XR[:, :, :], x_rows[load_row]).then_inc(x_in, 16)
                            sp.wait_ge(x_in, 16)
                        if store_row is not None:
                            sp.dma_start(out_rows[store_row], X3[:, :, :]).then_inc(f_out, 16)
                            sp.wait_ge(f_out, 16)
                        if not delta:
                            return
                        a_v = a_dram.rearrange("(t c h) i j -> t c i h j", t=NT, c=4)
                        t_v = t_dram.rearrange("(t c h) i j -> c i t h j", t=NT, c=4)
                        for i in range(NT):
                            sp.wait_ge(d_a, i + 1)
                            for c in range(4):
                                sp.dma_start(a_v[i, c], AS[32 * c:32 * c + 32, i % 2, :].rearrange("p (h j) -> p h j", h=DH))\
                                  .then_inc(d_stores[i % 2], 16)
                        for parity in d_stores:
                            sp.wait_ge(parity, 8 * 16)
                        if ffn:
                            sp.wait_ge(f_c3, 1)
                        sp.dma_start(MAT[:, :, :], a_dram).then_inc(d_mat, 16)
                        sp.wait_ge(d_inv, 31)
                        sp.dma_start(t_dram, INV[:, :, :]).then_inc(d_tst, 16)
                        sp.wait_ge(d_tst, 16)
                        for c in range(4):
                            for i in range(NT):
                                sp.dma_start(TI[32 * c:32 * c + 32, i, :, :], t_v[c][:, i, :, :]).then_inc(d_tld, 16)
                        sp.wait_ge(d_tld, 16 * 16)

                    @block.tensor
                    def _(pe):
                        def project_in():
                            for a in range(NH):
                                b = take(pe, f"x{a}")
                                for i in range(NT):
                                    last = pe.transpose(b[:, i * P:i * P + P], ND[:, i, a * P:a * P + P], ident[:, :])
                                last.then_inc(filled, 1)

                        def project(i):
                            pe.wait_ge(d_xt, 2)
                            b = take(pe, ("kv", i))
                            for a in range(NH):
                                last = pe.matmul(b[:, :], XT[:, a, i * P:i * P + P], WKV[:, a, :], start=a == 0, stop=a == NH - 1)
                            last.then_inc(filled, 1)
                            b = take(pe, ("qb", i))
                            for a in range(NH):
                                last = pe.matmul(b[:, 0:C + DH], XT[:, a, i * P:i * P + P], WQB[:, a, :],
                                                 start=a == 0, stop=a == NH - 1)
                            last.then_inc(filled, 1)

                        def turn(i):
                            pe.wait_ge(d_kh, i + 1)
                            b = take(pe, ("t1", i))
                            for a in range(NH):
                                pe.transpose(b[:, a * P:a * P + P], Q[:, i, a * P:a * P + P], ident[:, :])
                                last = pe.transpose(b[:, C + a * P:C + a * P + P], KH[:, i, a * P:a * P + P], ident[:, :])
                            last.then_inc(filled, 1)
                            b = take(pe, ("t2", i))
                            pe.wait_ge(d_kb, i + 1)
                            for a in range(NH):
                                last = pe.transpose(b[:, a * P:a * P + P], KB[:, i % 2, a * P:a * P + P], ident[:, :])
                            last.then_inc(filled, 1)

                        def pairs(i):
                            pe.wait_ge(d_turn, 3 * i + 3)
                            pe.wait_ge(d_kx, 4 * i + 4)
                            pe.wait_ge(d_exp, i + 1)
                            b = take(pe, ("ap", i))
                            for c in range(4):
                                rows, toks = slice(32 * c, 32 * c + 32), slice(i * P + 32 * c, i * P + 32 * c + 32)
                                for a in range(NH):
                                    pe.matmul(b[rows, a * P:a * P + P], KBT[:, a, toks], KX[:, a, :, rows], start=True, stop=True)
                                    last = pe.matmul(b[rows, C + a * P:C + a * P + P], KHT[:, a, toks], QX[:, a, :, rows],
                                                     start=True, stop=True)
                            last.then_inc(filled, 1)

                        def key_state(g):
                            rows, toks = slice(32 * (g % 4), 32 * (g % 4) + 32), slice(g * 32, g * 32 + 32)
                            if g == 0:
                                for k in range(3):
                                    pe.wait_ge(emptied[k], uses(k))
                            pe.wait_ge(d_s, g + 1)
                            for a in range(NH):
                                last = pe.matmul(KS[rows, a * P:a * P + P], KBT[:, a, toks], S[:, a, :], start=True, stop=True)
                            last.then_inc(d_ks, 1)

                        def outputs(g):
                            return OB[32 * (g % 4):32 * (g % 4) + 32, 0:C]

                        def solve(g):
                            i, c = g // 4, g % 4
                            rows = slice(32 * c, 32 * c + 32)
                            pe.wait_ge(d_r, g + 1)
                            if g == 0:
                                pe.wait_ge(d_tld, 16 * 16)
                            for h in range(DH):
                                last = pe.matmul(KS[rows, C + 32 * h:C + 32 * h + 32], TI[:, i, h, :],
                                                 RP[:, c, 32 * h:32 * h + 32], start=True, stop=True)
                            last.then_inc(d_v, 1)
                            if c > 0:
                                values(g - 1)
                            elif i > 0:
                                pe.wait_ge(d_os, i)
                            for a in range(NH):
                                pe.matmul(outputs(g)[:, a * P:a * P + P], QT[:, a, g * 32:g * 32 + 32], S[:, a, :],
                                          start=a == 0, stop=False)

                        def values(g):
                            i, c = g // 4, g % 4
                            for h in range(DH):
                                last = pe.matmul(outputs(g)[:, 32 * h:32 * h + 32], PT[:, i, h, :],
                                                 VP[:, c, 32 * h:32 * h + 32], start=False, stop=h == DH - 1)
                            if c == 3:
                                last.then_inc(d_o, 1)

                        def update(g):
                            i, c = g // 4, g % 4
                            pe.wait_ge(d_vs, g + 1)
                            if g < 15:
                                for a in range(NH):
                                    last = pe.matmul(SP[:, a * P:a * P + P], KH[:, i, a * P:a * P + P],
                                                     VP[:, c, a * P:a * P + P], start=g == 0 and a == 0,
                                                     stop=True, skip_group_check=True)
                                last.then_inc(d_up, 1)
                            if c == 3:
                                values(g)

                        stages = dict(project_in=project_in, project=project, turn=turn, pairs=pairs, key_state=key_state,
                                      solve=solve, update=update)
                        follow(ORDER_B, ffn.on_tensor(pe) if ffn else {}, stages if delta else {})
                    @block.scalar
                    def _(act):
                        link = linker(act, a_chain)

                        def project_in():
                            for a in range(NH):
                                b = wait_fill(act, f"x{a}")
                                act.copy(XT[:, a, :], b[:, :]).then_inc(d_xt, 1)
                                act.wait_ge(d_xt, a + 1)
                                act.sem_inc(empty(f"x{a}"), 1)

                        def project(i):
                            b = wait_fill(act, ("kv", i))
                            if i >= 1:
                                act.wait_ge(d_ss, i)
                            act.activation(SQ[:, :], b[:, 0:C], ACT.Square).then_inc(d_sq, 1)
                            if i >= 2:
                                act.wait_ge(d_vbb, i - 1)
                            act.copy(KH[:, i, :], b[:, 0:C]).then_inc(d_kc, 1)
                            act.activation(SG[:, i % 2, 0:C], b[:, C:2 * C], ACT.Tanh, scale=0.5)
                            b = wait_fill(act, ("qb", i))
                            act.activation(SG[:, i % 2, C:C + DH], b[:, C:C + DH], ACT.Tanh, scale=0.5)
                            act.copy(Q[:, i, :], b[:, 0:C]).then_inc(d_qk, 1)
                            act.wait_ge(d_qk, i + 1)
                            act.sem_inc(empty(("qb", i)), 1)

                        def turn(i):
                            b = wait_fill(act, ("t1", i))
                            toks = slice(i * P, i * P + P)
                            act.copy(QT[:, :, toks], b[:, 0:C].rearrange("p (a n) -> p a n", a=NH)).then_inc(d_turn, 1)
                            act.copy(KHT[:, :, toks], b[:, C:2 * C].rearrange("p (a n) -> p a n", a=NH)).then_inc(d_turn, 1)
                            if i == 0:
                                act.wait_ge(d_zero, 1)
                            else:
                                act.wait_ge(filled, TURN["ap", i - 1] + 1)
                            for h in range(4):
                                rows = slice(DN * h, DN * h + DN)
                                act.copy(KX[rows, :, h, :], b[rows, C:2 * C].rearrange("p (a n) -> p a n", a=NH))\
                                   .then_inc(d_kx, 1)
                            act.wait_ge(d_turn, 3 * i + 2)
                            act.wait_ge(d_kx, 4 * i + 4)
                            act.sem_inc(empty(("t1", i)), 1)
                            b = wait_fill(act, ("t2", i))
                            act.copy(KBT[:, :, toks], b[:, 0:C].rearrange("p (a n) -> p a n", a=NH)).then_inc(d_turn, 1)
                            act.wait_ge(d_turn, 3 * i + 3)
                            act.sem_inc(empty(("t2", i)), 1)

                        def pairs(i):
                            b = wait_fill(act, ("ap", i))
                            if i >= 2:
                                act.wait_ge(d_stores[i % 2], 64 * (i // 2))
                            act.copy(AS[:, i % 2, :], b[:, 0:C]).then_inc(d_a, 1)

                        def solve(g):
                            c = g % 4
                            rows = slice(32 * c, 32 * c + 32)
                            act.wait_ge(d_v, g + 1)
                            act.copy(VP[rows, c, :], KS[rows, C:2 * C]).then_inc(d_vs, 1)

                        def update(g):
                            if g % 4 == 3:
                                act.wait_ge(d_o, g // 4 + 1)
                                act.copy(O[:, g // 4, :], OB[:, 0:C]).then_inc(d_os, 1)

                        stages = dict(project_in=project_in, project=project, turn=turn, pairs=pairs, solve=solve,
                                      update=update)
                        follow(ORDER_B, ffn.on_scalar(act) if ffn else {}, stages if delta else {})
                    @block.vector
                    def _(dve):
                        link = linker(dve, d_chain)

                        def project(i):
                            b = wait_fill(dve, ("kv", i))
                            dve.wait_ge(d_sq, i + 1)
                            link(dve.tensor_reduce(SS[:, i, 0, :], SQ[:, :].rearrange("p (h n) -> p h n", n=DN), AX.X, ALU.add))
                            dve.tensor_scalar(SS[:, i, 0, :], SS[:, i, 0, :], 1e-24, None, ALU.max).then_inc(d_ss, 1)
                            dve.wait_ge(d_qk, i + 1)
                            sg = SG[:, i % 2, :]
                            link(dve.tensor_scalar(sg, sg, 0.5, 0.5, ALU.mult, ALU.add))
                            dve.tensor_tensor(VB[:, i, :], b[:, C:2 * C], SG[:, i % 2, 0:C], ALU.mult).then_inc(d_vb, 1)
                            dve.wait_ge(d_vb, i + 1)
                            dve.sem_inc(empty(("kv", i)), 1)
                            dve.wait_ge(d_kc, i + 1)
                            dve.wait_ge(d_rn, i + 1)
                            kh = KH[:, i, :].rearrange("p (h n) -> p h n", n=DN)
                            dve.tensor_tensor(kh, kh, SS[:, i, 1, :].unsqueeze(2).to_broadcast([P, DH, DN]), ALU.mult)\
                               .then_inc(d_kh, 1)

                        def pairs(i):
                            b = wait_fill(dve, ("ap", i))
                            dve.wait_ge(d_a, i + 1)
                            dve.tensor_tensor(PT[:, i, :, :], b[:, C:2 * C].rearrange("p (h n) -> p h n", n=DQ),
                                              K32["causal"][:, :].unsqueeze(1).to_broadcast([P, DH, DQ]), ALU.mult)\
                               .then_inc(d_pt, 1)
                            dve.wait_ge(d_pt, i + 1)
                            dve.sem_inc(empty(("ap", i)), 1)

                        def invert(r):
                            if r == 1:
                                link(dve.memset(S[:, :, :], 0.0))
                                dve.sem_inc(d_s, 1)
                                dve.wait_ge(d_mat, 16)
                            link(dve.tensor_tensor(TMP[:, 0:r, 0:r], INV[:, 0:r, 0:r],
                                                   MAT[:, r, 0:r].unsqueeze(1).to_broadcast([P, r, r]), ALU.mult))
                            dve.tensor_reduce(INV[:, 0:r, r], TMP[:, 0:r, 0:r], AX.X, ALU.add, negate=True)\
                               .then_inc(d_inv, 1)
                            dve.wait_ge(d_inv, r)

                        def key_state(g):
                            i, c = g // 4, g % 4
                            rows = slice(32 * c, 32 * c + 32)
                            dve.wait_ge(d_ks, g + 1)
                            if g == 0:
                                dve.wait_ge(d_vbb, NT)
                            dve.tensor_tensor(RP[rows, c, :], VB[rows, i, :], KS[rows, 0:C], ALU.subtract).then_inc(d_r, 1)

                        def update(g):
                            if g < 15:
                                dve.wait_ge(d_up, g + 1)
                                dve.tensor_tensor(S[:, :, :], SP[:, 0:C].rearrange("p (a n) -> p a n", a=NH),
                                                  K32["same32"][:, :].unsqueeze(1).to_broadcast([P, NH, P]), ALU.mult)\
                                   .then_inc(d_s, 1)

                        def finish(i, part):
                            o = O[:, i, :]
                            if part == 0:
                                dve.wait_ge(d_os, i + 1)
                                link(dve.bn_stats(ostats[:, i, :], o))
                                link(dve.bn_aggr(omv[:, i, :], ostats[:, i, :]))
                                dve.tensor_scalar(ove[:, i, 0:1], omv[:, i, 1:2], EPS, None, ALU.add).then_inc(d_ov, 1)
                            elif part == 1:
                                dve.wait_ge(d_or, i + 1)
                                link(dve.tensor_scalar(o, o, omv[:, i, 0:1], ove[:, i, 1:2], ALU.subtract, ALU.mult))
                                link(dve.tensor_tensor(o, o, LNB[:, 0, :], ALU.mult))
                            elif part == 2:
                                link(dve.tensor_tensor(o, o, LNB[:, 1, :], ALU.add))
                                if i == 0 and store_row is not None:
                                    dve.wait_ge(f_out, 16)
                                link(dve.tensor_tensor(X3[:, i, :], o, X2[:, i, :], ALU.add))
                            else:
                                normalise(dve, link, X3, NF, (i, i + 1), x3_turn(i))

                        def norm_x():
                            dve.wait_ge(x_in, 16)
                            normalise(dve, link, XR, NR, (0, NT), 1)

                        stages = dict(project=project, pairs=pairs, invert=invert, key_state=key_state, update=update,
                                      finish=finish)
                        always = {"norm_x": norm_x} if loads else {}
                        follow(ORDER_B, ffn.on_vector(dve, link) if ffn else {}, stages if delta else {}, always)
                    @block.gpsimd
                    def _(pool):
                        def project(i):
                            pool.wait_ge(d_ss, i + 1)
                            pool.tensor_tensor(SS[:, i, 1, :], SS[:, i, 0, :], K32["nhalf"][:, 0:DH], ALU.pow).then_inc(d_rn, 1)
                            beta = SG[:, i % 2, C:C + DH].unsqueeze(2).to_broadcast([P, DH, DN])
                            pool.wait_ge(d_kh, i + 1)
                            if i >= 2:
                                pool.wait_ge(filled, TURN["t2", i - 2] + 1)
                            pool.tensor_tensor(KB[:, i % 2, :].rearrange("p (h n) -> p h n", n=DN),
                                               KH[:, i, :].rearrange("p (h n) -> p h n", n=DN), beta, ALU.mult)\
                                .then_inc(d_kb, 1)
                            pool.wait_ge(d_vb, i + 1)
                            vb = VB[:, i, :].rearrange("p (h n) -> p h n", n=DN)
                            pool.tensor_tensor(vb, vb, beta, ALU.mult).then_inc(d_vbb, 1)

                        def turn(i):
                            pool.wait_ge(d_turn, 3 * i + 1)
                            if i >= 1:
                                pool.wait_ge(filled, TURN["ap", i - 1] + 1)
                            toks = slice(i * P, i * P + P)
                            for a in range(NH):
                                last = pool.tensor_tensor(
                                    QX[:, a, :, :], QT[:, a, toks].unsqueeze(1).to_broadcast([P, 4, P]),
                                    K32["heads4"][:, :].unsqueeze(2).to_broadcast([P, 4, P]), ALU.mult)
                            last.then_inc(d_exp, 1)

                        def finish(i, part):
                            if part == 0:
                                pool.wait_ge(d_ov, i + 1)
                                pool.tensor_tensor(ove[:, i, 1:2], ove[:, i, 0:1], K32["nhalf"][:, 0:1], ALU.pow)\
                                    .then_inc(d_or, 1)
                            elif part == 3:
                                root(pool, (i, i + 1), x3_turn(i))

                        if delta:
                            pool.memset(KX[:, :, :, :], 0.0).then_inc(d_zero, 1)
                        stages = dict(project=project, turn=turn, finish=finish)
                        always = {"norm_x": lambda: root(pool, (0, NT), 1)} if loads else {}
                        follow(ORDER_B, stages if delta else {}, always)
            end_block()

        with nc.Block() as block:
            @block.sync
            def _(sp):
                sp.dma_start(XR[:, :, :], x_rows[0]).then_inc(x_in, 16)
                sp.wait_ge(x_in, 16)

            @block.vector
            def _(dve):
                dve.wait_ge(x_in, 16)
                normalise(dve, linker(dve, d_chain), XR, NR, (0, NT), 1)

            @block.gpsimd
            def _(pool):
                root(pool, (0, NT), 1)
        end_block()

        rwkv_ffn(ffn_on=False, norm_row=False)
        delta_ffn(delta=False, load_row=1)
        rwkv_ffn(ffn_on=False)
        delta_ffn(load_row=2)
        with nc.Fori(2, B - 1) as i:
            rwkv_ffn()
            delta_ffn(load_row=i + 1, store_row=i - 2)
        rwkv_ffn()
        delta_ffn(store_row=B - 3)
        rwkv_ffn(rwkv=False)
        delta_ffn(ffn_on=False, store_row=B - 2)
        rwkv_ffn(rwkv=False, norm_row=False, store_row=B - 1)


def constants():
    import numpy as np
    p = np.arange(P)
    chunk, q = p // RQ, p % RQ
    same = chunk[:, None] == chunk[None, :]
    eye = np.eye(P)
    mats = {
        "ident": eye,
        "before": -(same & (p[:, None] < p[None, :])).astype(np.float32),
        "after": -(same & (p[:, None] > p[None, :])).astype(np.float32),
        "earlier": q[:, None] < np.arange(RQ)[None, :],
        "chunks": -(chunk[:, None] == np.arange(2)[None, :]).astype(np.float32),
        "heads8": p[:, None] // RN == np.arange(8)[None, :],
        "same16": p[:, None] // RN == p[None, :] // RN,
        "same32": p[:, None] // DN == p[None, :] // DN,
        "heads4": p[:, None] // DN == np.arange(4)[None, :],
        "causal": np.arange(DQ)[None, :] >= (p % DQ)[:, None],
        "group_low": np.tile((np.arange(4)[None, :] < np.arange(4)[:, None]).reshape(1, -1), (P, 1)),
        "expert_low": np.tile((np.arange(E)[None, :] < np.arange(E)[:, None]).reshape(1, -1), (P, 1)),
        "nhalf": np.full((P, 32), -0.5),
        "lane_eye": np.tile(np.eye(DQ).reshape(1, -1), (P, 1)),
    }
    c32 = np.concatenate([np.asarray(mats[k], np.float32) for k in CONST32], 1)
    forbid = np.where(np.arange(RQ)[None, :] <= q[:, None], -BIG, 0.0)
    pick = [(p[:, None] % E == e) & (p[:, None] < 3 * E) & np.ones((1, P), bool) for e in range(E)]
    b16 = mybir.dt.np(mybir.dt.bfloat16)
    c16 = np.concatenate([eye, np.tile(forbid, (1, 8)), np.concatenate(pick, 1)], 1).astype(b16)
    return np.ascontiguousarray(c32), np.ascontiguousarray(c16)


def kernel(**inputs):
    import numpy as np
    import concourse.bacc as bacc
    from concourse.bass_utils import run_bass_kernel_spmd as run

    i = {k[3:]: np.asarray(v) for k, v in inputs.items()}

    def halves(v):
        return v.reshape(NH, P).T

    def experts(routed, shared):
        return np.concatenate([shared, routed.reshape(E * EH, C)], 0).T

    down = np.concatenate([i["ffn_sh_down_w"].T.reshape(NS, EH, C), i["ffn_down_w"].transpose(0, 2, 1)], 0)
    c32, c16 = constants()
    arrays = {
        "x": i["attn_a_x"],
        "maa": np.concatenate([halves(i["attn_a_time_maa_" + f]) for f in "xwkvr"], 1),
        "maa_w1": i["attn_a_maa_w1"], "maa_w2": i["attn_a_maa_w2"],
        "decay_w1": i["attn_a_decay_w1"], "decay_w2": i["attn_a_decay_w2"],
        "time_decay": i["attn_a_time_decay"].reshape(C),
        "u_col": halves(i["attn_a_time_faaaa"].reshape(C)) ,
        "w_rkvo": np.stack([i["attn_a_W" + f] for f in "rkvo"]),
        "ln_a": np.concatenate([halves(i["attn_a_ln_g"]), halves(i["attn_a_ln_b"])], 1),
        "w_delta_kv": np.concatenate([i["attn_b_Wk"], i["attn_b_Wv"]], 1),
        "w_delta_qb": np.concatenate([i["attn_b_Wq"], i["attn_b_Wb"]], 1),
        "ln_b": np.stack([i["attn_b_ln_w"], i["attn_b_ln_b"]]),
        "router": i["ffn_router_weight"].T, "e_bias": i["ffn_e_bias"],
        "gate": experts(i["ffn_gate_w"], i["ffn_sh_gate_w"]),
        "up": experts(i["ffn_up_w"], i["ffn_sh_up_w"]),
        "down": down, "c32": c32, "c16": c16,
    }
    nc = bacc.Bacc("TRN2", target_bir_lowering=False, num_devices=1)
    args, feeds = [], {}
    for name, a in arrays.items():
        a = np.ascontiguousarray(a)
        feeds[f"in_{name}"] = a
        args.append(nc.dram_tensor(f"in_{name}", a.shape, mybir.dt.from_np(a.dtype), kind="ExternalInput").ap())
    out = nc.dram_tensor("out", (B, T, C), mybir.dt.float32, kind="ExternalOutput").ap()
    hybrid_layers(nc, *args, out)
    r = run(nc, [feeds], core_ids=[0])
    return r.results[0]["out"]
```

```python
import concourse.bass as bass
from concourse import mybir
from contextlib import ExitStack

B, T, C = 16, 512, 256
P = 128
NT = T // P
NH = C // P
E, EH = 16, 128
NS = 2
NE = NS + E
RH, RN, RQ = 16, 16, 64
DH, DN, DQ = 8, 32, 32
EPS = 1e-5
BIG = 1e9
FULL = 2.0 ** 15
XS = FULL / C ** 0.5
ROUTE = 2.5
HS = FULL / (C * ROUTE)
TINY = 1e-30

CONST32 = {"ident": 128, "before": 128, "after": 128, "earlier": RQ, "chunks": 2, "heads8": 8,
           "same16": 128, "same32": 128, "heads4": 4, "causal": DQ, "nhalf": 32, "lane_eye": DQ * DQ}
CONST16 = {"identb": 128, "forbid": 512, "pick": E * P, "group_low": 16, "expert_low": 256}

SCHEDULE_A = """
    ffn_turn mix_in route +2 mix_first rank_groups mix.0 rank_experts +1 use.0 +2 mix.1 +1 weigh +4 use.1
    decay_rates parts mix.2 +4 use.2 decays +1 mix.3 +4 use.3 +2 prep +7 args.0 +2 scores.0 +3 intra.0 +5
    inter.0 +2 norm_y.0 +2 args.1 +3 scores.1 +6 turn_y.0 +1 project_y.0 +1 intra.1 +4 inter.1 +2 norm_x1.0 +4
    norm_y.1 norm_x2 args.2 +1 scores.2 +3 turn_y.1 +2 project_y.1 intra.2 +2 norm_x1.1 inter.2 +4 norm_y.2
    args.3 +1 scores.3 +5 turn_y.2 +1 project_y.2 +1 intra.3 +5 norm_x1.2 +1 inter.3 +2 norm_y.3 +5 turn_y.3 +4
    project_y.3 +2 norm_x1.3
"""
SCHEDULE_B = """
    project_in ffn_turn project.0 route project.1 +2 turn.0 rank_groups +2 project.2 pairs.0 +2 turn.1 project.3
    pairs.1 +2 turn.2 rank_experts +1 pairs.2 turn.3 +4 pairs.3 weigh parts +3 invert.1.0 invert.1.1 +1
    invert.2.0 invert.2.1 +1 invert.3.0 invert.3.1 +1 invert.4.0 invert.4.1 +1 invert.5.0 invert.5.1 invert.6.0
    invert.6.1 +1 invert.7.0 invert.7.1 +1 invert.8.0 invert.8.1 +1 invert.9.0 +1 invert.9.1 +1 invert.10.0
    invert.10.1 +1 invert.11.0 invert.11.1 invert.12.0 +1 invert.12.1 +1 invert.13.0 +1 invert.13.1 +2
    invert.14.0 +1 invert.14.1 +1 invert.15.0 +1 invert.15.1 +1 invert.16.0 +1 invert.16.1 +1 invert.17.0 +1
    invert.17.1 +1 invert.18.0 +1 invert.18.1 +1 invert.19.0 +1 invert.19.1 +1 invert.20.0 +1 invert.20.1 +1
    invert.21.0 +1 invert.21.1 +1 invert.22.0 +1 invert.22.1 +1 invert.23.0 +1 invert.23.1 +1 invert.24.0 +1
    invert.24.1 +1 invert.25.0 +1 invert.25.1 +1 invert.26.0 +1 invert.26.1 +1 invert.27.0 +1 invert.27.1 +1
    invert.28.0 invert.28.1 invert.29.0 +1 invert.29.1 +2 invert.30.0 +1 invert.30.1 +1 invert.31.0 +1
    invert.31.1 +1 norm_x +11 apply.0 +1 apply.1 key_state.0 +1 query.0 update.0 key_state.1 +1 query.1 update.1
    +1 key_state.2 +1 query.2 update.2 +1 key_state.3 query.3 update.3 key_state.4 +1 query.4 update.4 +1
    finish.0.0 key_state.5 +1 query.5 update.5 finish.0.1 key_state.6 +2 query.6 update.6 finish.0.2 key_state.7
    query.7 update.7 +1 finish.0.3 key_state.8 +1 query.8 update.8 finish.0.4 finish.1.0 key_state.9 +1 query.9
    update.9 finish.1.1 key_state.10 query.10 update.10 +1 finish.1.2 +1 key_state.11 +1 query.11 update.11
    finish.1.3 key_state.12 +1 query.12 update.12 finish.1.4 finish.2.0 key_state.13 +1 query.13 update.13 +1
    finish.2.1 key_state.14 +1 query.14 update.14 finish.2.2 key_state.15 +1 query.15 update.15 finish.2.3
    finish.2.4 finish.3.0 finish.3.1 finish.3.2 finish.3.3 +1 finish.3.4
"""


def experts_in_order():
    for e in range(NE):
        yield from (("g", e, 0), ("g", e, 1), ("u", e, 0), ("u", e, 1))
        if e > 0:
            yield from (("d", e - 1, 0), ("d", e - 1, 1))
    yield from (("d", NE - 1, 0), ("d", NE - 1, 1))


def ordered(schedule):
    items, order = experts_in_order(), []
    for word in schedule.split():
        if word[0] == "+":
            order += [next(items) for _ in range(int(word[1:]))]
        else:
            name, *numbers = word.split(".")
            order.append((name, *map(int, numbers)))
    return order + list(items) + [("ffn_out",)]


ORDER_A, ORDER_B = ordered(SCHEDULE_A), ordered(SCHEDULE_B)


def follow(order, *stages):
    for step in order:
        for named in stages:
            if step[0] in named:
                named[step[0]](*step[1:])


def hybrid_layers(nc, x, maa, maa_w1, maa_w2, decay_w1, decay_w2, time_decay, u_col, w_rkvo, ln_a,
                  w_delta_kv, w_delta_qb, ln_b, router, e_bias, gate, up, down, c32, c16, out):
    f32, bf16 = mybir.dt.float32, mybir.dt.bfloat16
    ALU, ACT, AX = mybir.AluOpType, mybir.ActivationFunctionType, mybir.AxisListType
    x_rows = x.rearrange("b (t p) c -> b p t c", p=P)
    out_rows = out.rearrange("b (t p) c -> b p t c", p=P)

    ctx = ExitStack()
    with ctx:
        copies = [0]

        def sb(name, shape, dt=f32, stack=ctx):
            if stack is not ctx:
                name = f"{name}_{copies[0]}"
            return stack.enter_context(nc.sbuf_tensor(name, shape, dt))

        f16 = mybir.dt.float16
        WG, WU = (sb(n, [P, 2, NH, NE * EH], f16) for n in ("WG", "WU"))
        WD = sb("WD", [EH, 2, NE, C], f16)
        FG, FH, FO = sb("FG", [P, NE]), sb("FH", [P, NE]), sb("FO", [P, 1])
        WRT = sb("WRT", [P, NH, E])
        EB = sb("EB", [P, E])
        MAA = sb("MAA", [P, 5, NH])
        W1 = sb("W1", [P, NH, P])
        W2 = sb("W2", [P, 4, C])
        DW1 = sb("DW1", [P, NH, 64])
        DWM = sb("DWM", [P, RH])
        UC = sb("UC", [P, NH])
        UB = sb("UB", [P, NH, P])
        WR = sb("WR", [P, 4, NH, C])
        LNA = sb("LNA", [P, 2, NH])
        WKV, WQB = sb("WKV", [P, NH, 2 * C]), sb("WQB", [P, NH, C + DH])
        LNB = sb("LNB", [P, 2, C])
        K32 = {k: sb("c_" + k, [P, n]) for k, n in CONST32.items() if k != "lane_eye"}
        K16 = {k: sb("c_" + k, [P, n], bf16) for k, n in CONST16.items()}
        XR, X1, X2, X3 = (sb(n, [P, NT, C]) for n in ("XR", "X1", "X2", "X3"))
        NR, NF, ND = (sb(n, [P, NT, C]) for n in ("NR", "NF", "ND"))
        stats, mv, ve = sb("stats", [P, NT, 6]), sb("mv", [P, NT, 2]), sb("ve", [P, NT, 2])
        KWP = sb("KWP", [P, 2, C])
        VP = sb("VP", [P, 4, C])
        INV = sb("INV", [P, DQ, DQ])
        C3 = sb("C3", [P, NT, P], bf16)
        MAT = sb("MAT", [P, DQ, DQ])
        DW2, TD = (MAT[0:64, 8 * k:8 * k + 8, :].rearrange("p a b -> p (a b)") for k in range(2))
        a_dram = nc.dram_tensor("a_scratch", (P, DQ, DQ), f32).ap()
        t_dram = nc.dram_tensor("t_scratch", (P, DQ, DQ), f32).ap()
        ident, identb = K32["ident"], K16["identb"]

        banks = [ctx.enter_context(nc.psum_tensor(f"bank{i}", [P, 512], f32)) for i in range(8)]
        GB, UBK, CBK, YA, YB = banks[:5]
        RING = banks[5:]

        sems = {}

        def sem(name):
            sems[name] = ctx.enter_context(nc.semaphore(name))
            return sems[name]

        loaded = sem("loaded")
        n_var, n_rstd = sem("norm_var"), sem("norm_rstd")
        d_chain, p_chain = sem("dve_chain"), sem("pool_chain")
        f_tr, f_xt, f_xh, f_xl = (sem(n) for n in ("ffn_transposed", "ffn_xt", "ffn_xt_hi", "ffn_xt_lo"))
        f_ya = sem("ffn_first_half")
        f_hi, f_lo = sem("ffn_hidden_hi"), sem("ffn_hidden_lo")
        w_in = [sem(n) for n in ("gate_loaded", "up_loaded", "down_loaded")]
        w_sq, w_norm, w_root, w_turn, w_max, w_scaled, w_hi, w_lo, w_dsq, w_half = (sem("w_" + n) for n in (
            "squares", "norms", "roots", "turned", "maxima", "scaled", "hi", "lo", "down_squares", "halves"))
        f_lg, f_th, f_lt, f_c3, f_ct, f_cs = (sem(n) for n in (
            "ffn_logits", "ffn_logit_tanh", "ffn_logit_turned", "ffn_parts", "ffn_parts_turned", "ffn_parts_ready"))
        f_g, f_u, f_c, f_tanh, f_gd, f_h, f_dn = (sem(n) for n in (
            "ffn_gate", "ffn_up", "ffn_spread", "ffn_tanh", "ffn_gate_read", "ffn_hidden", "ffn_down"))
        f_res, f_out = sem("ffn_result"), sem("ffn_stored")
        filled = sem("ring_filled")
        emptied = [sem(f"ring{i}_emptied") for i in range(3)]
        x_in = sem("x_loaded")
        r_xt, r_xx = sem("r_xt"), sem("r_xx")
        r_mixin, r_m, r_half, r_mixed = (sem(n) for n in ("r_mix_in", "r_tanh", "r_half_mixed", "r_mixed"))
        r_dt, r_we, r_dec, r_ws = (sem(n) for n in ("r_decay_tanh", "r_rate", "r_decays", "r_chunk_decay"))
        r_k, r_v, r_r, r_kt, r_prod, r_rx = (sem(n) for n in ("r_k", "r_v", "r_rT", "r_kT", "r_product", "r_spread"))
        r_wm, r_e, r_p, r_kw, r_s = (sem(n) for n in ("r_rate_masked", "r_weights", "r_scores", "r_kw", "r_state"))
        r_yn, r_yt, r_used = (sem(n) for n in ("r_y_norm", "r_yT", "r_scores_used"))
        r_yv, r_yr = sem("r_y_var"), sem("r_y_rstd")
        r_wx = sem("r_rate_by_channel")
        d_xt, d_vb, d_kb, d_vbb = (sem(n) for n in ("d_xt", "d_values_silu", "d_keys_by_beta", "d_values_by_beta"))
        d_ov, d_or, d_kc = sem("d_out_var"), sem("d_out_rstd"), sem("d_k_copied")
        d_zero, d_kx = sem("d_spread_cleared"), sem("d_keys_spread")
        d_qk, d_sq, d_ss, d_rn, d_kh, d_pt, d_turn, d_exp, d_a, d_st = (sem(n) for n in (
            "d_evacuated", "d_squares", "d_sums", "d_rnorm", "d_keys", "d_causal", "d_turned", "d_spread", "d_pairs", "d_pairs_stored_even"))
        d_stores = [d_st, sem("d_pairs_stored_odd")]
        d_mat, d_inv, d_tst, d_tld = (sem(n) for n in ("d_problems", "d_inverse", "d_inverse_stored", "d_inverse_loaded"))
        d_mul, d_tz, d_wv, d_wk, d_ks, d_vs, d_up, d_s, d_o, d_os = (sem(n) for n in (
            "d_products", "d_zeros", "d_values_solved", "d_keys_solved", "d_key_state", "d_values", "d_updated", "d_state", "d_out", "d_out_read"))

        numbers = [s.num for s in sems.values()]
        assert numbers == list(range(numbers[0], numbers[0] + len(numbers)))
        every_sem = range(numbers[0], numbers[-1] + 1)

        def end_block():
            copies[0] += 1
            nc.sync.sem_clear(every_sem)
            nc.all_engine_barrier(sem_only=True)

        def linker(eng, chain):
            count = [0]

            def link(ins):
                count[0] += 1
                ins.then_inc(chain, 1)
                eng.wait_ge(chain, count[0])
            return link

        with nc.Block() as block:
            staged = ExitStack()
            G32, U32 = (sb(n, [P, NH, NE * EH], f32, staged) for n in ("g32", "u32"))
            SQ = WD[:, :, :, :].rearrange("p s e n -> p (s e n)").bitcast(f32).rearrange("p (a n) -> p a n", a=NH)
            D32 = sb("d32", [EH, NE, C], f32, staged)
            ONE = sb("one", [P, 1], f32, staged)
            N2, RN_, NM = (sb(n, [P, 2 * NE], f32, staged) for n in ("norm2", "rnorm", "norm"))
            MX, MB = sb("mx", [2 * NE, 1], f32, staged), sb("mb", [2 * NE, P], f32, staged)
            MS, RS, NN, RR = (sb(n, [P, 2 * NE], f32, staged) for n in ("ms", "rs", "nn", "rr"))
            DM, DX, DB, DR = (sb(n, [P, 1], f32, staged) for n in ("dm", "dx", "db", "dr"))
            DXB = sb("dxb", [1, P], f32, staged)

            @block.sync
            def _(sp):
                sp.dma_start(G32[:, :, :], gate.rearrange("(a p) n -> p a n", p=P)).then_inc(w_in[0], 16)
                sp.dma_start(U32[:, :, :], up.rearrange("(a p) n -> p a n", p=P)).then_inc(w_in[1], 16)
                sp.dma_start(D32[:, :, :], down.rearrange("e p n -> p e n")).then_inc(w_in[2], 16)
                n = 0
                for k, (dst, src) in enumerate([
                        (WRT[:, :, :], router.rearrange("(a p) n -> p a n", p=P)),
                        (EB[:, :], e_bias.unsqueeze(0).to_broadcast([P, E])),
                        (MAA[:, :, :], maa.rearrange("p (f a) -> p f a", a=NH)),
                        (W1[:, :, :], maa_w1.rearrange("(a p) n -> p a n", p=P)),
                        (DW1[:, :, :], decay_w1.rearrange("(a p) n -> p a n", p=P)),
                        (DW2[:, :], decay_w2),
                        (TD[:, :], time_decay.unsqueeze(0).to_broadcast([64, C])),
                        (UC[:, :], u_col),
                        (WR[:, :, :, :], w_rkvo.rearrange("f (a p) n -> p f a n", p=P)),
                        (LNA[:, :, :], ln_a.rearrange("p (f a) -> p f a", a=NH)),
                        (WKV[:, :, :], w_delta_kv.rearrange("(a p) n -> p a n", p=P)),
                        (WQB[:, :, :], w_delta_qb.rearrange("(a p) n -> p a n", p=P)),
                        (LNB[:, :, :], ln_b.unsqueeze(0).to_broadcast([P, 2, C]))]):
                    sp.dma_start(dst, src).then_inc(loaded, 16)
                    n += 16
                at = 0
                for k, cols in CONST32.items():
                    dst = INV[:, :, :].rearrange("p a b -> p (a b)") if k == "lane_eye" else K32[k][:, :]
                    sp.dma_start(dst, c32[:, at:at + cols]).then_inc(loaded, 16)
                    at += cols
                    n += 16
                at = 0
                for k, cols in CONST16.items():
                    sp.dma_start(K16[k][:, :], c16[:, at:at + cols]).then_inc(loaded, 16)
                    at += cols
                    n += 16
                sp.wait_ge(p_chain, 1)
                for f in range(4):
                    sp.dma_start(W2[32 * f:32 * f + 32, f, :], maa_w2[f]).then_inc(loaded, 16)
                    n += 16
                sp.wait_ge(loaded, n)
                sp.sem_inc(x_in, 1)
                for weights in w_in:
                    sp.wait_ge(weights, 16)

            @block.tensor
            def _(pe):
                pe.wait_ge(p_chain, 1)
                for m in range(2):
                    pe.wait_ge(w_half, m + 1)
                    for e in range(NE):
                        last = pe.matmul(banks[0][:, m * NE + e:m * NE + e + 1], SQ[:, 0, e * EH:e * EH + EH],
                                         ONE[:, :], start=True, stop=True)
                    last.then_inc(w_norm, 1)
                pe.wait_ge(x_in, 1)
                pe.wait_ge(w_turn, 1)
                pe.transpose(banks[1][0:2 * NE, 0:P], NM[:, :], ident[:, :]).then_inc(w_norm, 1)
                pe.wait_ge(w_max, 1)
                pe.matmul(banks[2][:, 0:2 * NE], MB[:, :], ident[0:2 * NE, 0:2 * NE], start=True, stop=True)\
                  .then_inc(w_norm, 1)
                pe.wait_ge(w_turn, 2)
                pe.transpose(banks[3][0:1, 0:P], DM[:, :], ident[:, :]).then_inc(w_norm, 1)
                pe.wait_ge(w_max, 2)
                pe.matmul(banks[4][:, 0:1], DXB[:, :], ident[0:1, 0:1], start=True, stop=True).then_inc(w_norm, 1)

            @block.scalar
            def _(act):
                act.wait_ge(w_in[0], 16)
                act.activation(SQ[:, :, :], G32[:, :, :], ACT.Square).then_inc(w_sq, 1)
                act.wait_ge(w_in[1], 16)
                act.wait_ge(w_norm, 1)
                act.activation(SQ[:, :, :], U32[:, :, :], ACT.Square).then_inc(w_sq, 1)
                act.wait_ge(w_scaled, 1)
                act.activation(SQ[:, :, :].rearrange("p a n -> p (a n)"), D32[:, :, :].rearrange("p e n -> p (e n)"),
                               ACT.Square).then_inc(w_dsq, 1)
                act.wait_ge(w_scaled, 2)
                act.copy(WG[:, 0, :, :], G32[:, :, :]).then_inc(w_hi, 1)
                act.wait_ge(w_scaled, 3)
                act.copy(WU[:, 0, :, :], U32[:, :, :]).then_inc(w_hi, 1)
                act.wait_ge(w_scaled, 4)
                act.copy(WD[:, 0, :, :], D32[:, :, :]).then_inc(w_hi, 1)

            @block.gpsimd
            def _(pool):
                pool.memset(ONE[:, :], 1.0)
                pool.memset(W2[:, :, :], 0.0).then_inc(p_chain, 1)
                pool.memset(KWP[:, :, :], 0.0)
                pool.memset(VP[:, :, :], 0.0)
                pool.memset(C3[:, :, :], 0.0)
                pool.memset(DWM[:, :], 0.0).then_inc(p_chain, 1)
                pool.wait_ge(p_chain, 2)
                pool.wait_ge(x_in, 1)
                pool.wait_ge(w_root, 1)
                for m in range(2):
                    last = pool.tensor_tensor(RN_[:, m * NE:m * NE + NE], N2[:, m * NE:m * NE + NE],
                                              K32["nhalf"][:, 0:NE], ALU.pow)
                last.then_inc(p_chain, 1)
                for n, (w16, w32) in enumerate(((WG[:, :, :, :], G32[:, :, :]), (WU[:, :, :, :], U32[:, :, :]))):
                    pool.wait_ge(w_hi, n + 1)
                    pool.tensor_tensor(w16[:, 1], w32, w16[:, 0], ALU.subtract).then_inc(w_lo, 1)
                    if n == 0:
                        pool.wait_ge(w_root, 2)
                        pool.tensor_tensor(DR[:, :], DB[:, :], K32["nhalf"][:, 0:1], ALU.pow).then_inc(p_chain, 1)

            @block.vector
            def _(dve):
                link = linker(dve, d_chain)
                for m in range(2):
                    dve.wait_ge(w_sq, m + 1)
                    dve.tensor_tensor(SQ[:, 0, :], SQ[:, 0, :], SQ[:, 1, :], ALU.add).then_inc(w_half, 1)
                dve.wait_ge(x_in, 1)
                dve.wait_ge(p_chain, 2)
                link(dve.tensor_reduce(DWM[0:64, :], DW2[:, :].rearrange("p (h n) -> p h n", n=RN), AX.X, ALU.add))
                link(dve.tensor_reduce(DWM[64:65, :], TD[0:1, :].rearrange("p (h n) -> p h n", n=RN), AX.X, ALU.add))
                dve.tensor_scalar(DWM[0:64, :], DWM[0:64, :], 1.0 / RN, None, ALU.mult)
                dve.tensor_scalar(DWM[64:65, :], DWM[64:65, :], 1.0 / RN, None, ALU.mult)
                for a in range(NH):
                    dve.tensor_scalar(UB[:, a, :], K32["same16"][:, :], UC[:, a:a + 1], None, ALU.mult)

                dve.wait_ge(w_norm, 2)
                dve.tensor_scalar(N2[:, :], banks[0][:, 0:2 * NE], TINY, None, ALU.max).then_inc(w_root, 1)
                dve.wait_ge(w_root, 1)
                dve.wait_ge(p_chain, 3)
                dve.tensor_tensor(NM[:, :], N2[:, :], RN_[:, :], ALU.mult).then_inc(w_turn, 1)
                dve.wait_ge(w_turn, 1)
                link(dve.tensor_tensor(NN[:, 0:NE], NM[:, 0:NE], NM[:, NE:], ALU.mult))
                link(dve.tensor_tensor(RR[:, 0:NE], RN_[:, 0:NE], RN_[:, NE:], ALU.mult))
                dve.wait_ge(w_norm, 3)
                link(dve.tensor_reduce(MX[:, :], banks[1][0:2 * NE, 0:P], AX.X, ALU.max))
                dve.tensor_copy(MB[:, :], MX[:, :].to_broadcast([2 * NE, P])).then_inc(w_max, 1)
                dve.wait_ge(w_norm, 4)
                link(dve.tensor_scalar(MS[:, :], banks[2][:, 0:2 * NE], 1.0 / FULL, None, ALU.mult))
                link(dve.reciprocal(RS[:, :], MS[:, :]))
                g4, u4 = (w[:, :, :].rearrange("p a (e n) -> p a e n", n=EH) for w in (G32, U32))

                def scale(w4, m):
                    for a in range(NH):
                        last = dve.tensor_tensor(w4[:, a], w4[:, a], RS[:, m * NE:m * NE + NE].unsqueeze(2)
                                                 .to_broadcast([P, NE, EH]), ALU.mult)
                    last.then_inc(w_scaled, 1)

                dve.wait_ge(w_in[2], 16)
                dve.tensor_tensor(D32[:, :, :], D32[:, :, :], NN[:, 0:NE].unsqueeze(2).to_broadcast([P, NE, C]), ALU.mult)\
                   .then_inc(w_scaled, 1)
                scale(g4, 0)
                dve.tensor_scalar(FG[:, :], MS[:, 0:NE], 0.5 / XS, None, ALU.mult)
                link(dve.tensor_tensor(FH[:, :], MS[:, 0:NE], MS[:, NE:], ALU.mult))
                link(dve.tensor_tensor(FH[:, :], FH[:, :], RR[:, 0:NE], ALU.mult))
                dve.tensor_scalar(FH[:, :], FH[:, :], 0.5 * HS / (XS * XS), None, ALU.mult)
                dve.wait_ge(w_dsq, 1)
                link(dve.tensor_reduce(DM[:, :], SQ[:, :, :].rearrange("p a n -> p (a n)"), AX.X, ALU.max))
                dve.sem_inc(w_turn, 1)
                scale(u4, 1)
                dve.wait_ge(w_norm, 5)
                link(dve.tensor_reduce(DX[0:1, :], banks[3][0:1, 0:P], AX.X, ALU.max))
                link(dve.tensor_scalar(DX[0:1, :], DX[0:1, :], TINY, None, ALU.max))
                dve.tensor_copy(DXB[:, :], DX[0:1, :].to_broadcast([1, P])).then_inc(w_max, 1)
                dve.wait_ge(w_norm, 6)
                dve.tensor_copy(DB[:, :], banks[4][:, 0:1]).then_inc(w_root, 1)
                dve.wait_ge(p_chain, 4)
                link(dve.tensor_scalar(DR[:, :], DR[:, :], FULL, None, ALU.mult))
                dve.tensor_scalar(D32[:, :, :], D32[:, :, :], DR[:, :], None, ALU.mult).then_inc(w_scaled, 1)
                link(dve.reciprocal(FO[:, :], DR[:, :]))
                dve.tensor_scalar(FO[:, :], FO[:, :], 1.0 / HS, None, ALU.mult)
                dve.wait_ge(w_hi, 3)
                dve.tensor_tensor(WD[:, 1, :, :], D32[:, :, :], WD[:, 0, :, :], ALU.subtract).then_inc(w_lo, 1)
            staged.close()
        end_block()

        def turns(names):
            return {name: n for n, name in enumerate(names)}

        def measure(dve, link, src, tiles):
            a, b = tiles
            for t in range(a, b):
                last = dve.bn_stats(stats[:, t, :], src[:, t, :])
            link(last)
            for t in range(a, b):
                last = dve.bn_aggr(mv[:, t, :], stats[:, t, :])
            link(last)
            dve.tensor_scalar(ve[:, a:b, 0], mv[:, a:b, 1], EPS, None, ALU.add).then_inc(n_var, 1)

        def standardise(dve, link, src, dst, tiles, turn):
            a, b = tiles
            dve.wait_ge(n_rstd, turn)
            for t in range(a, b):
                last = dve.tensor_scalar(dst[:, t, :], src[:, t, :], mv[:, t, 0:1], ve[:, t, 1:2],
                                         ALU.subtract, ALU.mult)
            link(last)

        def normalise(dve, link, src, dst, tiles, turn):
            measure(dve, link, src, tiles)
            standardise(dve, link, src, dst, tiles, turn)

        def root(pool, tiles, turn):
            a, b = tiles
            pool.wait_ge(n_var, turn)
            pool.tensor_tensor(ve[:, a:b, 1], ve[:, a:b, 0], K32["nhalf"][:, 0:b - a], ALU.pow).then_inc(n_rstd, 1)
            pool.wait_ge(n_rstd, turn)

        class Ffn:

            def __init__(self, tag, src, dst, stack, spare=None, lo_on_pool=True):
                self.lo_on_pool = lo_on_pool
                def t(n, shape, dt=f32):
                    return sb(f"{tag}_{n}", shape, dt, stack)
                self.src, self.dst = src, dst
                self.xt = t("xt", [P, 2, NH, T], f16)
                self.th, self.h = t("th", [P, 512]), t("h", [P, 512])
                self.hp = t("hp", [P, 2, 2, 512], f16)
                self.lt = t("lt", [E, T])
                self.sc, self.scb, self.gs, self.rk, self.wt, self.cw = (
                    t(n, [P, NT * E]) for n in ("sc", "scb", "gs", "rk", "wt", "cw"))
                self.pair, self.sum = t("pair", [P, NT * 4, 6]), t("sum", [P, 2 * NT])
                spare = spare or (t("gt", [P, 1024])[:, :], t("eq", [P, 1024])[:, :])
                self.gt, self.eq = (v.bitcast(bf16)[:, 0:NT * E * E].rearrange("p (t a b) -> p t a b", a=E, b=E) for v in spare)
                self.x32 = spare[0].rearrange("p (a t) -> p a t", a=NH)
                self.c3t = t("c3t", [P, T], bf16)

            def pe_turn(self, pe):
                for a, bank in enumerate((YA, YB)):
                    for t in range(NT):
                        last = pe.transpose(bank[:, t * P:t * P + P], NF[:, t, a * P:a * P + P], ident[:, :])
                last.then_inc(f_tr, 1)

            def pe_route(self, pe):
                pe.wait_ge(f_xt, 2)
                for a in range(NH):
                    last = pe.matmul(GB[0:E, :], WRT[:, a, :], self.x32[:, a, :], start=a == 0, stop=a == NH - 1)
                last.then_inc(f_lg, 1)
                pe.wait_ge(f_th, 1)
                for t in range(NT):
                    last = pe.transpose(CBK[:, t * E:t * E + E], self.lt[:, t * P:t * P + P], ident[0:E, 0:E])
                last.then_inc(f_lt, 1)

            def in_parts(self, pe, bank, w, e, a):
                for n, (pw, px) in enumerate(((1, 0), (0, 1), (0, 0))):
                    last = pe.matmul(bank[:, :], w[:, pw, a, e * EH:e * EH + EH], self.xt[:, px, a, :],
                                     start=a == 0 and n == 0, stop=a == NH - 1 and n == 2)
                return last

            def pe_gate(self, pe, e, a):
                if a == 0 and e > 0:
                    pe.wait_ge(f_gd, e)
                elif a == 0:
                    pe.wait_ge(f_xl, 2)
                last = self.in_parts(pe, GB, WG, e, a)
                if a == NH - 1:
                    last.then_inc(f_g, 1)

            def pe_up(self, pe, e, a):
                if a == 0 and e > 0:
                    pe.wait_ge(f_h, e)
                last = self.in_parts(pe, UBK, WU, e, a)
                if a < NH - 1:
                    return
                last.then_inc(f_u, 1)
                if e >= NS:
                    r = e - NS
                    if r == 0:
                        pe.wait_ge(f_cs, 1)
                    pe.matmul(CBK[:, :], K16["pick"][:, r * P:r * P + P], self.c3t[:, :], start=True, stop=True)\
                      .then_inc(f_c, 1)

            def pe_parts(self, pe):
                pe.wait_ge(f_c3, 1)
                cb = CBK[:, :].bitcast(bf16)
                for t in range(NT):
                    last = pe.transpose(cb[:, t * P:t * P + P], C3[:, t, :], identb[:, :])
                last.then_inc(f_ct, 1)

            def pe_down(self, pe, e, part):
                pe.wait_ge(f_lo, e + 1)
                for t in (2 * part, 2 * part + 1):
                    for n, (ph, pw) in enumerate(((1, 0), (0, 1), (0, 0))):
                        last = pe.matmul((YA, YB)[t // 2][:, (t % 2) * C:(t % 2) * C + C],
                                         self.hp[:, e % 2, ph, t * P:t * P + P], WD[:, pw, e, :],
                                         start=e == 0 and t % 2 == 0 and n == 0,
                                         stop=e == NE - 1 and t % 2 == 1 and n == 2)
                if part == 1:
                    last.then_inc(f_dn, 1)
                elif e == NE - 1:
                    last.then_inc(f_ya, 1)

            def on_tensor(self, pe):
                return {"ffn_turn": lambda: self.pe_turn(pe), "route": lambda: self.pe_route(pe),
                        "parts": lambda: self.pe_parts(pe), "g": lambda e, a: self.pe_gate(pe, e, a),
                        "u": lambda e, a: self.pe_up(pe, e, a), "d": lambda e, part: self.pe_down(pe, e, part)}

            def act_turn(self, act):
                act.wait_ge(f_tr, 1)
                for a, bank in enumerate((YA, YB)):
                    act.activation(self.x32[:, a, :], bank[:, :], ACT.Copy, scale=XS).then_inc(f_xt, 1)
                    act.activation(self.xt[:, 0, a, :], bank[:, :], ACT.Copy, scale=XS).then_inc(f_xh, 1)

            def act_route(self, act):
                act.wait_ge(f_lg, 1)
                act.activation(self.lt[:, :], GB[0:E, :], ACT.Tanh, scale=0.5 / XS).then_inc(f_th, 1)

            def act_parts(self, act):
                act.wait_ge(f_ct, 1)
                act.copy(self.c3t[:, :], CBK[:, :].bitcast(bf16)[:, 0:T]).then_inc(f_cs, 1)

            def act_gate(self, act, e, a):
                if a < NH - 1:
                    if e > 0:
                        self.act_hi(act, e - 1)
                    return
                act.wait_ge(f_g, e + 1)
                act.activation(self.th[:, :], GB[:, :], ACT.Tanh, scale=FG[:, e:e + 1]).then_inc(f_tanh, 1)

            def act_hi(self, act, e):
                act.wait_ge(f_h, e + 1)
                if e >= 2:
                    act.wait_ge(f_dn, e - 1)
                act.copy(self.hp[:, e % 2, 0, :], self.h[:, :]).then_inc(f_hi, 1)

            def on_scalar(self, act):
                return {"ffn_turn": lambda: self.act_turn(act), "route": lambda: self.act_route(act),
                        "parts": lambda: self.act_parts(act), "g": lambda e, a: self.act_gate(act, e, a),
                        "d": lambda e, part: self.act_hi(act, e) if (e, part) == (NE - 1, 0) else None}

            def lo(self, eng, e):
                eng.wait_ge(f_hi, e + 1)
                eng.tensor_tensor(self.hp[:, e % 2, 1, :], self.h[:, :], self.hp[:, e % 2, 0, :], ALU.subtract)\
                    .then_inc(f_lo, 1)

            def on_gpsimd(self, pool):
                if not self.lo_on_pool:
                    return {}
                return {"g": lambda e, a: self.lo(pool, e - 1) if e > 0 and a == 0 else None,
                        "d": lambda e, part: self.lo(pool, e) if (e, part) == (NE - 1, 0) else None}

            def dve_turn(self, dve):
                for a in range(NH):
                    dve.wait_ge(f_xh, a + 1)
                    dve.tensor_tensor(self.xt[:, 1, a, :], self.x32[:, a, :], self.xt[:, 0, a, :], ALU.subtract)\
                       .then_inc(f_xl, 1)

            def dve_ranks(self, dve, link, values, n, low, ranks_out):
                v = values.rearrange("p (t e) -> p t e", e=n)
                mine = v.unsqueeze(3).to_broadcast([P, NT, n, n])
                other = v.unsqueeze(2).to_broadcast([P, NT, n, n])
                gt, eq = self.gt[:, :, 0:n, 0:n], self.eq[:, :, 0:n, 0:n]
                dve.tensor_tensor(gt, other, mine, ALU.is_gt)
                link(dve.tensor_tensor(eq, other, mine, ALU.is_equal))
                lo = low.rearrange("p (a b) -> p a b", b=n).unsqueeze(1).to_broadcast([P, NT, n, n])
                link(dve.tensor_tensor(eq, eq, lo, ALU.mult))
                link(dve.tensor_tensor(gt, gt, eq, ALU.add))
                link(dve.tensor_reduce(ranks_out.rearrange("p (t e) -> p t e", e=n), gt, AX.X, ALU.add))

            def dve_rank_groups(self, dve, link):
                dve.wait_ge(f_xl, 2)
                dve.wait_ge(f_lt, 1)
                link(dve.tensor_scalar(self.sc[:, :], CBK[:, 0:NT * E], 0.5, 0.5, ALU.mult, ALU.add))
                sc4 = self.sc[:, :].rearrange("p (t e) -> p t e", e=E)
                link(dve.tensor_tensor(self.scb[:, :].rearrange("p (t e) -> p t e", e=E), sc4,
                                       EB[:, :].unsqueeze(1).to_broadcast([P, NT, E]), ALU.add))
                g4 = self.scb[:, :].rearrange("p (g e) -> p g e", e=4)
                dve.tensor_tensor(self.pair[:, :, 0:3], g4[:, :, 0:3], g4[:, :, 1:4], ALU.add)
                dve.tensor_tensor(self.pair[:, :, 3:5], g4[:, :, 0:2], g4[:, :, 2:4], ALU.add)
                link(dve.tensor_tensor(self.pair[:, :, 5:6], g4[:, :, 0:1], g4[:, :, 3:4], ALU.add))
                link(dve.tensor_reduce(self.gs[:, 0:16], self.pair[:, :, :], AX.X, ALU.max))
                self.dve_ranks(dve, link, self.gs[:, 0:16], 4, K16["group_low"][:, :], self.rk[:, 0:16])
                link(dve.tensor_scalar(self.gs[:, 16:32], self.rk[:, 0:16], 1.5, None, ALU.is_lt))
                link(dve.tensor_tensor(self.wt[:, :].rearrange("p (g e) -> p g e", e=4), g4,
                                       self.gs[:, 16:32].unsqueeze(2).to_broadcast([P, 16, 4]), ALU.mult))

            def dve_rank_experts(self, dve, link):
                self.dve_ranks(dve, link, self.wt[:, :], E, K16["expert_low"][:, :], self.rk[:, :])

            def dve_weigh(self, dve, link):
                link(dve.scalar_tensor_tensor(self.cw[:, :], self.rk[:, :], 3.5, self.sc[:, :], ALU.is_lt, ALU.mult))
                cw4 = self.cw[:, :].rearrange("p (t e) -> p t e", e=E)
                link(dve.tensor_reduce(self.sum[:, 0:NT], cw4, AX.X, ALU.add))
                link(dve.tensor_scalar(self.sum[:, 0:NT], self.sum[:, 0:NT], 1e-20, None, ALU.add))
                link(dve.reciprocal(self.sum[:, NT:], self.sum[:, 0:NT]))
                link(dve.tensor_tensor(cw4, cw4, self.sum[:, NT:].unsqueeze(2).to_broadcast([P, NT, E]), ALU.mult))
                link(dve.tensor_scalar(self.cw[:, :], self.cw[:, :], ROUTE, None, ALU.mult))
                link(dve.tensor_copy(C3[:, :, 0:E], cw4))
                link(dve.tensor_tensor(cw4, cw4, C3[:, :, 0:E], ALU.subtract))
                link(dve.tensor_copy(C3[:, :, E:2 * E], cw4))
                link(dve.tensor_tensor(cw4, cw4, C3[:, :, E:2 * E], ALU.subtract))
                dve.tensor_copy(C3[:, :, 2 * E:3 * E], cw4).then_inc(f_c3, 1)

            def dve_gate(self, dve, e, a):
                if a < NH - 1:
                    if e > 0 and not self.lo_on_pool:
                        self.lo(dve, e - 1)
                    return
                dve.wait_ge(f_tanh, e + 1)
                dve.scalar_tensor_tensor(self.th[:, :], self.th[:, :], 1.0, GB[:, :], ALU.add, ALU.mult)\
                   .then_inc(f_gd, 1)

            def dve_up(self, dve, link, e, a):
                if a < NH - 1:
                    return
                dve.wait_ge(f_gd, e + 1)
                dve.wait_ge(f_u, e + 1)
                if e >= 1:
                    dve.wait_ge(f_lo, e)
                h = self.h[:, :]
                if e < NS:
                    dve.scalar_tensor_tensor(h, UBK[:, :], FH[:, e:e + 1], self.th[:, :], ALU.mult, ALU.mult).then_inc(f_h, 1)
                else:
                    link(dve.scalar_tensor_tensor(h, UBK[:, :], FH[:, e:e + 1], self.th[:, :], ALU.mult, ALU.mult))
                    dve.wait_ge(f_c, e - NS + 1)
                    dve.tensor_tensor(h, h, CBK[:, :], ALU.mult).then_inc(f_h, 1)

            def dve_out(self, dve):
                for n, bank in enumerate((YA, YB)):
                    dve.wait_ge(*((f_ya, 1), (f_dn, NE))[n])
                    dve.scalar_tensor_tensor(self.dst[:, 2 * n:2 * n + 2, :], bank[:, :].rearrange("p (t c) -> p t c", c=C),
                                             FO[:, :], self.src[:, 2 * n:2 * n + 2, :], ALU.mult, ALU.add).then_inc(f_res, 1)

            def on_vector(self, dve, link):
                return {"ffn_turn": lambda: self.dve_turn(dve), "rank_groups": lambda: self.dve_rank_groups(dve, link),
                        "rank_experts": lambda: self.dve_rank_experts(dve, link), "weigh": lambda: self.dve_weigh(dve, link),
                        "g": lambda e, a: self.dve_gate(dve, e, a), "u": lambda e, a: self.dve_up(dve, link, e, a),
                        "d": lambda e, part: self.lo(dve, e) if (e, part, self.lo_on_pool) == (NE - 1, 0, False) else None,
                        "ffn_out": lambda: self.dve_out(dve)}

        def rwkv_ffn(rwkv_to=X1, ffn_rows=(X3, X3), norm_row=True, stores=()):
            rwkv, ffn_on = rwkv_to is not None, ffn_rows is not None
            def x1_turn(i):
                return i + 1 + (norm_row and i >= 1)

            def x2_turn():
                return 2 if rwkv else 1

            with ExitStack() as stack:
                def t(n, shape, dt=f32):
                    return sb("a_" + n, shape, dt, stack)

                if rwkv:
                    ystats, ymv, yve = (t(n, [P, NT, k]) for n, k in (("yst", 6), ("ymv", 2), ("yve", 2)))
                    XT, XX = t("xt", [P, NH, T + 1]), t("xx", [P, NH, T])
                    TM = t("tm", [P, T])
                    XF = t("xf", [P, 2, NH, T])
                    DT = t("dt", [P, T])
                    WE = t("we", [P, NT * RH])
                    WX = NR[:, :, :].rearrange("p t c -> p (t c)")
                    EW = XF
                    KK, VV, RT, KT = t("k", [P, NT, C]), t("v", [P, NT, C]), t("rT", [P, NH, T]), t("kT", [P, NH, T])
                    RX = t("rx", [P, NH, 8, P])
                    WM = t("wm", [P, 2, 512])
                    DEC, WS = t("dec", [P, 2, NT * RH]), t("ws", [P, NH, NT, 2])
                    S = t("s", [P, 2, NH, P])
                    SM, Y, YN, YT, DV = t("sm", [P, NH, P]), t("y", [P, C]), t("yn", [P, C]), t("yT", [P, C]), t("dv", [P, C])
                PR = XX if rwkv else None
                ffn = None
                if ffn_on:
                    spare = [RX[:, a, :, :].rearrange("p h n -> p (h n)") for a in range(NH)] if rwkv else None
                    ffn = Ffn("fa", *ffn_rows, stack, spare, lo_on_pool=False)

                def fills(step):
                    n = step[1] if len(step) > 1 else None
                    return {"mix_in": ["x0", "x1"], "mix_first": ["m"], "mix": [("mix", n, 0), ("mix", n, 1)],
                            "use": {0: ["dt"], 1: ["k0", "k1"], 2: ["v0", "v1"], 3: ["r0", "r1"]}.get(n),
                            "decay_rates": ["w"], "decays": ["dec"], "prep": ["kT0", "kT1"],
                            "args": [("arg", n, 0), ("arg", n, 1)], "scores": [("score", n, 0), ("score", n, 1)],
                            "intra": [("diag", n), ("kv", n)], "inter": [("y", n)],
                            "turn_y": [("yT", n)], "project_y": [("o", n)]}.get(step[0], [])

                TURN = turns([name for step in ORDER_A for name in fills(step)])

                def bank(name):
                    return RING[TURN[name] % 3]

                def take(pe, name):
                    n = TURN[name]
                    if n >= 3:
                        pe.wait_ge(emptied[n % 3], n // 3)
                    return RING[n % 3]

                def wait_fill(eng, name):
                    eng.wait_ge(filled, TURN[name] + 1)
                    return bank(name)

                def empty(name):
                    return emptied[TURN[name] % 3]

                with nc.Block() as block:
                    @block.sync
                    def _(sp):
                        for n, (src, row) in enumerate(stores):
                            if src is ffn.dst:
                                sp.wait_ge(f_res, 2)
                            sp.dma_start(out_rows[row], src[:, :, :]).then_inc(f_out, 16)
                        if stores:
                            sp.wait_ge(f_out, 16 * len(stores))

                    @block.tensor
                    def _(pe):
                        def mix_in():
                            for a in range(NH):
                                b = take(pe, f"x{a}")
                                for i in range(NT):
                                    last = pe.transpose(b[:, i * P:i * P + P], NR[:, i, a * P:a * P + P], ident[:, :])
                                last.then_inc(filled, 1)

                        def mix_first():
                            b = take(pe, "m")
                            pe.wait_ge(r_mixin, 1)
                            for a in range(NH):
                                last = pe.matmul(b[:, :], W1[:, a, :], XF[:, 1, a, :], start=a == 0, stop=a == NH - 1)
                            last.then_inc(filled, 1)

                        def mix(f):
                            pe.wait_ge(r_m, 1)
                            for a in range(NH):
                                pe.matmul(take(pe, ("mix", f, a))[:, :], W2[:, f, a * P:a * P + P], TM[:, :],
                                          start=True, stop=True).then_inc(filled, 1)

                        def use(f):
                            pe.wait_ge(r_mixed, f + 1)
                            xf = XF[:, f % 2, :, :]
                            if f == 0:
                                b = take(pe, "dt")
                                for a in range(NH):
                                    last = pe.matmul(b[0:64, :], DW1[:, a, :], xf[:, a, :], start=a == 0, stop=a == NH - 1)
                                last.then_inc(filled, 1)
                            elif f < 3:
                                for n in range(2):
                                    b = take(pe, f"{'_kv'[f]}{n}")
                                    for j in range(2):
                                        i = 2 * n + j
                                        for a in range(NH):
                                            last = pe.matmul(b[:, j * C:j * C + C], xf[:, a, i * P:i * P + P],
                                                             WR[:, f, a, :], start=a == 0, stop=a == NH - 1)
                                    last.then_inc(filled, 1)
                            else:
                                for n in range(NH):
                                    b = take(pe, f"r{n}")
                                    for a in range(NH):
                                        last = pe.matmul(b[:, :], WR[:, 0, a, n * P:n * P + P], xf[:, a, :],
                                                         start=a == 0, stop=a == NH - 1)
                                    last.then_inc(filled, 1)

                        def decay_rates():
                            b = take(pe, "w")
                            pe.wait_ge(r_dt, 1)
                            for i in range(NT):
                                last = pe.matmul(b[:, i * RH:i * RH + RH], DT[:, i * P:i * P + P], DWM[:, :],
                                                 start=True, stop=True)
                            last.then_inc(filled, 1)

                        def decays():
                            b = take(pe, "dec")
                            pe.wait_ge(r_we, 1)
                            pe.matmul(b[:, 0:64], K32["before"][:, :], WE[:, :], start=True, stop=True)
                            pe.matmul(b[:, 64:128], K32["after"][:, :], WE[:, :], start=True, stop=True)
                            pe.wait_ge(r_wx, 1)
                            for i in range(NT):
                                for a in range(NH):
                                    rates = WX[:, i * C + a * P:i * C + a * P + P]
                                    at = 128 + a * 8 + 2 * i
                                    last = pe.matmul(b[:, at:at + 2], rates, K32["chunks"][:, :], start=True, stop=True)
                            last.then_inc(filled, 1)

                        def prep():
                            pe.wait_ge(r_k, 2)
                            for a in range(NH):
                                b = take(pe, f"kT{a}")
                                for i in range(NT):
                                    last = pe.transpose(b[:, i * P:i * P + P], KK[:, i, a * P:a * P + P], ident[:, :])
                                last.then_inc(filled, 1)

                        def args(i):
                            for n in range(2):
                                b = take(pe, ("arg", i, n))
                                pe.wait_ge(r_wm, 2 * i + n + 1)
                                pe.matmul(b[:, :], K32["after"][:, :], WM[:, n, :], start=True, stop=False)
                                pe.matmul(b[:, :], identb[:, :], K16["forbid"][:, :], start=False, stop=True)\
                                  .then_inc(filled, 1)

                        def scores(i):
                            pe.wait_ge(r_kt, 2)
                            pe.wait_ge(r_rx, 2 * i + 2)
                            for a in range(NH):
                                b = take(pe, ("score", i, a))
                                for c in range(2):
                                    at = i * P + c * RQ
                                    last = pe.matmul(b[c * RQ:c * RQ + RQ, :], KT[:, a, at:at + RQ],
                                                     RX[:, a, :, c * RQ:c * RQ + RQ], start=True, stop=True)
                                last.then_inc(filled, 1)

                        def carried(i, c):
                            b, at = bank(("y", i)), i * P + c * RQ
                            pe.wait_ge(r_s, 2 * i + c + 1)
                            for a in range(NH):
                                last = pe.matmul(b[c * RQ:c * RQ + RQ, C + a * P:C + a * P + P],
                                                 RT[:, a, at:at + RQ], S[:, c, a, :], start=True, stop=True)
                            return last

                        def intra(i):
                            b = take(pe, ("y", i))
                            pe.wait_ge(r_p, 2 * i + 2)
                            pe.wait_ge(r_v, 2)
                            for c in range(2):
                                rows = slice(c * RQ, c * RQ + RQ)
                                for h in range(RH):
                                    last = pe.matmul(b[rows, h * RN:h * RN + RN],
                                                     EW[rows, i % 2, h // 8, (h % 8) * RQ:(h % 8) * RQ + RQ],
                                                     VV[rows, i, h * RN:h * RN + RN], start=True, stop=True)
                            last.then_inc(r_used, 1)
                            carried(i, 0)
                            b = take(pe, ("diag", i))
                            pe.wait_ge(r_prod, 1)
                            for a in range(NH):
                                last = pe.matmul(b[:, a * P:a * P + P], PR[:, a, i * P:i * P + P], UB[:, a, :],
                                                 start=True, stop=True)
                            last.then_inc(filled, 1)
                            b = take(pe, ("kv", i))
                            pe.wait_ge(r_kw, 2 * i + 2)
                            for c in range(2):
                                for a in range(NH):
                                    last = pe.matmul(b[:, c * C + a * P:c * C + a * P + P],
                                                     KWP[:, c, a * P:a * P + P], VV[:, i, a * P:a * P + P],
                                                     start=True, stop=True)
                            last.then_inc(filled, 1)

                        def inter(i):
                            carried(i, 1).then_inc(filled, 1)

                        def turn_y(i):
                            b = take(pe, ("yT", i))
                            pe.wait_ge(r_yn, i + 1)
                            for a in range(NH):
                                last = pe.transpose(b[:, a * P:a * P + P], YN[:, a * P:a * P + P], ident[:, :])
                            last.then_inc(filled, 1)

                        def project_y(i):
                            b = take(pe, ("o", i))
                            pe.wait_ge(r_yt, 2 * i + 2)
                            for a in range(NH):
                                last = pe.matmul(b[:, 0:C], YT[:, a * P:a * P + P], WR[:, 3, a, :],
                                                 start=a == 0, stop=a == NH - 1)
                            last.then_inc(filled, 1)

                        stages = dict(mix_in=mix_in, mix_first=mix_first, mix=mix, use=use, decay_rates=decay_rates,
                                      decays=decays, prep=prep, args=args, scores=scores, intra=intra, inter=inter,
                                      turn_y=turn_y, project_y=project_y)
                        follow(ORDER_A, ffn.on_tensor(pe) if ffn else {}, stages if rwkv else {})
                    @block.scalar
                    def _(act):
                        def mix_in():
                            for a in range(NH):
                                b = wait_fill(act, f"x{a}")
                                act.copy(XT[:, a, 1:T + 1], b[:, :]).then_inc(r_xt, 1)
                                act.wait_ge(r_xt, a + 1)
                                act.sem_inc(empty(f"x{a}"), 1)

                        def mix_first():
                            b = wait_fill(act, "m")
                            act.activation(TM[:, :], b[:, :], ACT.Tanh).then_inc(r_m, 1)
                            act.wait_ge(r_m, 1)
                            act.sem_inc(empty("m"), 1)

                        def use(f):
                            if f == 0:
                                b = wait_fill(act, "dt")
                                act.activation(DT[0:64, :], b[0:64, :], ACT.Tanh).then_inc(r_dt, 1)
                                act.wait_ge(r_dt, 1)
                                act.sem_inc(empty("dt"), 1)
                                return
                            done = (None, r_k, r_v, r_r)[f]
                            for n in range(2):
                                b = wait_fill(act, f"{'_kvr'[f]}{n}")
                                if f < 3:
                                    dst = (None, KK, VV)[f][:, 2 * n:2 * n + 2, :]
                                    act.copy(dst, b[:, :].rearrange("p (t c) -> p t c", c=C)).then_inc(done, 1)
                                else:
                                    act.copy(RT[:, n, :], b[:, :]).then_inc(done, 1)
                                act.wait_ge(done, n + 1)
                                act.sem_inc(empty(f"{'_kvr'[f]}{n}"), 1)

                        def decay_rates():
                            b = wait_fill(act, "w")
                            act.activation(WE[:, :], b[:, 0:NT * RH], ACT.Exp).then_inc(r_we, 1)
                            act.wait_ge(r_we, 1)
                            act.sem_inc(empty("w"), 1)

                        def decays():
                            b = wait_fill(act, "dec")
                            act.activation(DEC[:, :, :], b[:, 0:128].rearrange("p (a n) -> p a n", a=2), ACT.Exp)\
                               .then_inc(r_dec, 1)
                            act.activation(WS[:, :, :, :].rearrange("p a t c -> p (a t c)"), b[:, 128:144], ACT.Exp)\
                               .then_inc(r_ws, 1)
                            act.wait_ge(r_ws, 1)
                            act.sem_inc(empty("dec"), 1)

                        def prep():
                            for a in range(NH):
                                b = wait_fill(act, f"kT{a}")
                                act.copy(KT[:, a, :], b[:, :]).then_inc(r_kt, 1)
                                act.wait_ge(r_kt, a + 1)
                                act.sem_inc(empty(f"kT{a}"), 1)

                        def args(i):
                            for n in range(2):
                                b = wait_fill(act, ("arg", i, n))
                                if i >= 2:
                                    act.wait_ge(r_used, i - 1)
                                act.activation(EW[:, i % 2, n, :], b[:, :], ACT.Exp).then_inc(r_e, 1)
                                act.wait_ge(r_e, 2 * i + n + 1)
                                act.sem_inc(empty(("arg", i, n)), 1)

                        def turn_y(i):
                            b = wait_fill(act, ("yT", i))
                            for a in range(NH):
                                act.activation(YT[:, a * P:a * P + P], b[:, a * P:a * P + P], ACT.Identity,
                                               bias=LNA[:, 1, a:a + 1], scale=LNA[:, 0, a:a + 1]).then_inc(r_yt, 1)
                            act.wait_ge(r_yt, 2 * i + 2)
                            act.sem_inc(empty(("yT", i)), 1)

                        stages = dict(mix_in=mix_in, mix_first=mix_first, use=use, decay_rates=decay_rates, decays=decays,
                                      prep=prep, args=args, turn_y=turn_y)
                        follow(ORDER_A, ffn.on_scalar(act) if ffn else {}, stages if rwkv else {})
                    @block.vector
                    def _(dve):
                        link = linker(dve, d_chain)

                        def mix_in():
                            dve.memset(XT[:, :, 0:1], 0.0)
                            dve.memset(DT[64:128, :], 1.0)
                            link(dve.memset(S[:, 0, :, :], 0.0))
                            dve.sem_inc(r_s, 1)
                            dve.wait_ge(r_xt, 2)
                            dve.tensor_tensor(XX[:, :, :], XT[:, :, 0:T], XT[:, :, 1:T + 1], ALU.subtract).then_inc(r_xx, 1)
                            dve.wait_ge(r_xx, 1)
                            for a in range(NH):
                                last = dve.scalar_tensor_tensor(XF[:, 1, a, :], XX[:, a, :], MAA[:, 0, a:a + 1],
                                                                XT[:, a, 1:T + 1], ALU.mult, ALU.add)
                            last.then_inc(r_mixin, 1)

                        def mix(f):
                            if f >= 1:
                                dve.wait_ge(filled, TURN[{1: "m", 2: "dt", 3: "k1"}[f]] + 1)
                            for a in range(NH):
                                b = wait_fill(dve, ("mix", f, a))
                                dve.scalar_tensor_tensor(XF[:, f % 2, a, :], b[:, :], MAA[:, f + 1, a:a + 1],
                                                         XX[:, a, :], ALU.add, ALU.mult).then_inc(r_half, 1)
                                dve.wait_ge(r_half, 2 * f + a + 1)
                                dve.sem_inc(empty(("mix", f, a)), 1)
                            xf = XF[:, f % 2, :, :]
                            dve.tensor_tensor(xf, xf, XT[:, :, 1:T + 1], ALU.add).then_inc(r_mixed, 1)

                        def decay_rates():
                            dve.wait_ge(r_we, 1)
                            dve.tensor_copy(WX[:, :].rearrange("p (h n) -> p h n", n=RN),
                                            WE[:, :].unsqueeze(2).to_broadcast([P, NT * RH, RN])).then_inc(r_wx, 1)

                        def scores(i):
                            for n in range(2):
                                b = wait_fill(dve, ("score", i, n))
                                dve.wait_ge(r_e, 2 * i + n + 1)
                                ew = EW[:, i % 2, n, :]
                                dve.tensor_tensor(ew, ew, b[:, :], ALU.mult).then_inc(r_p, 1)
                                dve.wait_ge(r_p, 2 * i + n + 1)
                                dve.sem_inc(empty(("score", i, n)), 1)

                        def intra(i):
                            b = wait_fill(dve, ("diag", i))
                            link(dve.tensor_tensor(DV[:, :], b[:, 0:C], VV[:, i, :], ALU.mult))
                            dve.sem_inc(empty(("diag", i)), 1)
                            b = wait_fill(dve, ("kv", i))
                            dve.wait_ge(r_ws, 1)
                            for c in range(2):
                                n = 2 * i + c
                                link(dve.tensor_tensor(SM[:, :, :], b[:, c * C:c * C + C].rearrange("p (a n) -> p a n", a=NH),
                                                       K32["same16"][:, :].unsqueeze(1).to_broadcast([P, NH, P]), ALU.mult))
                                if c == 1:
                                    dve.sem_inc(empty(("kv", i)), 1)
                                if n == 2 * NT - 1:
                                    break
                                if c == 0 and i >= 1:
                                    dve.wait_ge(filled, TURN["y", i - 1] + 1)
                                for a in range(NH):
                                    last = dve.scalar_tensor_tensor(S[:, (c + 1) % 2, a, :], S[:, c, a, :],
                                                                    WS[:, a, i, c:c + 1], SM[:, a, :], ALU.mult, ALU.add)
                                last.then_inc(r_s, 1)
                                dve.wait_ge(r_s, n + 2)

                        def inter(i):
                            b = wait_fill(dve, ("y", i))
                            dve.wait_ge(r_dec, 1)
                            dec = DEC[:, 0, i * RH:i * RH + RH].unsqueeze(2).to_broadcast([P, RH, RN])
                            link(dve.tensor_tensor(Y[:, :].rearrange("p (h n) -> p h n", n=RN),
                                                   b[:, C:2 * C].rearrange("p (h n) -> p h n", n=RN), dec, ALU.mult))
                            link(dve.tensor_tensor(Y[:, :], Y[:, :], b[:, 0:C], ALU.add))
                            dve.sem_inc(empty(("y", i)), 1)
                            link(dve.tensor_tensor(Y[:, :], Y[:, :], DV[:, :], ALU.add))
                            link(dve.bn_stats(ystats[:, i, :], Y[:, :]))
                            link(dve.bn_aggr(ymv[:, i, :], ystats[:, i, :]))
                            dve.tensor_scalar(yve[:, i, 0:1], ymv[:, i, 1:2], EPS, None, ALU.add).then_inc(r_yv, 1)

                        def norm_y(i):
                            dve.wait_ge(r_yr, i + 1)
                            if i >= 1:
                                dve.wait_ge(filled, TURN["yT", i - 1] + 1)
                            dve.tensor_scalar(YN[:, :], Y[:, :], ymv[:, i, 0:1], yve[:, i, 1:2], ALU.subtract, ALU.mult)\
                               .then_inc(r_yn, 1)
                            dve.wait_ge(r_yn, i + 1)

                        def project_y(i):
                            b = wait_fill(dve, ("o", i))
                            link(dve.tensor_tensor(rwkv_to[:, i, :], XR[:, i, :], b[:, 0:C], ALU.add))
                            dve.sem_inc(empty(("o", i)), 1)
                            measure(dve, link, rwkv_to, (i, i + 1))

                        def norm_x1(i):
                            standardise(dve, link, rwkv_to, NF, (i, i + 1), x1_turn(i))

                        stages = dict(mix_in=mix_in, mix=mix, decay_rates=decay_rates, scores=scores,
                                      intra=intra, inter=inter, norm_y=norm_y, project_y=project_y, norm_x1=norm_x1)
                        always = {"norm_x2": lambda: normalise(dve, link, X2, ND, (0, NT), x2_turn())} if norm_row else {}
                        follow(ORDER_A, ffn.on_vector(dve, link) if ffn else {}, stages if rwkv else {}, always)
                    @block.gpsimd
                    def _(pool):
                        def rates(i):
                            for n in range(2):
                                if i >= 1:
                                    pool.wait_ge(filled, TURN["arg", i - 1, n] + 1)
                                pool.tensor_tensor(
                                    WM[:, n, :].rearrange("p (h q) -> p h q", q=RQ),
                                    WE[:, i * RH + 8 * n:i * RH + 8 * n + 8].unsqueeze(2).to_broadcast([P, 8, RQ]),
                                    K32["earlier"][:, :].unsqueeze(1).to_broadcast([P, 8, RQ]), ALU.mult).then_inc(r_wm, 1)

                        def spread(i):
                            if i >= 1:
                                pool.wait_ge(filled, TURN["score", i - 1, 1] + 1)
                            elif ffn:
                                pool.wait_ge(f_c3, 1)
                            for a in range(NH):
                                pool.tensor_tensor(
                                    RX[:, a, :, :], RT[:, a, i * P:i * P + P].unsqueeze(1).to_broadcast([P, 8, P]),
                                    K32["heads8"][:, :].unsqueeze(2).to_broadcast([P, 8, P]), ALU.mult).then_inc(r_rx, 1)

                        def decayed(i):
                            if i >= 1:
                                pool.wait_ge(filled, TURN["kv", i - 1] + 1)
                                pool.wait_ge(r_yr, i)
                            pool.wait_ge(r_wm, 2 * i + 2)
                            pool.wait_ge(r_rx, 2 * i + 2)
                            for c in range(2):
                                rows = slice(c * RQ, c * RQ + RQ)
                                pool.tensor_tensor(
                                    KWP[rows, c, :].rearrange("p (h n) -> p h n", n=RN),
                                    KK[rows, i, :].rearrange("p (h n) -> p h n", n=RN),
                                    DEC[rows, 1, i * RH:i * RH + RH].unsqueeze(2).to_broadcast([RQ, RH, RN]), ALU.mult)\
                                    .then_inc(r_kw, 1)
                                pool.wait_ge(r_kw, 2 * i + c + 1)

                        def decays():
                            pool.wait_ge(r_we, 1)
                            rates(0)

                        def prep():
                            pool.wait_ge(r_r, 2)
                            spread(0)
                            pool.wait_ge(r_dec, 1)
                            pool.wait_ge(r_k, 2)
                            decayed(0)
                            pool.wait_ge(r_kt, 2)
                            pool.wait_ge(r_mixed, 4)
                            pool.tensor_tensor(PR[:, :, :], RT[:, :, :], KT[:, :, :], ALU.mult).then_inc(r_prod, 1)
                            pool.wait_ge(r_prod, 1)

                        def scores(i):
                            if i < NT - 1:
                                rates(i + 1)
                                spread(i + 1)

                        def inter(i):
                            pool.wait_ge(r_yv, i + 1)
                            pool.tensor_tensor(yve[:, i, 1:2], yve[:, i, 0:1], K32["nhalf"][:, 0:1], ALU.pow)\
                                .then_inc(r_yr, 1)

                        def turn_y(i):
                            if i < NT - 1:
                                decayed(i + 1)

                        def project_y(i):
                            root(pool, (i, i + 1), x1_turn(i))

                        stages = dict(decays=decays, prep=prep, scores=scores, inter=inter, turn_y=turn_y,
                                      project_y=project_y)
                        always = {"norm_x2": lambda: root(pool, (0, NT), x2_turn())} if norm_row else {}
                        follow(ORDER_A, ffn.on_gpsimd(pool) if ffn else {}, stages if rwkv else {}, always)
            end_block()

        def delta_ffn(delta_to=X3, ffn_rows=(X1, X2), load_row=None, store_row=None):
            loads = load_row is not None

            def x3_turn(i):
                return i + 1 + loads

            with ExitStack() as stack:
                def t(n, shape, dt=f32):
                    return sb("b_" + n, shape, dt, stack)

                XT = t("xt", [P, NH, T])
                ostats, omv, ove = (t(n, [P, NT, k]) for n, k in (("ost", 6), ("omv", 2), ("ove", 2)))
                Q, KH, KB, VB = t("q", [P, NT, C]), t("kh", [P, NT, C]), t("kb", [P, NT, C]), t("vb", [P, NT, C])
                SQ, SG, SS = t("sq", [P, C]), t("sg", [P, 2, C + DH]), t("ss", [P, NT, 2, DH])
                QT, KHT, KBT = t("qT", [P, NH, T]), t("khT", [P, NH, T]), t("kbT", [P, NH, T])
                QX, KX = t("qx", [P, NH, 4, P]), t("kx", [P, NH, 4, P])
                TMP = QX[:, :, :, :].rearrange("p a h n -> p (a h n)").rearrange("p (c j) -> p c j", j=DQ)
                AS = t("as", [P, 2, C])
                PT = t("pT", [P, NT, DH, DQ])
                TI = t("ti", [P, DH, P])
                TB = [XT[:, :, :].rearrange("p a (h n) -> p (a h) n", n=P), KX[:, :, :, :].rearrange("p a h n -> p (a h) n"),
                      TI[:, :, :], QX[:, :, :, :].rearrange("p a h n -> p (a h) n")]
                S = t("s", [P, NH, P])
                UT = KHT
                O = ND

                spare = [v.rearrange("p a b -> p (a b)") for v in
                         (MAT[:, :, :], TI[:, :, :])]
                ffn = Ffn("fb", *ffn_rows, stack, spare)

                def fills(step):
                    n = step[1] if len(step) > 1 else None
                    return {"project_in": ["x0", "x1"], "project": [("kv", n), ("qb", n)],
                            "turn": [("t1", n), ("t2", n)], "pairs": [("ap", n)], "apply": [("wk", n), ("wv", n)]}.get(step[0], [])

                TURN = turns([name for step in ORDER_B for name in fills(step)])
                KS, OB, SP = RING

                def take(pe, name):
                    n = TURN[name]
                    if n >= 3:
                        pe.wait_ge(emptied[n % 3], n // 3)
                    return RING[n % 3]

                def wait_fill(eng, name):
                    eng.wait_ge(filled, TURN[name] + 1)
                    return RING[TURN[name] % 3]

                def empty(name):
                    return emptied[TURN[name] % 3]

                def uses(k):
                    return len([n for n in TURN.values() if n % 3 == k])

                with nc.Block() as block:
                    @block.sync
                    def _(sp):
                        if loads:
                            sp.dma_start(XR[:, :, :], x_rows[load_row]).then_inc(x_in, 16)
                            sp.wait_ge(x_in, 16)
                        if store_row is not None:
                            sp.dma_start(out_rows[store_row], X3[:, :, :]).then_inc(f_out, 16)
                            sp.wait_ge(f_out, 16)
                        a_v = a_dram.rearrange("(t c h) i j -> t c i h j", t=NT, c=4)
                        t_v = t_dram.rearrange("(t c h) i j -> c i t h j", t=NT, c=4)
                        for i in range(NT):
                            sp.wait_ge(d_a, i + 1)
                            for c in range(4):
                                sp.dma_start(a_v[i, c], AS[32 * c:32 * c + 32, i % 2, :].rearrange("p (h j) -> p h j", h=DH))\
                                  .then_inc(d_stores[i % 2], 16)
                        for parity in d_stores:
                            sp.wait_ge(parity, 8 * 16)
                        sp.wait_ge(f_c3, 1)
                        sp.dma_start(MAT[:, :, :], a_dram).then_inc(d_mat, 16)
                        sp.wait_ge(d_inv, 31)
                        sp.dma_start(t_dram, INV[:, :, :]).then_inc(d_tst, 16)
                        sp.wait_ge(d_tst, 16)
                        sp.wait_ge(d_tz, 4)
                        for i in range(NT):
                            for c in range(4):
                                sp.dma_start(TB[i][32 * c:32 * c + 32, :, 32 * c:32 * c + 32], t_v[c][:, i, :, :])\
                                  .then_inc(d_tld, 16)
                        sp.wait_ge(d_tld, 16 * 16)

                    @block.tensor
                    def _(pe):
                        def project_in():
                            for a in range(NH):
                                b = take(pe, f"x{a}")
                                for i in range(NT):
                                    last = pe.transpose(b[:, i * P:i * P + P], ND[:, i, a * P:a * P + P], ident[:, :])
                                last.then_inc(filled, 1)

                        def project(i):
                            pe.wait_ge(d_xt, 2)
                            b = take(pe, ("kv", i))
                            for a in range(NH):
                                last = pe.matmul(b[:, :], XT[:, a, i * P:i * P + P], WKV[:, a, :], start=a == 0, stop=a == NH - 1)
                            last.then_inc(filled, 1)
                            b = take(pe, ("qb", i))
                            for a in range(NH):
                                last = pe.matmul(b[:, 0:C + DH], XT[:, a, i * P:i * P + P], WQB[:, a, :],
                                                 start=a == 0, stop=a == NH - 1)
                            last.then_inc(filled, 1)

                        def turn(i):
                            pe.wait_ge(d_kh, i + 1)
                            b = take(pe, ("t1", i))
                            for a in range(NH):
                                pe.transpose(b[:, a * P:a * P + P], Q[:, i, a * P:a * P + P], ident[:, :])
                                last = pe.transpose(b[:, C + a * P:C + a * P + P], KH[:, i, a * P:a * P + P], ident[:, :])
                            last.then_inc(filled, 1)
                            b = take(pe, ("t2", i))
                            pe.wait_ge(d_kb, i + 1)
                            for a in range(NH):
                                last = pe.transpose(b[:, a * P:a * P + P], KB[:, i, a * P:a * P + P], ident[:, :])
                            last.then_inc(filled, 1)

                        def pairs(i):
                            pe.wait_ge(d_turn, 3 * i + 3)
                            pe.wait_ge(d_kx, 4 * i + 4)
                            pe.wait_ge(d_exp, i + 1)
                            b = take(pe, ("ap", i))
                            for c in range(4):
                                rows, toks = slice(32 * c, 32 * c + 32), slice(i * P + 32 * c, i * P + 32 * c + 32)
                                for a in range(NH):
                                    pe.matmul(b[rows, a * P:a * P + P], KBT[:, a, toks], KX[:, a, :, rows], start=True, stop=True)
                                    last = pe.matmul(b[rows, C + a * P:C + a * P + P], KHT[:, a, toks], QX[:, a, :, rows],
                                                     start=True, stop=True)
                            last.then_inc(filled, 1)

                        def key_state(g):
                            rows, toks = slice(32 * (g % 4), 32 * (g % 4) + 32), slice(g * 32, g * 32 + 32)
                            if g == 0:
                                for k in range(3):
                                    pe.wait_ge(emptied[k], uses(k))
                                pe.wait_ge(d_wk, NT)
                                pe.wait_ge(d_wv, NT)
                                solved_values(0)
                            pe.wait_ge(d_s, g + 1)
                            for a in range(NH):
                                last = pe.matmul(KS[rows, a * P:a * P + P], KBT[:, a, toks], S[:, a, :],
                                                 start=False, stop=a == NH - 1)
                            last.then_inc(d_ks, 1)

                        def apply(n):
                            if n == 0:
                                pe.wait_ge(d_tld, 16 * 16)
                                pe.wait_ge(d_vbb, NT)
                            for name, x in (("wk", KB), ("wv", VB)):
                                b = take(pe, (name, n))
                                for j in range(2):
                                    for h in range(DH):
                                        at = j * C + (h // 4) * P
                                        last = pe.matmul(b[32 * (h % 4):32 * (h % 4) + 32, at:at + P],
                                                         x[:, 2 * n + j, 32 * h:32 * h + 32], TB[2 * n + j][:, h, :],
                                                         start=True, stop=True)
                                last.then_inc(filled, 1)

                        def solved_values(g):
                            rows, toks = slice(32 * (g % 4), 32 * (g % 4) + 32), slice(g * 32, g * 32 + 32)
                            if g >= 4:
                                pe.wait_ge(d_vs, g - 3)
                            for a in range(NH):
                                pe.matmul(KS[rows, a * P:a * P + P], UT[:, a, toks], ident[:, :], start=a == 0, stop=False)

                        def outputs(g):
                            return OB[32 * (g % 4):32 * (g % 4) + 32, 0:C]

                        def query(g):
                            i, c = g // 4, g % 4
                            if c > 0:
                                values(g - 1)
                            elif i > 0:
                                pe.wait_ge(d_os, i)
                            for a in range(NH):
                                pe.matmul(outputs(g)[:, a * P:a * P + P], QT[:, a, g * 32:g * 32 + 32], S[:, a, :],
                                          start=a == 0, stop=False)

                        def values(g):
                            i, c = g // 4, g % 4
                            for h in range(DH):
                                last = pe.matmul(outputs(g)[:, 32 * h:32 * h + 32], PT[:, i, h, :],
                                                 VP[:, c, 32 * h:32 * h + 32], start=False, stop=h == DH - 1)
                            if c == 3:
                                last.then_inc(d_o, 1)

                        def update(g):
                            i, c = g // 4, g % 4
                            pe.wait_ge(d_vs, g + 1)
                            if g < 15:
                                for a in range(NH):
                                    last = pe.matmul(SP[:, a * P:a * P + P], KH[:, i, a * P:a * P + P],
                                                     VP[:, c, a * P:a * P + P], start=g == 0 and a == 0,
                                                     stop=True, skip_group_check=True)
                                last.then_inc(d_up, 1)
                                solved_values(g + 1)
                            if c == 3:
                                values(g)

                        stages = dict(project_in=project_in, project=project, turn=turn, pairs=pairs, apply=apply,
                                      key_state=key_state, query=query, update=update)
                        follow(ORDER_B, ffn.on_tensor(pe), stages)
                    @block.scalar
                    def _(act):
                        def project_in():
                            for a in range(NH):
                                b = wait_fill(act, f"x{a}")
                                act.copy(XT[:, a, :], b[:, :]).then_inc(d_xt, 1)
                                act.wait_ge(d_xt, a + 1)
                                act.sem_inc(empty(f"x{a}"), 1)

                        def project(i):
                            b = wait_fill(act, ("kv", i))
                            if i >= 1:
                                act.wait_ge(d_ss, i)
                            act.activation(SQ[:, :], b[:, 0:C], ACT.Square).then_inc(d_sq, 1)
                            if i >= 2:
                                act.wait_ge(d_vbb, i - 1)
                            act.copy(KH[:, i, :], b[:, 0:C]).then_inc(d_kc, 1)
                            act.activation(SG[:, i % 2, 0:C], b[:, C:2 * C], ACT.Tanh, scale=0.5)
                            b = wait_fill(act, ("qb", i))
                            act.activation(SG[:, i % 2, C:C + DH], b[:, C:C + DH], ACT.Tanh, scale=0.5)
                            act.copy(Q[:, i, :], b[:, 0:C]).then_inc(d_qk, 1)
                            act.wait_ge(d_qk, i + 1)
                            act.sem_inc(empty(("qb", i)), 1)

                        def turn(i):
                            b = wait_fill(act, ("t1", i))
                            toks = slice(i * P, i * P + P)
                            act.copy(QT[:, :, toks], b[:, 0:C].rearrange("p (a n) -> p a n", a=NH)).then_inc(d_turn, 1)
                            act.copy(KHT[:, :, toks], b[:, C:2 * C].rearrange("p (a n) -> p a n", a=NH)).then_inc(d_turn, 1)
                            if i == 0:
                                act.wait_ge(d_zero, 1)
                            else:
                                act.wait_ge(filled, TURN["ap", i - 1] + 1)
                            for h in range(4):
                                rows = slice(DN * h, DN * h + DN)
                                act.copy(KX[rows, :, h, :], b[rows, C:2 * C].rearrange("p (a n) -> p a n", a=NH))\
                                   .then_inc(d_kx, 1)
                            act.wait_ge(d_turn, 3 * i + 2)
                            act.wait_ge(d_kx, 4 * i + 4)
                            act.sem_inc(empty(("t1", i)), 1)
                            b = wait_fill(act, ("t2", i))
                            act.copy(KBT[:, :, toks], b[:, 0:C].rearrange("p (a n) -> p a n", a=NH)).then_inc(d_turn, 1)
                            act.wait_ge(d_turn, 3 * i + 3)
                            act.sem_inc(empty(("t2", i)), 1)

                        def pairs(i):
                            b = wait_fill(act, ("ap", i))
                            if i >= 2:
                                act.wait_ge(d_stores[i % 2], 64 * (i // 2))
                            act.copy(AS[:, i % 2, :], b[:, 0:C]).then_inc(d_a, 1)

                        def apply(n):
                            b = wait_fill(act, ("wk", n))
                            for j in range(2):
                                toks = slice((2 * n + j) * P, (2 * n + j) * P + P)
                                act.activation(KBT[:, :, toks], b[:, j * C:j * C + C].rearrange("p (a n) -> p a n", a=NH),
                                               ACT.Copy, scale=-1.0).then_inc(d_wk, 1)
                            act.wait_ge(d_wk, 2 * n + 2)
                            act.sem_inc(empty(("wk", n)), 1)

                        def key_state(g):
                            c = g % 4
                            rows = slice(32 * c, 32 * c + 32)
                            act.wait_ge(d_ks, g + 1)
                            act.copy(VP[rows, c, :], KS[rows, 0:C]).then_inc(d_vs, 1)

                        def update(g):
                            if g % 4 == 3:
                                act.wait_ge(d_o, g // 4 + 1)
                                act.copy(O[:, g // 4, :], OB[:, 0:C]).then_inc(d_os, 1)

                        stages = dict(project_in=project_in, project=project, turn=turn, pairs=pairs, apply=apply,
                                      key_state=key_state, update=update)
                        follow(ORDER_B, ffn.on_scalar(act), stages)
                    @block.vector
                    def _(dve):
                        link = linker(dve, d_chain)

                        def project(i):
                            b = wait_fill(dve, ("kv", i))
                            dve.wait_ge(d_sq, i + 1)
                            link(dve.tensor_reduce(SS[:, i, 0, :], SQ[:, :].rearrange("p (h n) -> p h n", n=DN), AX.X, ALU.add))
                            dve.tensor_scalar(SS[:, i, 0, :], SS[:, i, 0, :], 1e-24, None, ALU.max).then_inc(d_ss, 1)
                            dve.wait_ge(d_qk, i + 1)
                            sg = SG[:, i % 2, :]
                            link(dve.tensor_scalar(sg, sg, 0.5, 0.5, ALU.mult, ALU.add))
                            dve.tensor_tensor(VB[:, i, :], b[:, C:2 * C], SG[:, i % 2, 0:C], ALU.mult).then_inc(d_vb, 1)
                            dve.wait_ge(d_vb, i + 1)
                            dve.sem_inc(empty(("kv", i)), 1)
                            dve.wait_ge(d_kc, i + 1)
                            dve.wait_ge(d_rn, i + 1)
                            kh = KH[:, i, :].rearrange("p (h n) -> p h n", n=DN)
                            dve.tensor_tensor(kh, kh, SS[:, i, 1, :].unsqueeze(2).to_broadcast([P, DH, DN]), ALU.mult)\
                               .then_inc(d_kh, 1)

                        def pairs(i):
                            b = wait_fill(dve, ("ap", i))
                            dve.wait_ge(d_a, i + 1)
                            dve.tensor_tensor(PT[:, i, :, :], b[:, C:2 * C].rearrange("p (h n) -> p h n", n=DQ),
                                              K32["causal"][:, :].unsqueeze(1).to_broadcast([P, DH, DQ]), ALU.mult)\
                               .then_inc(d_pt, 1)
                            dve.wait_ge(d_pt, i + 1)
                            dve.sem_inc(empty(("ap", i)), 1)

                        def invert(r, step):
                            half = r // 2 if r >= 14 else r
                            parts = ((0, half), (half, r))[:1 + (half < r)]
                            if r == 1 and step == 0:
                                link(dve.memset(S[:, :, :], 0.0))
                                dve.sem_inc(d_s, 1)
                                dve.wait_ge(d_mat, 16)
                            if step == 0:
                                if r > 1:
                                    dve.wait_ge(d_inv, r - 1)
                                for a, b in parts:
                                    last = dve.tensor_tensor(TMP[:, a:b, a:r], INV[:, a:b, a:r],
                                                             MAT[:, r, a:r].unsqueeze(1).to_broadcast([P, b - a, r - a]), ALU.mult)
                                last.then_inc(d_mul, 1)
                            else:
                                dve.wait_ge(d_mul, r)
                                for a, b in parts:
                                    last = dve.tensor_reduce(INV[:, a:b, r], TMP[:, a:b, a:r], AX.X, ALU.add, negate=True)
                                last.then_inc(d_inv, 1)

                        def apply(n):
                            b = wait_fill(dve, ("wv", n))
                            for j in range(2):
                                toks = slice((2 * n + j) * P, (2 * n + j) * P + P)
                                dve.tensor_copy(UT[:, :, toks], b[:, j * C:j * C + C].rearrange("p (a n) -> p a n", a=NH))\
                                   .then_inc(d_wv, 1)
                            dve.wait_ge(d_wv, 2 * n + 2)
                            dve.sem_inc(empty(("wv", n)), 1)

                        def update(g):
                            if g < 15:
                                dve.wait_ge(d_up, g + 1)
                                dve.tensor_tensor(S[:, :, :], SP[:, 0:C].rearrange("p (a n) -> p a n", a=NH),
                                                  K32["same32"][:, :].unsqueeze(1).to_broadcast([P, NH, P]), ALU.mult)\
                                   .then_inc(d_s, 1)

                        def finish(i, part):
                            o = O[:, i, :]
                            if part == 0:
                                dve.wait_ge(d_os, i + 1)
                                link(dve.bn_stats(ostats[:, i, :], o))
                                link(dve.bn_aggr(omv[:, i, :], ostats[:, i, :]))
                                dve.tensor_scalar(ove[:, i, 0:1], omv[:, i, 1:2], EPS, None, ALU.add).then_inc(d_ov, 1)
                            elif part == 1:
                                dve.wait_ge(d_or, i + 1)
                                link(dve.tensor_scalar(o, o, omv[:, i, 0:1], ove[:, i, 1:2], ALU.subtract, ALU.mult))
                                link(dve.tensor_tensor(o, o, LNB[:, 0, :], ALU.mult))
                            elif part == 2:
                                link(dve.tensor_tensor(o, o, LNB[:, 1, :], ALU.add))
                                if i == 0 and store_row is not None:
                                    dve.wait_ge(f_out, 16)
                                link(dve.tensor_tensor(delta_to[:, i, :], o, X2[:, i, :], ALU.add))
                            elif part == 3:
                                measure(dve, link, delta_to, (i, i + 1))
                            else:
                                standardise(dve, link, delta_to, NF, (i, i + 1), x3_turn(i))

                        def norm_x():
                            dve.wait_ge(x_in, 16)
                            normalise(dve, link, XR, NR, (0, NT), 1)

                        stages = dict(project=project, pairs=pairs, invert=invert, apply=apply, update=update,
                                      finish=finish)
                        always = {"norm_x": norm_x} if loads else {}
                        follow(ORDER_B, ffn.on_vector(dve, link), stages, always)
                    @block.gpsimd
                    def _(pool):
                        def project(i):
                            pool.wait_ge(d_ss, i + 1)
                            pool.tensor_tensor(SS[:, i, 1, :], SS[:, i, 0, :], K32["nhalf"][:, 0:DH], ALU.pow).then_inc(d_rn, 1)
                            beta = SG[:, i % 2, C:C + DH].unsqueeze(2).to_broadcast([P, DH, DN])
                            pool.wait_ge(d_kh, i + 1)
                            pool.tensor_tensor(KB[:, i, :].rearrange("p (h n) -> p h n", n=DN),
                                               KH[:, i, :].rearrange("p (h n) -> p h n", n=DN), beta, ALU.mult)\
                                .then_inc(d_kb, 1)
                            pool.wait_ge(d_vb, i + 1)
                            vb = VB[:, i, :].rearrange("p (h n) -> p h n", n=DN)
                            pool.tensor_tensor(vb, vb, beta, ALU.mult).then_inc(d_vbb, 1)

                        def turn(i):
                            pool.wait_ge(d_turn, 3 * i + 1)
                            if i >= 1:
                                pool.wait_ge(filled, TURN["ap", i - 1] + 1)
                            toks = slice(i * P, i * P + P)
                            for a in range(NH):
                                last = pool.tensor_tensor(
                                    QX[:, a, :, :], QT[:, a, toks].unsqueeze(1).to_broadcast([P, 4, P]),
                                    K32["heads4"][:, :].unsqueeze(2).to_broadcast([P, 4, P]), ALU.mult)
                            last.then_inc(d_exp, 1)

                        def invert(r, step):
                            if step == 0:
                                return
                            if r == 12:
                                pool.wait_ge(filled, TURN["ap", NT - 1] + 1)
                                pool.wait_ge(f_c3, 1)
                                for n in range(3):
                                    pool.memset(TB[n], 0.0).then_inc(d_tz, 1)
                            elif r == DQ - 1:
                                pool.wait_ge(d_inv, r)
                                pool.memset(TB[3], 0.0).then_inc(d_tz, 1)

                        def finish(i, part):
                            if part == 0:
                                pool.wait_ge(d_ov, i + 1)
                                pool.tensor_tensor(ove[:, i, 1:2], ove[:, i, 0:1], K32["nhalf"][:, 0:1], ALU.pow)\
                                    .then_inc(d_or, 1)
                            elif part == 3:
                                root(pool, (i, i + 1), x3_turn(i))

                        pool.memset(KX[:, :, :, :], 0.0).then_inc(d_zero, 1)
                        stages = dict(project=project, turn=turn, invert=invert, finish=finish)
                        always = {"norm_x": lambda: root(pool, (0, NT), 1)} if loads else {}
                        follow(ORDER_B, ffn.on_gpsimd(pool), stages, always)
            end_block()

        def load_and_normalise(row):
            with nc.Block() as block:
                @block.sync
                def _(sp):
                    sp.dma_start(XR[:, :, :], x_rows[row]).then_inc(x_in, 16)
                    sp.wait_ge(x_in, 16)

                @block.vector
                def _(dve):
                    dve.wait_ge(x_in, 16)
                    normalise(dve, linker(dve, d_chain), XR, NR, (0, NT), 1)

                @block.gpsimd
                def _(pool):
                    root(pool, (0, NT), 1)
            end_block()

        load_and_normalise(0)
        rwkv_ffn(ffn_rows=None, norm_row=False)
        load_and_normalise(1)
        rwkv_ffn(rwkv_to=X3, ffn_rows=(X1, X2), norm_row=False)
        with nc.Block() as block:
            @block.vector
            def _(dve):
                link = linker(dve, d_chain)
                link(dve.tensor_copy(X1[:, :, :], X3[:, :, :]))
                normalise(dve, link, X2, ND, (0, NT), 1)

            @block.gpsimd
            def _(pool):
                root(pool, (0, NT), 1)
        end_block()
        delta_ffn(load_row=2)
        with nc.Fori(2, B - 1) as i:
            rwkv_ffn()
            delta_ffn(load_row=i + 1, store_row=i - 2)
        rwkv_ffn()
        delta_ffn(store_row=B - 3)
        with nc.Block() as block:
            @block.vector
            def _(dve):
                normalise(dve, linker(dve, d_chain), X2, ND, (0, NT), 1)

            @block.gpsimd
            def _(pool):
                root(pool, (0, NT), 1)
        end_block()
        delta_ffn(delta_to=X1, ffn_rows=(X3, X3))
        rwkv_ffn(rwkv_to=None, ffn_rows=(X1, X1), norm_row=False, stores=((X3, B - 2), (X1, B - 1)))


def constants():
    import numpy as np
    p = np.arange(P)
    chunk, q = p // RQ, p % RQ
    same = chunk[:, None] == chunk[None, :]
    eye = np.eye(P)
    mats = {
        "ident": eye,
        "before": -(same & (p[:, None] < p[None, :])).astype(np.float32),
        "after": -(same & (p[:, None] > p[None, :])).astype(np.float32),
        "earlier": q[:, None] < np.arange(RQ)[None, :],
        "chunks": -(chunk[:, None] == np.arange(2)[None, :]).astype(np.float32),
        "heads8": p[:, None] // RN == np.arange(8)[None, :],
        "same16": p[:, None] // RN == p[None, :] // RN,
        "same32": p[:, None] // DN == p[None, :] // DN,
        "heads4": p[:, None] // DN == np.arange(4)[None, :],
        "causal": np.arange(DQ)[None, :] >= (p % DQ)[:, None],
        "nhalf": np.full((P, 32), -0.5),
        "lane_eye": np.tile(np.eye(DQ).reshape(1, -1), (P, 1)),
    }
    c32 = np.concatenate([np.asarray(mats[k], np.float32) for k in CONST32], 1)
    forbid = np.where(np.arange(RQ)[None, :] <= q[:, None], -BIG, 0.0)
    pick = [(p[:, None] % E == e) & (p[:, None] < 3 * E) & np.ones((1, P), bool) for e in range(E)]
    b16 = mybir.dt.np(mybir.dt.bfloat16)
    group_low = np.tile((np.arange(4)[None, :] < np.arange(4)[:, None]).reshape(1, -1), (P, 1))
    expert_low = np.tile((np.arange(E)[None, :] < np.arange(E)[:, None]).reshape(1, -1), (P, 1))
    c16 = np.concatenate([eye, np.tile(forbid, (1, 8)), np.concatenate(pick, 1), group_low, expert_low], 1).astype(b16)
    return np.ascontiguousarray(c32), np.ascontiguousarray(c16)


def kernel(**inputs):
    import numpy as np
    import concourse.bacc as bacc
    from concourse.bass_utils import run_bass_kernel_spmd as run

    i = {k[3:]: np.asarray(v) for k, v in inputs.items()}

    def halves(v):
        return v.reshape(NH, P).T

    def experts(routed, shared):
        return np.concatenate([shared, routed.reshape(E * EH, C)], 0).T

    down = np.concatenate([i["ffn_sh_down_w"].T.reshape(NS, EH, C), i["ffn_down_w"].transpose(0, 2, 1)], 0)
    c32, c16 = constants()
    arrays = {
        "x": i["attn_a_x"],
        "maa": np.concatenate([halves(i["attn_a_time_maa_" + f]) for f in "xwkvr"], 1),
        "maa_w1": i["attn_a_maa_w1"], "maa_w2": i["attn_a_maa_w2"],
        "decay_w1": i["attn_a_decay_w1"], "decay_w2": i["attn_a_decay_w2"],
        "time_decay": i["attn_a_time_decay"].reshape(C),
        "u_col": halves(i["attn_a_time_faaaa"].reshape(C)) ,
        "w_rkvo": np.stack([i["attn_a_W" + f] for f in "rkvo"]),
        "ln_a": np.concatenate([halves(i["attn_a_ln_g"]), halves(i["attn_a_ln_b"])], 1),
        "w_delta_kv": np.concatenate([i["attn_b_Wk"], i["attn_b_Wv"]], 1),
        "w_delta_qb": np.concatenate([i["attn_b_Wq"], i["attn_b_Wb"]], 1),
        "ln_b": np.stack([i["attn_b_ln_w"], i["attn_b_ln_b"]]),
        "router": i["ffn_router_weight"].T, "e_bias": i["ffn_e_bias"],
        "gate": experts(i["ffn_gate_w"], i["ffn_sh_gate_w"]),
        "up": experts(i["ffn_up_w"], i["ffn_sh_up_w"]),
        "down": down, "c32": c32, "c16": c16,
    }
    nc = bacc.Bacc("TRN2", target_bir_lowering=False, num_devices=1)
    args, feeds = [], {}
    for name, a in arrays.items():
        a = np.ascontiguousarray(a)
        feeds[f"in_{name}"] = a
        args.append(nc.dram_tensor(f"in_{name}", a.shape, mybir.dt.from_np(a.dtype), kind="ExternalInput").ap())
    out = nc.dram_tensor("out", (B, T, C), mybir.dt.float32, kind="ExternalOutput").ap()
    hybrid_layers(nc, *args, out)
    r = run(nc, [feeds], core_ids=[0])
    return r.results[0]["out"]
```
